# Optimizing a Trainium2 kernel written in Bass

```python
import numpy as np
import jax
import jax.numpy as jnp

def _softmax(x, axis=-1):
    return jax.nn.softmax(x, axis=axis)

def _gelu(x):
    return jax.nn.gelu(x, approximate=True)

def _silu(x):
    return jax.nn.silu(x)

def _sigmoid(x):
    return jax.nn.sigmoid(x)

def _layernorm(x, axis=-1, eps=1e-05):
    m = jnp.mean(x, axis=axis, keepdims=True)
    v = jnp.var(x, axis=axis, keepdims=True)
    return (x - m) / jnp.sqrt(v + eps)

def _scatter_add(tgt, idx, src, axis=0):
    return tgt.at[idx].add(src)

def _segment_sum(src, seg, n):
    return jax.ops.segment_sum(src, seg, n)
kernel_name = 'mk_seq_preln_d1_jaxref_r4_302ab4'

def setup_inputs(seed: int=0):
    np.random.seed(seed)
    _w = jnp.asarray

    def _L0_attn_setup():
        import jax, jax.numpy as jnp
        import numpy as np
        B, S, D, H, DK, DL, DR = (2, 512, 512, 16, 128, 128, 64)
        EPS = 1e-06

        def _rmsnorm(x, w):
            return x * jax.lax.rsqrt(jnp.mean(x * x, axis=-1, keepdims=True) + EPS) * w

        def _rope_tables(seq_len, d):
            quarter = d // 4
            freq = (1.0 / 10000.0) ** jnp.linspace(0.0, 1.0, quarter, dtype=jnp.float32)
            freq = jnp.concatenate([freq, jnp.zeros((quarter,), jnp.float32)])
            theta = jnp.arange(seq_len, dtype=jnp.float32)[:, None] * freq[None, :]
            return (jnp.cos(theta), jnp.sin(theta))

        def _apply_rope(x, cos, sin):
            half = x.shape[-1] // 2
            x1, x2 = (x[..., :half], x[..., half:])
            c = cos[None, None, :, :]
            s = sin[None, None, :, :]
            y1 = x1 * c + x2 * s
            y2 = -x1 * s + x2 * c
            return jnp.concatenate([y1, y2], axis=-1)
        key = jax.random.key(seed)
        ks = jax.random.split(key, 9)
        w = lambda k, sh: jax.random.normal(k, sh, jnp.float32) * 0.02
        return {'x': jax.random.normal(ks[0], (B, S, D), jnp.float32), 'wq': w(ks[1], (D, H * DK)), 'w_kv_down': w(ks[2], (D, DL)), 'w_k_rope': w(ks[3], (DL, H * DR)), 'w_k_nope': w(ks[4], (DL, H * (DK - DR))), 'wv': w(ks[5], (DL, H * DK)), 'wo': w(ks[6], (H * DK, D)), 'q_norm_w': jnp.ones((DK,), jnp.float32), 'k_norm_w': jnp.ones((DK,), jnp.float32)}
    _L0_attn_in = _L0_attn_setup()

    def _L0_ffn_setup():
        import jax, jax.numpy as jnp
        import numpy as np
        from jax import lax
        H = 512
        I = 256
        E = 32
        K = 4
        SH_I = 512
        EPS = 1e-06

        def _rmsnorm(x, w, eps=EPS):
            var = jnp.mean(jnp.square(x.astype(jnp.float32)), axis=-1, keepdims=True)
            return (x * lax.rsqrt(var + eps)).astype(x.dtype) * w
        key = jax.random.key(seed)
        ks = jax.random.split(key, 8)
        s = lambda d: 1.0 / np.sqrt(d)
        return {'x': jax.random.normal(ks[0], (2, 512, H), jnp.float32), 'norm_w': jnp.ones((H,), jnp.float32), 'router_w': jax.random.normal(ks[1], (E, H), jnp.float32) * s(H), 'w1': jax.random.normal(ks[2], (E, H, 2 * I), jnp.float32) * s(H), 'w2': jax.random.normal(ks[3], (E, I, H), jnp.float32) * s(I), 'sg': jax.random.normal(ks[4], (H, SH_I), jnp.float32) * s(H), 'su': jax.random.normal(ks[5], (H, SH_I), jnp.float32) * s(H), 'sd': jax.random.normal(ks[6], (SH_I, H), jnp.float32) * s(SH_I)}
    _L0_ffn_in = _L0_ffn_setup()
    _d = {'L0_attn_x': _L0_attn_in['x'], 'L0_attn_wq': _L0_attn_in['wq'], 'L0_attn_w_kv_down': _L0_attn_in['w_kv_down'], 'L0_attn_w_k_rope': _L0_attn_in['w_k_rope'], 'L0_attn_w_k_nope': _L0_attn_in['w_k_nope'], 'L0_attn_wv': _L0_attn_in['wv'], 'L0_attn_wo': _L0_attn_in['wo'], 'L0_attn_q_norm_w': _L0_attn_in['q_norm_w'], 'L0_attn_k_norm_w': _L0_attn_in['k_norm_w'], 'L0_ffn_norm_w': _L0_ffn_in['norm_w'], 'L0_ffn_router_w': _L0_ffn_in['router_w'], 'L0_ffn_w1': _L0_ffn_in['w1'], 'L0_ffn_w2': _L0_ffn_in['w2'], 'L0_ffn_sg': _L0_ffn_in['sg'], 'L0_ffn_su': _L0_ffn_in['su'], 'L0_ffn_sd': _L0_ffn_in['sd']}
    _x0 = _d['L0_attn_x']
    _d['L0_attn_x'] = jax.random.normal(jax.random.fold_in(jax.random.key(seed), 1), (4, 1024, 512), dtype=_x0.dtype)
    del _x0
    return _d

def reference(L0_attn_x, L0_attn_wq, L0_attn_w_kv_down, L0_attn_w_k_rope, L0_attn_w_k_nope, L0_attn_wv, L0_attn_wo, L0_attn_q_norm_w, L0_attn_k_norm_w, L0_ffn_norm_w, L0_ffn_router_w, L0_ffn_w1, L0_ffn_w2, L0_ffn_sg, L0_ffn_su, L0_ffn_sd):

    def _L0_attn_ref(x, wq, w_kv_down, w_k_rope, w_k_nope, wv, wo, q_norm_w, k_norm_w):
        import jax, jax.numpy as jnp
        import numpy as np
        B, S, D, H, DK, DL, DR = (2, 512, 512, 16, 128, 128, 64)
        EPS = 1e-06

        def _rmsnorm(x, w):
            return x * jax.lax.rsqrt(jnp.mean(x * x, axis=-1, keepdims=True) + EPS) * w

        def _rope_tables(seq_len, d):
            quarter = d // 4
            freq = (1.0 / 10000.0) ** jnp.linspace(0.0, 1.0, quarter, dtype=jnp.float32)
            freq = jnp.concatenate([freq, jnp.zeros((quarter,), jnp.float32)])
            theta = jnp.arange(seq_len, dtype=jnp.float32)[:, None] * freq[None, :]
            return (jnp.cos(theta), jnp.sin(theta))

        def _apply_rope(x, cos, sin):
            half = x.shape[-1] // 2
            x1, x2 = (x[..., :half], x[..., half:])
            c = cos[None, None, :, :]
            s = sin[None, None, :, :]
            y1 = x1 * c + x2 * s
            y2 = -x1 * s + x2 * c
            return jnp.concatenate([y1, y2], axis=-1)
        b, s, _ = x.shape
        q = (x @ wq).reshape(b, s, H, DK)
        q = _rmsnorm(q, q_norm_w).transpose(0, 2, 1, 3)
        latent = x @ w_kv_down
        v = (latent @ wv).reshape(b, s, H, DK).transpose(0, 2, 1, 3)
        k_rope = (latent @ w_k_rope).reshape(b, s, H, DR).transpose(0, 2, 1, 3)
        k_nope = (latent @ w_k_nope).reshape(b, s, H, DK - DR).transpose(0, 2, 1, 3)
        cos, sin = _rope_tables(s, DR)
        q = jnp.concatenate([_apply_rope(q[..., :DR], cos, sin), q[..., DR:]], axis=-1)
        k = jnp.concatenate([_apply_rope(k_rope, cos, sin), k_nope], axis=-1)
        k = _rmsnorm(k, k_norm_w)
        scale = 1.0 / np.sqrt(DK).astype(np.float32)
        scores = jnp.einsum('bhqd,bhkd->bhqk', q, k) * scale
        causal = jnp.tril(jnp.ones((s, s), bool))
        scores = jnp.where(causal[None, None], scores, jnp.finfo(scores.dtype).min)
        attn = jax.nn.softmax(scores, axis=-1)
        out = jnp.einsum('bhqk,bhkd->bhqd', attn, v)
        out = out.transpose(0, 2, 1, 3).reshape(b, s, H * DK)
        return out @ wo

    def _L0_ffn_ref(x, norm_w, router_w, w1, w2, sg, su, sd):
        import jax, jax.numpy as jnp
        import numpy as np
        from jax import lax
        H = 512
        I = 256
        E = 32
        K = 4
        SH_I = 512
        EPS = 1e-06

        def _rmsnorm(x, w, eps=EPS):
            var = jnp.mean(jnp.square(x.astype(jnp.float32)), axis=-1, keepdims=True)
            return (x * lax.rsqrt(var + eps)).astype(x.dtype) * w
        B, S, _ = x.shape
        residual = x
        h = _rmsnorm(x, norm_w)
        flat = h.reshape(-1, H)
        T = flat.shape[0]
        logits = flat.astype(jnp.float32) @ router_w.T
        scores = jax.nn.softmax(logits, axis=-1)
        topk_w, topk_ids = lax.top_k(scores, K)
        topk_w = topk_w / jnp.sum(topk_w, axis=-1, keepdims=True)
        ids = topk_ids.reshape(-1)
        sort_idx = jnp.argsort(ids)
        tok_idx = sort_idx // K
        xs = jnp.take(flat, tok_idx, axis=0)
        group_sizes = jnp.bincount(ids, length=E).astype(jnp.int32)
        gu = lax.ragged_dot(xs, w1, group_sizes)
        g, u = jnp.split(gu, 2, axis=-1)
        act = jax.nn.silu(g) * u
        ys = lax.ragged_dot(act, w2, group_sizes)
        y = jnp.zeros((T * K, H), ys.dtype).at[sort_idx].set(ys)
        routed = jnp.sum(y.reshape(T, K, H) * topk_w[..., None].astype(ys.dtype), axis=1)
        shared = jax.nn.silu(flat @ sg) * (flat @ su) @ sd
        out = residual + (routed + shared).reshape(B, S, H)
        return out
    x = L0_attn_x
    x = x + _L0_attn_ref(_layernorm(x, axis=-1), L0_attn_wq, L0_attn_w_kv_down, L0_attn_w_k_rope, L0_attn_w_k_nope, L0_attn_wv, L0_attn_wo, L0_attn_q_norm_w, L0_attn_k_norm_w)
    x = x + _L0_ffn_ref(_layernorm(x, axis=-1), L0_ffn_norm_w, L0_ffn_router_w, L0_ffn_w1, L0_ffn_w2, L0_ffn_sg, L0_ffn_su, L0_ffn_sd)
    return x

_drawn_inputs = setup_inputs


def setup_inputs(seed=0):
    import zlib

    import numpy as np

    out = dict(_drawn_inputs(seed))
    spreads = {'L0_attn_q_norm_w': (1.0, 0.6),
     'L0_attn_k_norm_w': (1.0, 0.6),
     'L0_ffn_norm_w': (1.0, 0.2)}
    factors = {'L0_attn_wq': 3.223,
     'L0_attn_w_kv_down': 3.332,
     'L0_attn_w_k_rope': 4.172,
     'L0_attn_w_k_nope': 3.852,
     'L0_attn_wv': 2.836,
     'L0_attn_wo': 2.84}
    for name, (base, spread) in spreads.items():
        noise = np.random.default_rng([zlib.crc32(name.encode()), seed]).standard_normal(out[name].shape)
        drawn = base * np.exp(spread * noise) if base else spread * noise
        out[name] = jnp.asarray(drawn.astype(out[name].dtype))
    for name, factor in factors.items():
        out[name] = (out[name] * factor).astype(out[name].dtype)
    return out
```

```python
from contextlib import ExitStack

import concourse.bass as bass
from concourse import mybir
import numpy as np

ALU = mybir.AluOpType
ACT = mybir.ActivationFunctionType
AXIS_X = mybir.AxisListType.X
F32 = mybir.dt.float32
F32R = mybir.dt.float32r
BF16 = mybir.dt.bfloat16
U32 = mybir.dt.uint32

P = 128
B, S, D = 4, 1024, 512
H, DK, DL, DR = 16, 128, 128, 64
T = B * S
E, I, K = 32, 256, 4
SH = 512
BANK = 512
DC = D // P
TB = S // P
NT = T // P
PAIRS = H // 2
GT = BANK // P
RQ = DR // 4
LN_EPS, ATT_EPS, FFN_EPS = 1e-5, 1e-6, 1e-6
MASKED = -1e30
SLOT_TILES = T * K // P + E
SLOTS = SLOT_TILES * P
WQK = DC * 2 * DK + 2 * DK
WV = 2 * DL
WO = 2 * D


def mm3(pe, out, lhs, rhs, start=True, stop=True, signal=None):
    (a, a_rest), (b, b_rest) = lhs, rhs
    pe.matmul(out, a, b, start=start, stop=False)
    pe.matmul(out, a, b_rest, start=False, stop=False)
    last = pe.matmul(out, a_rest, b, start=False, stop=stop)
    if signal is not None:
        last.then_inc(signal, 1)


def wait_apart(eng, scratch, column, sem, value):
    eng.wait_ge(sem, value)
    eng.tensor_tensor(scratch[:, column:column + 1], scratch[:, 0:1], scratch[:, 0:1], ALU.add)


def prepare_weights(nc, attn_w, w_hi_dram, w_lo_dram):
    WIDE = WQK + WV + WO
    with ExitStack() as ctx:
        def sb(name, shape, dt):
            return ctx.enter_context(nc.sbuf_tensor(name, shape, dt))

        def sem(name):
            return ctx.enter_context(nc.semaphore(name))

        raw = sb("pw_raw", [P, 2, WIDE], F32)
        hi = sb("pw_hi", [P, 2, WIDE], F32R)
        lo = sb("pw_lo", [P, 2, WIDE], F32R)
        vo_hi = sb("pw_vo_hi", [P, 2, 2, D], F32R)
        vo_lo = sb("pw_vo_lo", [P, 2, 2, D], F32R)
        vo_ps = ctx.enter_context(nc.psum_tensor("pw_vo_ps", [P, 2, 2, BANK], F32))
        loaded = [sem("pw_loaded0"), sem("pw_loaded1")]
        hi_done, lo_done = sem("pw_hi_done"), sem("pw_lo_done")
        vo_filled, vo_hi_done, vo_lo_done = sem("pw_vo_filled"), sem("pw_vo_hi_done"), sem("pw_vo_lo_done")
        stored = [sem("pw_stored0"), sem("pw_stored1")]
        STORES = 4 * 16

        def wv_of(x, s, h):
            return x[:, s, WQK + h * DL:WQK + (h + 1) * DL]

        def wo_of(x, s, h):
            return x[:, s, WQK + WV + h * D:WQK + WV + (h + 1) * D]

        block = ctx.enter_context(nc.Block())

        @block.sync
        def _(sp):
            with sp.Fori(0, PAIRS // 2) as g:
                for s in range(2):
                    sp.wait_ge(lo_done, 2 * g)
                    sp.dma_start(raw[:, s, :], attn_w[bass.ds(2 * g + s, 1)].rearrange("o p n -> (o p) n")) \
                      .then_inc(loaded[s], 16)

        @block.scalar
        def _(act):
            with act.Fori(0, PAIRS // 2) as g:
                for s in range(2):
                    act.wait_ge(loaded[s], 16 * g + 16)
                    act.wait_ge(stored[s], STORES * g)
                    nc.scalar.activation(hi[:, s, :], raw[:, s, :], ACT.Copy).then_inc(hi_done, 1)
                    act.wait_ge(vo_filled, 2 * g + s + 1)
                    nc.scalar.activation(vo_hi[:, s], vo_ps[:, s], ACT.Copy).then_inc(vo_hi_done, 1)

        @block.vector
        def _(dve):
            with dve.Fori(0, PAIRS // 2) as g:
                for s in range(2):
                    dve.wait_ge(hi_done, 2 * g + s + 1)
                    nc.vector.tensor_tensor(lo[:, s, :], raw[:, s, :], hi[:, s, :], ALU.subtract) \
                      .then_inc(lo_done, 1)
                    dve.wait_ge(vo_hi_done, 2 * g + s + 1)
                    nc.vector.tensor_tensor(vo_lo[:, s], vo_ps[:, s], vo_hi[:, s], ALU.subtract) \
                      .then_inc(vo_lo_done, 1)

        @block.tensor
        def _(pe):
            with pe.Fori(0, PAIRS // 2) as g:
                for s in range(2):
                    pe.wait_ge(lo_done, 2 * g + s + 1)
                    pe.wait_ge(vo_lo_done, 2 * g)
                    for h in range(2):
                        mm3(nc.tensor, vo_ps[:, s, h, :], (wv_of(hi, s, h), wv_of(lo, s, h)),
                            (wo_of(hi, s, h), wo_of(lo, s, h)), signal=vo_filled if h == 1 else None)

        @block.gpsimd
        def _(pool):
            with pool.Fori(0, PAIRS // 2) as g:
                for s in range(2):
                    pool.wait_ge(lo_done, 2 * g + s + 1)
                    for src, dst in ((hi, w_hi_dram), (lo, w_lo_dram)):
                        pool.dma_start(dst[bass.ds(2 * g + s, 1), :, 0:WQK].rearrange("o p n -> (o p) n"),
                                       src[:, s, 0:WQK].bitcast(F32)).then_inc(stored[s], 16)
                    pool.wait_ge(vo_lo_done, 2 * g + s + 1)
                    for src, dst in ((vo_hi, w_hi_dram), (vo_lo, w_lo_dram)):
                        pool.dma_start(dst[bass.ds(2 * g + s, 1), :, WQK:WQK + WO].rearrange("o p n -> (o p) n"),
                                       src[:, s].rearrange("p h n -> p (h n)").bitcast(F32)) \
                            .then_inc(stored[s], 16)
            for s in range(2):
                pool.wait_ge(stored[s], STORES * (PAIRS // 2))


def attention(nc, x, w_kv_down, q_norm_rows, k_norm_col, cos, sin, w_hi_dram, w_lo_dram, x2_dram):
    STEPS = 2 * TB
    LAST_STEP = STEPS + 2

    def step_of(u):
        group = u // GT
        return group // 2, group % 2, GT * (group // 2) + u % GT

    def out_tiles_at(u):
        return {11: [0, 1], 12: [2, 3], STEPS + 2: [4, 5, 6, 7]}.get(u, [])

    def chunks(t):
        return [range(a, min(a + GT, t + 1)) for a in range(0, t + 1, GT)]

    ring = [("qk", i) for i in range(TB)]
    turns = {("qkT", i): i for i in range(TB)}
    for u in range(LAST_STEP + 1):
        if u < STEPS:
            ring.append(("scores", u))
        if 1 <= u <= STEPS:
            for c in range(len(chunks(step_of(u - 1)[2]))):
                turns["probsT", u - 1, c] = len(turns)
        ring += [("out", t) for t in out_tiles_at(u)]
    RING, TURNS = len(ring), len(turns)
    LN_RING, LN_TURNS = 2 + 2, TB
    assert RING % 2 == 0 and TURNS % 2 == 0

    with ExitStack() as ctx:
        def sb(name, shape, dt):
            return ctx.enter_context(nc.sbuf_tensor(name, shape, dt))

        def ps(name, shape):
            return ctx.enter_context(nc.psum_tensor(name, shape, F32))

        def sem(name):
            return ctx.enter_context(nc.semaphore(name))

        ident = sb("at_ident", [P, P], F32)
        ident_b = sb("at_ident_b", [P, P], BF16)
        mask_b = sb("at_mask_b", [P, P], BF16)
        minus_half = sb("at_minus_half", [P, TB], F32)
        scratch = sb("at_scratch", [P, 2], F32)
        ln_eps = sb("at_ln_eps", [P, TB], F32)
        att_eps = sb("at_att_eps", [P, 4], F32)
        cos_t = sb("at_cos", [P, TB, RQ], F32)
        sin_t = sb("at_sin", [P, TB, RQ], F32)
        q_norm = sb("at_q_norm", [P, DK], F32)
        k_norm = sb("at_k_norm", [P, 1], F32)
        k_scale = sb("at_k_scale", [P, 1], F32)
        down_raw = sb("at_down_raw", [P, DC, DL], F32)
        down_hi = sb("at_down_hi", [P, DC, DL], F32R)
        down_lo = sb("at_down_lo", [P, DC, DL], F32R)

        acc = sb("at_acc", [P, TB, D], F32)
        stats = sb("at_stats", [P, TB, 6], F32)
        mean_var = sb("at_mean_var", [P, TB, 2], F32)
        ln_var = sb("at_ln_var", [P, TB], F32)
        ln_rstd = sb("at_ln_rstd", [P, TB], F32)
        xn = sb("at_xn", [P, 2, D], F32)
        xT_hi = sb("at_xT_hi", [P, DC, S], F32R)
        xT_lo = sb("at_xT_lo", [P, DC, S], F32R)
        latT_hi = sb("at_latT_hi", [P, S], F32R)
        latT_lo = sb("at_latT_lo", [P, S], F32R)
        lat_hi = sb("at_lat_hi", [P, TB, DL], F32R)
        lat_lo = sb("at_lat_lo", [P, TB, DL], F32R)

        wqk_hi = sb("at_wqk_hi", [P, WQK], F32R)
        wqk_lo = sb("at_wqk_lo", [P, WQK], F32R)
        wvo_hi = sb("at_wvo_hi", [P, 2, D], F32R)
        wvo_lo = sb("at_wvo_lo", [P, 2, D], F32R)

        squares = sb("at_squares", [P, 2, 4, DK], F32)
        sums = sb("at_sums", [P, TB, 4], F32)
        sums_eps = sb("at_sums_eps", [P, TB, 4], F32)
        rstd = sb("at_rstd", [P, TB, 4], F32)
        qk = sb("at_qk", [P, 4, 4, DK], F32)
        turned = sb("at_turned", [P, 4, 4, RQ], F32)
        qkT_hi = sb("at_qkT_hi", [P, 4, S], F32R)
        qkT_lo = sb("at_qkT_lo", [P, 4, S], F32R)

        row_max = sb("at_row_max", [P, 2], F32)
        shift = sb("at_shift", [P, 2], F32)
        row_sum = sb("at_row_sum", [P, 2], F32)
        row_inv = sb("at_row_inv", [P, 2], F32)
        probs = sb("at_probs", [P, 2, S], F32)
        pT_hi = sb("at_pT_hi", [P, TB, BANK], F32R)
        pT_lo = sb("at_pT_lo", [P, TB, BANK], F32R)
        oT_hi = sb("at_oT_hi", [P, 2, BANK], F32R)
        oT_lo = sb("at_oT_lo", [P, 2, BANK], F32R)

        slot = ps("at_slot", [P, 2, 2 * BANK])
        turn = ps("at_turn", [P, 2, 4, P])
        pv = ps("at_pv", [P, BANK])

        consts_loaded, consts_made = sem("at_consts_loaded"), sem("at_consts_made")
        down_hi_done, down_lo_done, k_scaled = sem("at_down_hi"), sem("at_down_lo"), sem("at_k_scaled")
        x_loaded, x2_stored = sem("at_x_loaded"), sem("at_x2_stored")
        ln_stats, ln_aggr, ln_var_added, ln_rstd_ready, xn_ready = (
            sem("at_ln_stats"), sem("at_ln_aggr"), sem("at_ln_var_added"), sem("at_ln_rstd"), sem("at_xn_ready"))
        wqk_loaded, wvo_loaded = sem("at_wqk_loaded"), sem("at_wvo_loaded")
        slot_filled = sem("at_slot_filled")
        turn_filled = sem("at_turn_filled")
        turn_hi, turn_lo = sem("at_turn_hi"), sem("at_turn_lo")
        lat_hi_done, lat_lo_done = sem("at_lat_hi_done"), sem("at_lat_lo_done")
        squared, summed, eps_added, rstd_ready = (
            sem("at_squared"), sem("at_summed"), sem("at_eps_added"), sem("at_rstd_ready"))
        qk_scaled, rope_parts, rope_done = sem("at_qk_scaled"), sem("at_rope_parts"), sem("at_rope_done")
        max_ready, shift_ready, exp_done, inv_ready, probs_ready = (
            sem("at_max"), sem("at_shift_ready"), sem("at_exp"), sem("at_inv"), sem("at_probs_ready"))
        pv_filled, oT_hi_done, oT_lo_done = sem("at_pv_filled"), sem("at_oT_hi_done"), sem("at_oT_lo_done")
        out_added = sem("at_out_added")

        def batch_ring(b):
            return b * (LN_RING + PAIRS * RING)

        def round_ring(b, p):
            return batch_ring(b) + LN_RING + p * RING

        def batch_turns(b):
            return b * (LN_TURNS + PAIRS * TURNS)

        def round_turns(b, p):
            return batch_turns(b) + LN_TURNS + p * TURNS

        def use(kind, n):
            return ring.index((kind, n))

        def wqk(x, c):
            return x[:, c * 2 * DK:(c + 1) * 2 * DK]

        block = ctx.enter_context(nc.Block())

        @block.sync
        def _(sp):
            sp.dma_start(cos_t[:], cos).then_inc(consts_loaded, 16)
            sp.dma_start(sin_t[:], sin).then_inc(consts_loaded, 16)
            sp.dma_start(q_norm[:], q_norm_rows).then_inc(consts_loaded, 16)
            sp.dma_start(k_norm[:], k_norm_col).then_inc(consts_loaded, 16)
            sp.dma_start(down_raw[:], w_kv_down).then_inc(consts_loaded, 16)
            with sp.Fori(0, B) as b:
                sp.wait_ge(x2_stored, 16 * b)
                sp.dma_start(acc[:], x[bass.ds(b, 1)].rearrange("o (t p) d -> p (o t) d", p=P)) \
                  .then_inc(x_loaded, 16)
                with sp.Fori(0, PAIRS) as p:
                    r = b * PAIRS + p
                    sp.wait_ge(qk_scaled, r * TB)
                    for dst, src in ((wqk_hi, w_hi_dram), (wqk_lo, w_lo_dram)):
                        sp.dma_start(dst[:].bitcast(F32), src[bass.ds(p, 1), :, 0:WQK]
                                     .rearrange("o p n -> (o p) n")).then_inc(wqk_loaded, 16)
                    sp.wait_ge(out_added, r * TB)
                    for dst, src in ((wvo_hi, w_hi_dram), (wvo_lo, w_lo_dram)):
                        sp.dma_start(dst[:].rearrange("p h n -> p (h n)").bitcast(F32),
                                     src[bass.ds(p, 1), :, WQK:WQK + WO]
                                     .rearrange("o p n -> (o p) n")).then_inc(wvo_loaded, 16)
                sp.wait_ge(out_added, (b + 1) * (PAIRS * TB))
                sp.dma_start(x2_dram[bass.ds(b, 1)].rearrange("o (t p) d -> p (o t) d", p=P), acc[:]) \
                  .then_inc(x2_stored, 16)
            sp.wait_ge(x2_stored, 16 * B)

        @block.gpsimd
        def _(pool):
            nc.gpsimd.memset(ident[:], 0.0).then_inc(consts_made, 1)
            nc.gpsimd.memset(ident_b[:], 0.0).then_inc(consts_made, 1)
            nc.gpsimd.memset(mask_b[:], 0.0).then_inc(consts_made, 1)
            nc.gpsimd.memset(minus_half[:], -0.5).then_inc(consts_made, 1)
            nc.gpsimd.memset(ln_eps[:], LN_EPS).then_inc(consts_made, 1)
            nc.gpsimd.memset(att_eps[:], ATT_EPS * DK).then_inc(consts_made, 1)
            pool.wait_ge(consts_made, 6)
            for m in (ident, ident_b):
                nc.gpsimd.affine_select(out=m[:], in_=m[:], compare_op=ALU.not_equal, fill=1.0, base=0,
                                        pattern=[[-1, P]], channel_multiplier=1).then_inc(consts_made, 1)
            nc.gpsimd.affine_select(out=mask_b[:], in_=mask_b[:], compare_op=ALU.is_ge, fill=MASKED, base=0,
                                    pattern=[[-1, P]], channel_multiplier=1).then_inc(consts_made, 1)
            pool.wait_ge(consts_loaded, 16 * 5)
            with pool.Fori(0, B) as b:
                pool.wait_ge(ln_aggr, b * TB + TB)
                nc.gpsimd.tensor_tensor(ln_var[:], mean_var[:, :, 1:2].rearrange("p t o -> p (t o)"),
                                        ln_eps[:], ALU.add).then_inc(ln_var_added, 1)
                pool.wait_ge(ln_var_added, b + 1)
                nc.gpsimd.tensor_tensor(ln_rstd[:], ln_var[:], minus_half[:], ALU.pow) \
                  .then_inc(ln_rstd_ready, 1)
                with pool.Fori(0, PAIRS) as p:
                    r = b * PAIRS + p
                    for i in range(TB + 1):
                        if i < TB:
                            pool.wait_ge(summed, r * TB + i + 1)
                            nc.gpsimd.tensor_tensor(sums_eps[:, i, :], sums[:, i, :], att_eps[:], ALU.add) \
                                .then_inc(eps_added, 1)
                            pool.wait_ge(eps_added, r * TB + i + 1)
                            nc.gpsimd.tensor_tensor(rstd[:, i, :], sums_eps[:, i, :], minus_half[:, 0:4],
                                                    ALU.pow).then_inc(rstd_ready, 1)
                        if i >= 1:
                            n = i - 1
                            pool.wait_ge(qk_scaled, r * TB + n + 1)
                            a = qk[:, n % 4, :, 0:RQ]
                            c = qk[:, n % 4, :, DR // 2:DR // 2 + RQ]
                            co = cos_t[:, n, :].unsqueeze(1).to_broadcast([P, 4, RQ])
                            si = sin_t[:, n, :].unsqueeze(1).to_broadcast([P, 4, RQ])
                            for k, (u, v) in enumerate(((a, co), (c, si), (c, co), (a, si))):
                                nc.gpsimd.tensor_tensor(turned[:, k], u, v, ALU.mult).then_inc(rope_parts, 1)
                            pool.wait_ge(rope_parts, (r * TB + n) * 4 + 4)
                            nc.gpsimd.tensor_tensor(a, turned[:, 0], turned[:, 1], ALU.add).then_inc(rope_done, 1)
                            nc.gpsimd.tensor_tensor(c, turned[:, 2], turned[:, 3], ALU.subtract) \
                              .then_inc(rope_done, 1)
                            pool.wait_ge(rope_done, (r * TB + n) * 2 + 2)

        @block.scalar
        def _(act):
            def high(dst, src, signal, **more):
                nc.scalar.activation(dst, src, ACT.Copy, **more).then_inc(signal, 1)

            act.wait_ge(consts_loaded, 16 * 5)
            high(down_hi[:], down_raw[:], down_hi_done)
            act.wait_ge(k_scaled, 2)
            with act.Fori(0, B) as b:
                for t in range(TB):
                    act.wait_ge(turn_filled, batch_turns(b) + t + 1)
                    high(xT_hi[:, :, t * P:(t + 1) * P], turn[:, t % 2], turn_hi)
                for n in range(2):
                    act.wait_ge(slot_filled, batch_ring(b) + n + 1)
                    high(latT_hi[:, n * BANK:(n + 1) * BANK], slot[:, n, 0:BANK], lat_hi_done)
                for n in range(2):
                    act.wait_ge(slot_filled, batch_ring(b) + 2 + n + 1)
                    high(lat_hi[:, n * GT:(n + 1) * GT, :].rearrange("p t d -> p (t d)"), slot[:, n, 0:BANK],
                         lat_hi_done)
                with act.Fori(0, PAIRS) as p:
                    r = b * PAIRS + p
                    ring0, turns0 = round_ring(b, p), round_turns(b, p)
                    for i in range(TB + 2):
                        if i < TB:
                            act.wait_ge(slot_filled, ring0 + use("qk", i) + 1)
                            if i >= 2:
                                act.wait_ge(summed, r * TB + i - 1)
                            nc.scalar.activation(squares[:, i % 2].rearrange("p h d -> p (h d)"),
                                                 slot[:, use("qk", i) % 2, 0:4 * DK], ACT.Square) \
                                .then_inc(squared, 1)
                        if i >= 2:
                            n = i - 2
                            w = turns["qkT", n]
                            act.wait_ge(turn_filled, turns0 + w + 1)
                            nc.scalar.activation(qkT_hi[:, 0:2, n * P:(n + 1) * P], turn[:, w % 2, 0:2, :],
                                                 ACT.Copy)
                            high(qkT_hi[:, 2:4, n * P:(n + 1) * P], turn[:, w % 2, 2:4, :], turn_hi,
                                 scale=k_scale[:, 0:1])
                    for u in range(LAST_STEP + 1):
                        if u < STEPS:
                            _, _, t = step_of(u)
                            width = (t + 1) * P
                            act.wait_ge(shift_ready, r * STEPS + u + 1)
                            if u >= 2:
                                before = turns["probsT", u - 2, len(chunks(step_of(u - 2)[2])) - 1]
                                act.wait_ge(turn_filled, turns0 + before + 1)
                            nc.scalar.activation(probs[:, u % 2, 0:width],
                                                 slot[:, use("scores", u) % 2, 0:width], ACT.Exp,
                                                 bias=shift[:, u % 2:u % 2 + 1],
                                                 scale=rstd[:, t, step_of(u)[1]:step_of(u)[1] + 1],
                                                 accum_out=row_sum[:, u % 2:u % 2 + 1]).then_inc(exp_done, 1)
                        if u >= GT + 1 and (u - GT - 1) % GT == 0:
                            n = (u - GT - 1) // GT
                            act.wait_ge(pv_filled, r * 4 + n + 1)
                            high(oT_hi[:, n % 2, :], pv[:], oT_hi_done)
                        if 1 <= u <= STEPS:
                            _, _, t = step_of(u - 1)
                            j = (u - 1) % GT
                            for c, blocks in enumerate(chunks(t)):
                                w = turns["probsT", u - 1, c]
                                act.wait_ge(turn_filled, turns0 + w + 1)
                                high(pT_hi[:, blocks[0]:blocks[-1] + 1, j * P:(j + 1) * P],
                                     turn[:, w % 2, 0:len(blocks), :], turn_hi)

        @block.vector
        def _(dve):
            def low(dst, src, high, signal):
                nc.vector.tensor_tensor(dst, src, high, ALU.subtract).then_inc(signal, 1)

            dve.wait_ge(consts_loaded, 16 * 5)
            nc.vector.memset(scratch[:], 0.0).then_inc(k_scaled, 1)
            nc.vector.tensor_scalar(k_scale[:], k_norm[:], float(np.sqrt(DK)), None, ALU.mult).then_inc(k_scaled, 1)
            dve.wait_ge(k_scaled, 2)
            dve.wait_ge(down_hi_done, 1)
            low(down_lo[:], down_raw[:], down_hi[:], down_lo_done)
            with dve.Fori(0, B) as b:
                dve.wait_ge(x_loaded, 16 * b + 16)
                for t in range(TB):
                    nc.vector.bn_stats(stats[:, t, :], acc[:, t, :]).then_inc(ln_stats, 1)
                wait_apart(dve, scratch, 1, ln_stats, b * TB + TB)
                for t in range(TB):
                    nc.vector.bn_aggr(mean_var[:, t, :], stats[:, t, :]).then_inc(ln_aggr, 1)
                dve.wait_ge(ln_rstd_ready, b + 1)
                for t in range(TB + 1):
                    if t < TB:
                        if t >= 2:
                            dve.wait_ge(turn_filled, batch_turns(b) + t - 1)
                        nc.vector.tensor_scalar(xn[:, t % 2, :], acc[:, t, :], mean_var[:, t, 0:1],
                                                ln_rstd[:, t:t + 1], ALU.subtract, ALU.mult).then_inc(xn_ready, 1)
                    if t >= 1:
                        n = t - 1
                        dve.wait_ge(turn_hi, batch_turns(b) + n + 1)
                        low(xT_lo[:, :, n * P:(n + 1) * P], turn[:, n % 2], xT_hi[:, :, n * P:(n + 1) * P], turn_lo)
                for n in range(2):
                    dve.wait_ge(lat_hi_done, b * 4 + n + 1)
                    cols = slice(n * BANK, (n + 1) * BANK)
                    low(latT_lo[:, cols], slot[:, n, 0:BANK], latT_hi[:, cols], lat_lo_done)
                for n in range(2):
                    dve.wait_ge(lat_hi_done, b * 4 + 2 + n + 1)
                    low(lat_lo[:, n * GT:(n + 1) * GT, :].rearrange("p t d -> p (t d)"), slot[:, n, 0:BANK],
                        lat_hi[:, n * GT:(n + 1) * GT, :].rearrange("p t d -> p (t d)"), lat_lo_done)
                with dve.Fori(0, PAIRS) as p:
                    r = b * PAIRS + p
                    ring0, turns0 = round_ring(b, p), round_turns(b, p)
                    for i in range(TB + 2):
                        if i < TB:
                            tile = slot[:, use("qk", i) % 2, 0:4 * DK].rearrange("p (h d) -> p h d", h=4)
                            dve.wait_ge(squared, r * TB + i + 1)
                            nc.vector.tensor_reduce(sums[:, i, :], squares[:, i % 2], AXIS_X, ALU.add) \
                              .then_inc(summed, 1)
                            if i >= 4:
                                dve.wait_ge(turn_filled, turns0 + turns["qkT", i - 4] + 1)
                            nc.vector.tensor_tensor(qk[:, i % 4, 0:2, :], tile[:, 0:2, :],
                                                    q_norm[:].unsqueeze(1).to_broadcast([P, 2, DK]), ALU.mult)
                            dve.wait_ge(rstd_ready, r * TB + i + 1)
                            nc.vector.tensor_tensor(qk[:, i % 4, 2:4, :], tile[:, 2:4, :],
                                                    rstd[:, i, 2:4].unsqueeze(2).to_broadcast([P, 2, DK]),
                                                    ALU.mult).then_inc(qk_scaled, 1)
                        if i >= 2:
                            n = i - 2
                            w = turns["qkT", n]
                            cols = slice(n * P, (n + 1) * P)
                            dve.wait_ge(turn_hi, turns0 + w + 1)
                            nc.vector.tensor_tensor(qkT_lo[:, 0:2, cols], turn[:, w % 2, 0:2, :],
                                                    qkT_hi[:, 0:2, cols], ALU.subtract)
                            nc.vector.scalar_tensor_tensor(out=qkT_lo[:, 2:4, cols], in0=turn[:, w % 2, 2:4, :],
                                                           scalar=k_scale[:, 0:1], in1=qkT_hi[:, 2:4, cols],
                                                           op0=ALU.mult, op1=ALU.subtract).then_inc(turn_lo, 1)
                    for u in range(LAST_STEP + 1):
                        if u < STEPS:
                            _, h, t = step_of(u)
                            width = (t + 1) * P
                            one = slice(u % 2, u % 2 + 1)
                            dve.wait_ge(slot_filled, ring0 + use("scores", u) + 1)
                            nc.vector.tensor_reduce(row_max[:, one], slot[:, use("scores", u) % 2, 0:width],
                                                    AXIS_X, ALU.max).then_inc(max_ready, 1)
                            dve.wait_ge(max_ready, r * STEPS + u + 1)
                            nc.vector.tensor_scalar(shift[:, one], row_max[:, one], rstd[:, t, h:h + 1], -1.0,
                                                    ALU.mult, ALU.mult).then_inc(shift_ready, 1)

                        def turned_rest():
                            _, _, t = step_of(u - 1)
                            j = (u - 1) % GT
                            for c, blocks in enumerate(chunks(t)):
                                w = turns["probsT", u - 1, c]
                                there = slice(blocks[0], blocks[-1] + 1)
                                dve.wait_ge(turn_hi, turns0 + w + 1)
                                low(pT_lo[:, there, j * P:(j + 1) * P], turn[:, w % 2, 0:len(blocks), :],
                                    pT_hi[:, there, j * P:(j + 1) * P], turn_lo)

                        def normalise():
                            dve.wait_ge(exp_done, r * STEPS + u + 1)
                            nc.vector.reciprocal(row_inv[:, one], row_sum[:, one]).then_inc(inv_ready, 1)
                            dve.wait_ge(inv_ready, r * STEPS + u + 1)
                            nc.vector.tensor_scalar(probs[:, u % 2, 0:width], probs[:, u % 2, 0:width],
                                                    row_inv[:, one], None, ALU.mult).then_inc(probs_ready, 1)

                        group_ends = u >= GT + 1 and (u - GT - 1) % GT == 0
                        if group_ends:
                            if u < STEPS:
                                normalise()
                            n = (u - GT - 1) // GT
                            dve.wait_ge(oT_hi_done, r * 4 + n + 1)
                            low(oT_lo[:, n % 2, :], pv[:], oT_hi[:, n % 2, :], oT_lo_done)
                        if 1 <= u <= STEPS:
                            turned_rest()
                        if u < STEPS and not group_ends:
                            normalise()
                        for t in out_tiles_at(u):
                            dve.wait_ge(slot_filled, ring0 + use("out", t) + 1)
                            nc.vector.tensor_tensor(acc[:, t, :], slot[:, use("out", t) % 2, 0:D], acc[:, t, :],
                                                    ALU.add).then_inc(out_added, 1)

        @block.tensor
        def _(pe):
            pe.wait_ge(consts_made, 9)
            pe.wait_ge(down_lo_done, 1)
            with pe.Fori(0, B) as b:
                for t in range(TB):
                    pe.wait_ge(xn_ready, b * TB + t + 1)
                    if t >= 2:
                        pe.wait_ge(turn_lo, batch_turns(b) + t - 1)
                    for c in range(DC):
                        last = nc.tensor.transpose(turn[:, t % 2, c, :], xn[:, t % 2, c * P:(c + 1) * P], ident[:])
                    last.then_inc(turn_filled, 1)
                pe.wait_ge(turn_lo, batch_turns(b) + TB)
                for n in range(2):
                    cols = slice(n * BANK, (n + 1) * BANK)
                    for c in range(DC):
                        mm3(nc.tensor, slot[:, n, 0:BANK], (down_hi[:, c, :], down_lo[:, c, :]),
                            (xT_hi[:, c, cols], xT_lo[:, c, cols]), start=c == 0, stop=c == DC - 1,
                            signal=slot_filled if c == DC - 1 else None)
                for n in range(2):
                    pe.wait_ge(lat_lo_done, b * 4 + n + 1)
                    for j in range(GT):
                        cols = slice((n * GT + j) * P, (n * GT + j + 1) * P)
                        for c in range(DC):
                            mm3(nc.tensor, slot[:, n, j * P:(j + 1) * P], (xT_hi[:, c, cols], xT_lo[:, c, cols]),
                                (down_hi[:, c, :], down_lo[:, c, :]), start=c == 0, stop=c == DC - 1,
                                signal=slot_filled if c == DC - 1 and j == GT - 1 else None)
                with pe.Fori(0, PAIRS) as p:
                    r = b * PAIRS + p
                    turns0 = round_turns(b, p)
                    pe.wait_ge(lat_lo_done, b * 4 + 4)

                    def slot_free(kind, n):
                        at = use(kind, n) - 2
                        if at < 0:
                            pe.wait_ge(out_added, r * TB)
                            return
                        kind, n = ring[at]
                        if kind == "qk":
                            pe.wait_ge(qk_scaled, r * TB + n + 1)
                        elif kind == "scores":
                            pe.wait_ge(exp_done, r * STEPS + n + 1)
                        else:
                            pe.wait_ge(out_added, r * TB + n + 1)

                    def turn_free(w):
                        pe.wait_ge(turn_lo, turns0 + w - 1)

                    pe.wait_ge(wqk_loaded, 32 * r + 32)
                    for i in range(TB + 2):
                        if i < TB:
                            slot_free("qk", i)
                            s = use("qk", i) % 2
                            cols = slice(i * P, (i + 1) * P)
                            for c in range(DC):
                                mm3(nc.tensor, slot[:, s, 0:2 * DK], (xT_hi[:, c, cols], xT_lo[:, c, cols]),
                                    (wqk(wqk_hi, c), wqk(wqk_lo, c)), start=c == 0, stop=c == DC - 1)
                            mm3(nc.tensor, slot[:, s, 2 * DK:4 * DK], (latT_hi[:, cols], latT_lo[:, cols]),
                                (wqk(wqk_hi, DC), wqk(wqk_lo, DC)), signal=slot_filled)
                        if i >= 2:
                            n = i - 2
                            w = turns["qkT", n]
                            pe.wait_ge(rope_done, (r * TB + n) * 2 + 2)
                            turn_free(w)
                            for k in range(4):
                                last = nc.tensor.transpose(turn[:, w % 2, k, :], qk[:, n % 4, k, :], ident[:])
                            last.then_inc(turn_filled, 1)
                    pe.wait_ge(turn_lo, turns0 + TB)
                    for u in range(LAST_STEP + 1):
                        if u < STEPS:
                            _, h, t = step_of(u)
                            s = use("scores", u) % 2
                            slot_free("scores", u)
                            q_cols = slice(t * P, (t + 1) * P)
                            width = (t + 1) * P
                            for a in range(0, width, BANK):
                                z = min(a + BANK, width)
                                whole = z < width
                                mm3(nc.tensor, slot[:, s, a:z], (qkT_hi[:, h, q_cols], qkT_lo[:, h, q_cols]),
                                    (qkT_hi[:, 2 + h, a:z], qkT_lo[:, 2 + h, a:z]), stop=whole)
                            nc.tensor.matmul(slot[:, s, width - P:width], ident_b[:], mask_b[:], start=False,
                                             stop=True).then_inc(slot_filled, 1)
                        if u >= GT + 1 and (u - GT - 1) % GT == 0:
                            n = (u - GT - 1) // GT
                            g = n // 2
                            last_turn = turns["probsT", u - 2, len(chunks(step_of(u - 2)[2])) - 1]
                            pe.wait_ge(turn_lo, turns0 + last_turn + 1)
                            pe.wait_ge(oT_lo_done, r * 4 + n)
                            for k in range(GT * g + GT):
                                a = max(0, k - GT * g) * P
                                mm3(nc.tensor, pv[:, a:BANK], (lat_hi[:, k, :], lat_lo[:, k, :]),
                                    (pT_hi[:, k, a:BANK], pT_lo[:, k, a:BANK]), start=k == 0,
                                    stop=k == GT * g + GT - 1,
                                    signal=pv_filled if k == GT * g + GT - 1 else None)
                        if 1 <= u <= STEPS:
                            _, _, t = step_of(u - 1)
                            pe.wait_ge(probs_ready, r * STEPS + u)
                            for c, blocks in enumerate(chunks(t)):
                                w = turns["probsT", u - 1, c]
                                turn_free(w)
                                for k in blocks:
                                    last = nc.tensor.transpose(turn[:, w % 2, k - blocks[0], :],
                                                               probs[:, (u - 1) % 2, k * P:(k + 1) * P], ident[:])
                                last.then_inc(turn_filled, 1)
                        for t in out_tiles_at(u):
                            g, j = t // GT, t % GT
                            if j == 0:
                                pe.wait_ge(oT_lo_done, r * 4 + 2 * g + 2)
                                pe.wait_ge(wvo_loaded, 32 * r + 32)
                            slot_free("out", t)
                            s = use("out", t) % 2
                            cols = slice(j * P, (j + 1) * P)
                            for h in range(2):
                                mm3(nc.tensor, slot[:, s, 0:D], (oT_hi[:, h, cols], oT_lo[:, h, cols]),
                                    (wvo_hi[:, h, :], wvo_lo[:, h, :]), start=h == 0, stop=h == 1,
                                    signal=slot_filled if h == 1 else None)


def ffn_tokens(nc, keep, x2_dram, norm_rows, router_w, shared_w, h_dram, base_dram):
    G = T // BANK
    SF = SH // P
    with ExitStack() as ctx:
        def sb(name, shape, dt=F32):
            return ctx.enter_context(nc.sbuf_tensor("ft_" + name, shape, dt))

        def ps(name, shape):
            return ctx.enter_context(nc.psum_tensor("ft_" + name, shape, F32))

        def sem(name):
            return ctx.enter_context(nc.semaphore("ft_" + name))

        w_raw = sb("w_raw", [P, 3 * DC * SH])
        w_hi = sb("w_hi", [P, 3, DC, SH], F32R)
        w_lo = sb("w_lo", [P, 3, DC, SH], F32R)
        router_raw = sb("router_raw", [P, DC, E])
        router_hi = sb("router_hi", [P, DC, E], F32R)
        router_lo = sb("router_lo", [P, DC, E], F32R)
        norm_raw = sb("norm_raw", [P, D])
        norm = sb("norm", [P, D])
        ident = sb("ident", [P, P])
        before = sb("before", [P, P], BF16)
        ones = sb("ones", [P, P], BF16)
        iota_i = sb("iota_i", [P, E], mybir.dt.int32)
        iota = sb("iota", [P, E])
        minus_half = sb("minus_half", [P, GT])
        ln_eps = sb("ln_eps", [P, GT])
        ffn_eps = sb("ffn_eps", [P, GT])

        scratch = sb("scratch", [P, 5])
        x2 = sb("x2", [P, GT, D])
        stats = sb("stats", [P, GT, 6])
        mean_var = sb("mean_var", [P, GT, 2])
        var = sb("var", [P, GT])
        rstd = sb("rstd", [P, GT])
        h0 = sb("h0", [P, GT, D])
        squares = sb("squares", [P, D])
        sums = sb("sums", [P, GT])
        sums_eps = sb("sums_eps", [P, GT])
        rms = sb("rms", [P, GT])
        h = sb("h", [P, GT, D])
        residual = sb("residual", [P, GT, D])
        base = sb("base", [P, GT, D])
        hT_hi = sb("hT_hi", [P, DC, BANK], F32R)
        hT_lo = sb("hT_lo", [P, DC, BANK], F32R)
        logits = sb("logits", [P, GT, E])
        top = sb("top", [P, GT, 8])
        top_id = sb("top_id", [P, GT, 8], U32)
        top_idf = sb("top_idf", [P, GT, K])
        top_less = sb("top_less", [P, GT, K])
        top_exp = sb("top_exp", [P, GT, K])
        top_sum = sb("top_sum", [P, GT])
        top_inv = sb("top_inv", [P, GT])
        chosen = sb("chosen", [P, GT, E], BF16)
        silu = sb("silu", [P, 2, BANK])
        inner = sb("inner", [P, 2, BANK])
        inner_hi = sb("inner_hi", [P, SF, BANK], F32R)
        inner_lo = sb("inner_lo", [P, SF, BANK], F32R)

        turn = ps("turn", [P, 2, DC, P])
        gate_up = ps("gate_up", [P, 2, 2, BANK])
        small = ps("small", [P, GT, E])
        rank_ps = ps("rank_ps", [P, GT + 1, E])

        loaded, made, w_hi_done, w_lo_done, norm_done = (
            sem("loaded"), sem("made"), sem("w_hi_done"), sem("w_lo_done"), sem("norm_done"))
        x2_loaded, h_stored, base_stored = sem("x2_loaded"), sem("h_stored"), sem("base_stored")
        stats_done, aggr_done, var_done, rstd_done, h0_done = (
            sem("stats_done"), sem("aggr_done"), sem("var_done"), sem("rstd_done"), sem("h0_done"))
        squared, eps_done, rms_done, h_done, residual_done = (
            sem("squared"), sem("eps_done"), sem("rms_done"), sem("h_done"), sem("residual_done"))
        turn_filled, turn_hi, turn_lo = sem("turn_filled"), sem("turn_hi"), sem("turn_lo")
        logits_filled, logits_copied, top_done, id_done = (
            sem("logits_filled"), sem("logits_copied"), sem("top_done"), sem("id_done"))
        less_done, exp_done, sum_done, inv_done, weights_done = (
            sem("less_done"), sem("exp_done"), sem("sum_done"), sem("inv_done"), sem("weights_done"))
        hot_done, chosen_done, rank_filled, rank_done, count_done = (
            sem("hot_done"), sem("chosen_done"), sem("rank_filled"), sem("rank_done"), sem("count_done"))
        gu_filled, silu_done, inner_done, inner_hi_done, inner_lo_done = (
            sem("gu_filled"), sem("silu_done"), sem("inner_done"), sem("inner_hi_done"), sem("inner_lo_done"))
        down_filled, base_done = sem("down_filled"), sem("base_done")

        block = ctx.enter_context(nc.Block())

        @block.sync
        def _(sp):
            sp.dma_start(w_raw[:], shared_w).then_inc(loaded, 16)
            sp.dma_start(router_raw[:], router_w).then_inc(loaded, 16)
            sp.dma_start(norm_raw[:], norm_rows).then_inc(loaded, 16)
            with sp.Fori(0, G) as g:
                sp.wait_ge(residual_done, g)
                sp.dma_start(x2[:], x2_dram[bass.ds(g, 1)].rearrange("o (t p) d -> p (o t) d", p=P)) \
                  .then_inc(x2_loaded, 16)
                sp.wait_ge(h_done, g * GT + GT)
                sp.dma_start(h_dram[bass.ds(g, 1)].rearrange("o (t p) d -> p (o t) d", p=P), h[:]) \
                  .then_inc(h_stored, 16)
                sp.wait_ge(base_done, g * GT + GT)
                sp.dma_start(base_dram[bass.ds(g, 1)].rearrange("o (t p) d -> p (o t) d", p=P), base[:]) \
                  .then_inc(base_stored, 16)
            sp.wait_ge(h_stored, 16 * G)
            sp.wait_ge(base_stored, 16 * G)

        @block.gpsimd
        def _(pool):
            nc.gpsimd.memset(ident[:], 0.0).then_inc(made, 1)
            nc.gpsimd.memset(before[:], 1.0).then_inc(made, 1)
            nc.gpsimd.memset(ones[:], 1.0).then_inc(made, 1)
            nc.gpsimd.memset(minus_half[:], -0.5).then_inc(made, 1)
            nc.gpsimd.memset(ln_eps[:], LN_EPS).then_inc(made, 1)
            nc.gpsimd.memset(ffn_eps[:], FFN_EPS * D).then_inc(made, 1)
            nc.gpsimd.iota(iota_i[:], pattern=[[1, E]], base=0, channel_multiplier=0).then_inc(made, 1)
            pool.wait_ge(made, 7)
            nc.gpsimd.affine_select(out=ident[:], in_=ident[:], compare_op=ALU.not_equal, fill=1.0, base=0,
                                    pattern=[[-1, P]], channel_multiplier=1).then_inc(made, 1)
            nc.gpsimd.affine_select(out=before[:], in_=before[:], compare_op=ALU.is_gt, fill=0.0, base=0,
                                    pattern=[[1, P]], channel_multiplier=-1).then_inc(made, 1)
            nc.gpsimd.tensor_copy(iota[:], iota_i[:]).then_inc(made, 1)
            pool.wait_ge(made, 10)
            with pool.Fori(0, G) as g:
                pool.wait_ge(aggr_done, g * GT + GT)
                nc.gpsimd.tensor_tensor(var[:], mean_var[:, :, 1:2].rearrange("p t o -> p (t o)"), ln_eps[:],
                                        ALU.add).then_inc(var_done, 1)
                pool.wait_ge(var_done, g + 1)
                nc.gpsimd.tensor_tensor(rstd[:], var[:], minus_half[:], ALU.pow).then_inc(rstd_done, 1)
                pool.wait_ge(squared, g * GT + GT)
                nc.gpsimd.tensor_tensor(sums_eps[:], sums[:], ffn_eps[:], ALU.add).then_inc(eps_done, 1)
                pool.wait_ge(eps_done, g + 1)
                nc.gpsimd.tensor_tensor(rms[:], sums_eps[:], minus_half[:], ALU.pow).then_inc(rms_done, 1)
                pool.wait_ge(base_done, g * GT)
                nc.gpsimd.tensor_tensor(residual[:], x2[:], h0[:], ALU.add).then_inc(residual_done, 1)

        @block.scalar
        def _(act):
            act.wait_ge(loaded, 48)
            nc.scalar.activation(w_hi[:].rearrange("p w c n -> p (w c n)"), w_raw[:], ACT.Copy) \
                .then_inc(w_hi_done, 1)
            nc.scalar.activation(router_hi[:], router_raw[:], ACT.Copy).then_inc(w_hi_done, 1)
            with act.Fori(0, G) as g:
                for t in range(GT):
                    act.wait_ge(h0_done, g * GT + t + 1)
                    if t == 0:
                        act.wait_ge(squared, g * GT)
                    else:
                        act.wait_ge(squared, g * GT + t)
                    nc.scalar.activation(squares[:], h0[:, t, :], ACT.Square, accum_out=sums[:, t:t + 1]) \
                        .then_inc(squared, 1)
                for t in range(GT):
                    act.wait_ge(turn_filled, g * GT + t + 1)
                    nc.scalar.activation(hT_hi[:, :, t * P:(t + 1) * P], turn[:, t % 2], ACT.Copy) \
                        .then_inc(turn_hi, 1)
                act.wait_ge(logits_filled, g + 1)
                nc.scalar.activation(logits[:], small[:], ACT.Copy).then_inc(logits_copied, 1)
                act.wait_ge(less_done, g + 1)
                nc.scalar.activation(top_exp[:], top_less[:], ACT.Exp).then_inc(exp_done, 1)
                for f in range(SF):
                    act.wait_ge(gu_filled, g * SF + f + 1)
                    if f >= 2:
                        act.wait_ge(inner_done, g * SF + f - 1)
                    nc.scalar.activation(silu[:, f % 2, :], gate_up[:, f % 2, 0, :], ACT.Silu) \
                        .then_inc(silu_done, 1)
                    act.wait_ge(inner_done, g * SF + f + 1)
                    nc.scalar.activation(inner_hi[:, f, :], inner[:, f % 2, :], ACT.Copy) \
                        .then_inc(inner_hi_done, 1)

        @block.vector
        def _(dve):
            dve.wait_ge(loaded, 48)
            nc.vector.tensor_scalar(norm[:], norm_raw[:], float(np.sqrt(D)), None, ALU.mult).then_inc(norm_done, 1)
            nc.vector.memset(keep.count[:], 0.0).then_inc(count_done, 1)
            nc.vector.memset(scratch[:], 0.0).then_inc(norm_done, 1)
            dve.wait_ge(made, 10)
            dve.wait_ge(w_hi_done, 2)
            nc.vector.tensor_tensor(w_lo[:].rearrange("p w c n -> p (w c n)"), w_raw[:],
                                    w_hi[:].rearrange("p w c n -> p (w c n)"), ALU.subtract) \
                .then_inc(w_lo_done, 1)
            nc.vector.tensor_tensor(router_lo[:], router_raw[:], router_hi[:], ALU.subtract) \
                .then_inc(w_lo_done, 1)
            dve.wait_ge(norm_done, 2)
            with dve.Fori(0, G) as g:
                dve.wait_ge(x2_loaded, 16 * g + 16)
                for t in range(GT):
                    nc.vector.bn_stats(stats[:, t, :], x2[:, t, :]).then_inc(stats_done, 1)
                wait_apart(dve, scratch, 1, stats_done, g * GT + GT)
                for t in range(GT):
                    nc.vector.bn_aggr(mean_var[:, t, :], stats[:, t, :]).then_inc(aggr_done, 1)
                dve.wait_ge(rstd_done, g + 1)
                for t in range(GT):
                    nc.vector.tensor_scalar(h0[:, t, :], x2[:, t, :], mean_var[:, t, 0:1], rstd[:, t:t + 1],
                                            ALU.subtract, ALU.mult).then_inc(h0_done, 1)
                dve.wait_ge(rms_done, g + 1)
                dve.wait_ge(h_stored, 16 * g)
                for t in range(GT):
                    nc.vector.scalar_tensor_tensor(out=h[:, t, :], in0=h0[:, t, :], scalar=rms[:, t:t + 1],
                                                   in1=norm[:], op0=ALU.mult, op1=ALU.mult).then_inc(h_done, 1)
                for t in range(GT):
                    cols = slice(t * P, (t + 1) * P)
                    dve.wait_ge(turn_hi, g * GT + t + 1)
                    nc.vector.tensor_tensor(hT_lo[:, :, cols], turn[:, t % 2], hT_hi[:, :, cols], ALU.subtract) \
                        .then_inc(turn_lo, 1)
                wait_apart(dve, scratch, 2, logits_copied, g + 1)
                for t in range(GT):
                    nc.vector.max(top[:, t, :], logits[:, t, :]).then_inc(top_done, 1)
                wait_apart(dve, scratch, 3, top_done, g * GT + GT)
                for t in range(GT):
                    nc.vector.max_index(top_id[:, t, :], top[:, t, :], logits[:, t, :]).then_inc(id_done, 1)
                nc.vector.tensor_tensor(top_less[:], top[:, :, 0:K], top[:, :, 0:1].to_broadcast([P, GT, K]),
                                        ALU.subtract).then_inc(less_done, 1)
                dve.wait_ge(id_done, g * (GT + 1) + GT)
                nc.vector.tensor_copy(top_idf[:], top_id[:, :, 0:K]).then_inc(id_done, 1)
                dve.wait_ge(id_done, g * (GT + 1) + GT + 1)
                hot = keep.hot[:, bass.ds(g * GT * K, GT * K), :]
                nc.vector.tensor_tensor(hot, iota[:].unsqueeze(1).to_broadcast([P, GT * K, E]),
                                        top_idf[:].rearrange("p t k -> p (t k)").unsqueeze(2)
                                        .to_broadcast([P, GT * K, E]), ALU.is_equal).then_inc(hot_done, 1)
                dve.wait_ge(exp_done, g + 1)
                nc.vector.tensor_reduce(top_sum[:], top_exp[:], AXIS_X, ALU.add).then_inc(sum_done, 1)
                dve.wait_ge(sum_done, g + 1)
                nc.vector.reciprocal(top_inv[:], top_sum[:]).then_inc(inv_done, 1)
                dve.wait_ge(inv_done, g + 1)
                nc.vector.tensor_tensor(keep.top_w[:, bass.ds(g * GT * K, GT * K)].rearrange("p (t k) -> p t k", k=K), top_exp[:],
                                        top_inv[:].unsqueeze(2).to_broadcast([P, GT, K]), ALU.mult) \
                    .then_inc(weights_done, 1)
                wait_apart(dve, scratch, 4, hot_done, g + 1)
                with nc.allow_low_precision("a sum of at most four ones"):
                    nc.vector.tensor_reduce(chosen[:], hot.rearrange("p (t k) e -> p t e k", k=K), AXIS_X,
                                            ALU.add).then_inc(chosen_done, 1)
                dve.wait_ge(rank_filled, g + 1)
                dve.wait_ge(count_done, g + 1)
                nc.vector.tensor_tensor(keep.rank[:, bass.ds(g * GT, GT), :], rank_ps[:, 0:GT, :],
                                        keep.count[:].unsqueeze(1).to_broadcast([P, GT, E]), ALU.add) \
                    .then_inc(rank_done, 1)
                dve.wait_ge(rank_done, g + 1)
                nc.vector.tensor_tensor(keep.count[:], rank_ps[:, GT, :], keep.count[:], ALU.add) \
                    .then_inc(count_done, 1)
                for f in range(SF):
                    dve.wait_ge(silu_done, g * SF + f + 1)
                    if f >= 2:
                        dve.wait_ge(inner_hi_done, g * SF + f - 1)
                        dve.wait_ge(inner_lo_done, g * SF + f - 1)
                    nc.vector.tensor_tensor(inner[:, f % 2, :], gate_up[:, f % 2, 1, :], silu[:, f % 2, :],
                                            ALU.mult).then_inc(inner_done, 1)
                    dve.wait_ge(inner_hi_done, g * SF + f + 1)
                    nc.vector.tensor_tensor(inner_lo[:, f, :], inner[:, f % 2, :], inner_hi[:, f, :],
                                            ALU.subtract).then_inc(inner_lo_done, 1)
                dve.wait_ge(residual_done, g + 1)
                dve.wait_ge(base_stored, 16 * g)
                for t in range(GT):
                    dve.wait_ge(down_filled, g * GT + t + 1)
                    nc.vector.tensor_tensor(base[:, t, :], gate_up[:, t % 2, 0, :], residual[:, t, :], ALU.add) \
                        .then_inc(base_done, 1)

        @block.tensor
        def _(pe):
            pe.wait_ge(made, 10)
            pe.wait_ge(w_lo_done, 2)
            with pe.Fori(0, G) as g:
                for t in range(GT):
                    pe.wait_ge(h_done, g * GT + t + 1)
                    if t < 2:
                        pe.wait_ge(turn_lo, g * GT)
                    else:
                        pe.wait_ge(turn_lo, g * GT + t - 1)
                    for c in range(DC):
                        last = nc.tensor.transpose(turn[:, t % 2, c, :], h[:, t, c * P:(c + 1) * P], ident[:])
                    last.then_inc(turn_filled, 1)
                pe.wait_ge(turn_lo, g * GT + GT)
                pe.wait_ge(logits_copied, g)
                for t in range(GT):
                    cols = slice(t * P, (t + 1) * P)
                    for c in range(DC):
                        mm3(nc.tensor, small[:, t, :], (hT_hi[:, c, cols], hT_lo[:, c, cols]),
                            (router_hi[:, c, :], router_lo[:, c, :]), start=c == 0, stop=c == DC - 1,
                            signal=logits_filled if c == DC - 1 and t == GT - 1 else None)

                def ranks():
                    pe.wait_ge(chosen_done, g + 1)
                    pe.wait_ge(count_done, g + 1)
                    for t in range(GT + 1):
                        for s in range(min(t + 1, GT)):
                            last = nc.tensor.matmul(rank_ps[:, t, :], before[:] if s == t else ones[:],
                                                    chosen[:, s, :], start=s == 0, stop=s == min(t, GT - 1))
                    last.then_inc(rank_filled, 1)

                for f in range(SF):
                    if f < 2:
                        pe.wait_ge(base_done, g * GT)
                    else:
                        pe.wait_ge(inner_done, g * SF + f - 1)
                    for w in range(2):
                        for c in range(DC):
                            cols = slice(f * P, (f + 1) * P)
                            mm3(nc.tensor, gate_up[:, f % 2, w, :], (w_hi[:, w, c, cols], w_lo[:, w, c, cols]),
                                (hT_hi[:, c, :], hT_lo[:, c, :]), start=c == 0, stop=c == DC - 1,
                                signal=gu_filled if c == DC - 1 and w == 1 else None)
                    if f == 1:
                        ranks()
                pe.wait_ge(inner_lo_done, g * SF + SF)
                for t in range(GT):
                    if t >= 2:
                        pe.wait_ge(base_done, g * GT + t - 1)
                    cols = slice(t * P, (t + 1) * P)
                    for f in range(SF):
                        mm3(nc.tensor, gate_up[:, t % 2, 0, :], (inner_hi[:, f, cols], inner_lo[:, f, cols]),
                            (w_hi[:, 2, f, :], w_lo[:, 2, f, :]), start=f == 0, stop=f == SF - 1,
                            signal=down_filled if f == SF - 1 else None)


def dispatch(nc, keep, table_dram):
    with ExitStack() as ctx:
        def sb(name, shape, dt=F32):
            return ctx.enter_context(nc.sbuf_tensor("di_" + name, shape, dt))

        def sem(name):
            return ctx.enter_context(nc.semaphore("di_" + name))

        I32 = mybir.dt.int32
        padded = sb("padded", [P, E], I32)
        tiles_i = sb("tiles_i", [P, E], I32)
        tiles = sb("tiles", [P, E])
        ones = sb("ones", [P, E])
        ends = sb("ends", [P, E])
        starts = sb("starts", [P, E])
        first = sb("first", [P, E])
        place = sb("place", [P, NT, E])
        placed = sb("placed", [P, NT * K, E])
        slot_f = sb("slot_f", [P, NT * K])
        tile_i = sb("tile_i", [P, SLOT_TILES], I32)
        tile_n = sb("tile_n", [P, SLOT_TILES])
        ended = sb("ended", [P, SLOT_TILES, E])
        owner = sb("owner", [P, SLOT_TILES])
        token_i = sb("token_i", [P, NT], I32)
        token = sb("token", [P, NT])
        zeros = sb("zeros", [P, SLOT_TILES])
        scratch = sb("scratch", [P, 5])
        token_now = sb("token_now", [P, 2, 1])
        slot_now = sb("slot_now", [P, 2, K], U32)
        made, step, zeroed, slots_ready = sem("made"), sem("step"), sem("zeroed"), sem("slots_ready")
        copied, scattered = sem("copied"), [sem("scattered0"), sem("scattered1")]
        block = ctx.enter_context(nc.Block())

        @block.sync
        def _(sp):
            sp.wait_ge(made, 4)
            sp.dma_start(table_dram.rearrange("(p n) o -> p (n o)", p=P), zeros[:]).then_inc(zeroed, 16)
            sp.wait_ge(zeroed, 16)

        @block.vector
        def _(dve):
            done = [0]

            def then(ins):
                done[0] += 1
                ins.then_inc(step, 1)
                dve.wait_ge(step, done[0])

            nc.vector.memset(ones[:], 1.0)
            then(nc.vector.tensor_scalar(padded[:], keep.count[:], float(P - 1), None, ALU.add))
            then(nc.vector.tensor_scalar(tiles_i[:], padded[:], P.bit_length() - 1, None,
                                         ALU.logical_shift_right))
            then(nc.vector.tensor_copy(tiles[:], tiles_i[:]))
            then(nc.vector.tensor_tensor_scan(ends[:], ones[:], tiles[:], 0.0, ALU.mult, ALU.add))
            then(nc.vector.tensor_tensor(starts[:], ends[:], tiles[:], ALU.subtract))
            then(nc.vector.tensor_scalar(first[:], starts[:], float(P), None, ALU.mult))
            then(nc.vector.tensor_tensor(place[:], keep.rank[:], first[:].unsqueeze(1).to_broadcast([P, NT, E]),
                                         ALU.add))
            for k in range(K):
                ins = nc.vector.tensor_tensor(
                    placed[:].rearrange("p (t k) e -> p t k e", k=K)[:, :, k, :],
                    keep.hot[:].rearrange("p (t k) e -> p t k e", k=K)[:, :, k, :], place[:], ALU.mult)
            then(ins)
            then(nc.vector.tensor_reduce(slot_f[:], placed[:], AXIS_X, ALU.add))
            nc.vector.tensor_copy(keep.slots[:], slot_f[:]).then_inc(slots_ready, 1)
            dve.wait_ge(made, 6)
            then(nc.vector.tensor_tensor(ended[:], tile_n[:].unsqueeze(2).to_broadcast([P, SLOT_TILES, E]),
                                         ends[:].unsqueeze(1).to_broadcast([P, SLOT_TILES, E]), ALU.is_ge))
            then(nc.vector.tensor_reduce(owner[:], ended[:], AXIS_X, ALU.add))
            then(nc.vector.tensor_scalar(keep.owner[:], owner[:], float(E - 1), None, ALU.min))

        @block.gpsimd
        def _(pool):
            nc.gpsimd.iota(tile_i[:], pattern=[[1, SLOT_TILES]], base=0, channel_multiplier=0).then_inc(made, 1)
            nc.gpsimd.iota(token_i[:], pattern=[[P, NT]], base=0, channel_multiplier=1).then_inc(made, 1)
            nc.gpsimd.memset(zeros[:], 0.0).then_inc(made, 1)
            nc.gpsimd.memset(scratch[:], 0.0).then_inc(made, 1)
            pool.wait_ge(made, 4)
            nc.gpsimd.tensor_copy(tile_n[:], tile_i[:]).then_inc(made, 1)
            nc.gpsimd.tensor_copy(token[:], token_i[:]).then_inc(made, 1)
            pool.wait_ge(made, 6)
            pool.wait_ge(slots_ready, 1)
            pool.wait_ge(zeroed, 16)
            with pool.Fori(0, NT // 2) as i:
                for s in range(2):
                    pool.wait_ge(scattered[s], 16 * K * i)
                    nc.gpsimd.tensor_copy(token_now[:, s, :], token[:, bass.ds(2 * i + s, 1)]).then_inc(copied, 1)
                    nc.gpsimd.tensor_copy(slot_now[:, s, :], keep.slots[:, bass.ds((2 * i + s) * K, K)]) \
                        .then_inc(copied, 1)
                    wait_apart(pool, scratch, 1 + s, copied, 4 * i + 2 * s + 2)
                    for k in range(K):
                        nc.gpsimd.indirect_dma_start(
                            table_dram, bass.IndirectOffsetOnAxis(ap=slot_now[:, s, k:k + 1], axis=0),
                            token_now[:, s, :], None).then_inc(scattered[s], 16)
            for s in range(2):
                pool.wait_ge(scattered[s], 16 * K * (NT // 2))


def experts(nc, keep, table_dram, h_dram, w1, w2, y_dram):
    with ExitStack() as ctx:
        def sb(name, shape, dt=F32):
            return ctx.enter_context(nc.sbuf_tensor("ex_" + name, shape, dt))

        def ps(name, shape):
            return ctx.enter_context(nc.psum_tensor("ex_" + name, shape, F32))

        def sem(name):
            return ctx.enter_context(nc.semaphore("ex_" + name))

        def sems(name):
            return [sem(name + "0"), sem(name + "1")]

        FC = I // P
        N = SLOT_TILES
        LEFT = N - P
        ident = sb("ident", [P, P])
        table = sb("table", [P, P])
        table_rest = sb("table_rest", [LEFT, P])
        token = sb("token", [P, N], U32)
        scratch = sb("scratch", [P, 5])
        token_now = sb("token_now", [P, 2, 1], U32)
        w1_sb = sb("w1_sb", [P, 2, DC, 2 * I])
        w2_sb = sb("w2_sb", [P, 2, FC, D])
        rows = sb("rows", [P, 2, D])
        rowsT = sb("rowsT", [P, 2, DC, P])
        silu = sb("silu", [P, 2, I])
        inner = sb("inner", [P, 2, I])
        innerT = sb("innerT", [P, 2, FC, P])
        y = sb("y", [P, 2, D])
        turn = ps("turn", [P, 2, DC, P])
        gate_up = ps("gate_up", [P, 2, 2 * I])
        inner_turn = ps("inner_turn", [P, 2, BANK])
        y_ps = ps("y_ps", [P, 2, D])

        made, table_loaded, table_turned, token_ready = (
            sem("made"), sem("table_loaded"), sem("table_turned"), sem("token_ready"))
        w_loaded, copied, gathered, turned, rowsT_done = (
            sems("w_loaded"), sems("copied"), sems("gathered"), sems("turned"), sems("rowsT_done"))
        gu_filled, silu_done, inner_done, inner_turned, innerT_done = (
            sems("gu_filled"), sems("silu_done"), sems("inner_done"), sems("inner_turned"), sems("innerT_done"))
        y_filled, y_done, y_stored = sems("y_filled"), sems("y_done"), sems("y_stored")
        block = ctx.enter_context(nc.Block())

        def halves(eng, first, second):
            first(0, 0, 0)
            with eng.Fori(0, N // 2 - 1) as i:
                first(2 * i + 1, i, 1)
                second(2 * i, i, 0)
                first(2 * i + 2, i + 1, 0)
                second(2 * i + 1, i, 1)
            first(N - 1, N // 2 - 1, 1)
            second(N - 2, N // 2 - 1, 0)
            second(N - 1, N // 2 - 1, 1)

        @block.sync
        def _(sp):
            tiles = table_dram.rearrange("(j s) o -> j (s o)", s=P)
            sp.dma_start(table[:], tiles[0:P, :]).then_inc(table_loaded, 16)
            sp.dma_start(table_rest[:], tiles[P:N, :]).then_inc(table_loaded, 16)
            with sp.Fori(0, N // 2) as m:
                for s in range(2):
                    e = sp.value_load(keep.owner[0:1, bass.ds(2 * m + s, 1)], min_val=0, max_val=E - 1)
                    sp.wait_ge(y_filled[s], m)
                    sp.dma_start(w1_sb[:, s], w1[bass.ds(e, 1)].rearrange("o p c n -> p (o c) n")) \
                      .then_inc(w_loaded[s], 16)
                    sp.dma_start(w2_sb[:, s], w2[bass.ds(e, 1)].rearrange("o p c n -> p (o c) n")) \
                      .then_inc(w_loaded[s], 16)

        @block.gpsimd
        def _(pool):
            nc.gpsimd.memset(ident[:], 0.0).then_inc(made, 1)
            nc.gpsimd.memset(scratch[:], 0.0).then_inc(made, 1)
            pool.wait_ge(made, 2)
            nc.gpsimd.affine_select(out=ident[:], in_=ident[:], compare_op=ALU.not_equal, fill=1.0, base=0,
                                    pattern=[[-1, P]], channel_multiplier=1).then_inc(made, 1)
            pool.wait_ge(token_ready, 2)
            with pool.Fori(0, N // 2) as m:
                for s in range(2):
                    wait_apart(pool, scratch, 1 + s, gathered[s], 16 * m)
                    nc.gpsimd.tensor_copy(token_now[:, s, :], token[:, bass.ds(2 * m + s, 1)]) \
                        .then_inc(copied[s], 1)
                    pool.wait_ge(turned[s], m)
                    wait_apart(pool, scratch, 3 + s, copied[s], m + 1)
                    nc.gpsimd.indirect_dma_start(
                        rows[:, s, :], None, h_dram,
                        bass.IndirectOffsetOnAxis(ap=token_now[:, s, :], axis=0)).then_inc(gathered[s], 16)

        @block.scalar
        def _(act):
            def first(n, m, s):
                act.wait_ge(gu_filled[s], m + 1)
                act.wait_ge(inner_done[s], m)
                nc.scalar.activation(silu[:, s, :], gate_up[:, s, 0:I], ACT.Silu).then_inc(silu_done[s], 1)

            def second(n, m, s):
                act.wait_ge(inner_turned[s], m + 1)
                act.wait_ge(y_filled[s], m)
                nc.scalar.activation(innerT[:, s].rearrange("p c n -> p (c n)"), inner_turn[:, s, 0:I],
                                     ACT.Copy).then_inc(innerT_done[s], 1)
                act.wait_ge(y_done[s], m + 1)
                act.dma_start(y_dram[bass.ds(n, 1)].rearrange("o p d -> (o p) d"), y[:, s, :]) \
                   .then_inc(y_stored[s], 16)

            halves(act, first, second)
            for s in range(2):
                act.wait_ge(y_stored[s], 16 * (N // 2))

        @block.vector
        def _(dve):
            dve.wait_ge(table_turned, 1)
            nc.vector.tensor_copy(token[:, 0:P], turn[:, 0, 0, :]).then_inc(token_ready, 1)
            nc.vector.tensor_copy(token[:, P:N], turn[:, 0, 1, 0:LEFT]).then_inc(token_ready, 1)

            def first(n, m, s):
                dve.wait_ge(turned[s], m + 1)
                dve.wait_ge(gu_filled[s], m)
                nc.vector.tensor_copy(rowsT[:, s], turn[:, s]).then_inc(rowsT_done[s], 1)
                dve.wait_ge(silu_done[s], m + 1)
                dve.wait_ge(inner_turned[s], m)
                nc.vector.tensor_tensor(inner[:, s, :], gate_up[:, s, I:2 * I], silu[:, s, :], ALU.mult) \
                    .then_inc(inner_done[s], 1)

            def second(n, m, s):
                dve.wait_ge(y_filled[s], m + 1)
                dve.wait_ge(y_stored[s], 16 * m)
                nc.vector.tensor_copy(y[:, s, :], y_ps[:, s, :]).then_inc(y_done[s], 1)

            halves(dve, first, second)

        @block.tensor
        def _(pe):
            pe.wait_ge(made, 3)
            pe.wait_ge(table_loaded, 32)
            nc.tensor.transpose(turn[:, 0, 0, :], table[:], ident[:])
            nc.tensor.transpose(turn[:, 0, 1, 0:LEFT], table_rest[:], ident[0:LEFT, 0:LEFT]) \
                .then_inc(table_turned, 1)
            pe.wait_ge(token_ready, 2)

            def first(n, m, s):
                pe.wait_ge(gathered[s], 16 * m + 16)
                pe.wait_ge(rowsT_done[s], m)
                for c in range(DC):
                    last = nc.tensor.transpose(turn[:, s, c, :], rows[:, s, c * P:(c + 1) * P], ident[:])
                last.then_inc(turned[s], 1)
                pe.wait_ge(w_loaded[s], 32 * m + 32)
                pe.wait_ge(rowsT_done[s], m + 1)
                pe.wait_ge(inner_done[s], m)
                for c in range(DC):
                    last = nc.tensor.matmul(gate_up[:, s, :], rowsT[:, s, c, :], w1_sb[:, s, c, :], start=c == 0,
                                            stop=c == DC - 1)
                last.then_inc(gu_filled[s], 1)

            def second(n, m, s):
                pe.wait_ge(inner_done[s], m + 1)
                pe.wait_ge(innerT_done[s], m)
                for c in range(FC):
                    last = nc.tensor.transpose(inner_turn[:, s, c * P:(c + 1) * P],
                                               inner[:, s, c * P:(c + 1) * P], ident[:])
                last.then_inc(inner_turned[s], 1)
                pe.wait_ge(innerT_done[s], m + 1)
                pe.wait_ge(y_done[s], m)
                for c in range(FC):
                    last = nc.tensor.matmul(y_ps[:, s, :], innerT[:, s, c, :], w2_sb[:, s, c, :], start=c == 0,
                                            stop=c == FC - 1)
                last.then_inc(y_filled[s], 1)

            halves(pe, first, second)


def combine(nc, keep, y_dram, base_dram, out):
    with ExitStack() as ctx:
        def sb(name, shape, dt=F32):
            return ctx.enter_context(nc.sbuf_tensor("co_" + name, shape, dt))

        def sems(name):
            return [ctx.enter_context(nc.semaphore(f"co_{name}{s}")) for s in range(2)]

        started = ctx.enter_context(nc.semaphore("co_started"))
        scratch = sb("scratch", [P, 5])
        slot_now = sb("slot_now", [P, 2, K], U32)
        rows = sb("rows", [P, 2, K, D])
        total = sb("total", [P, 2, D])
        base_loaded, copied, gathered, added, stored = (
            sems("base_loaded"), sems("copied"), sems("gathered"), sems("added"), sems("stored"))
        block = ctx.enter_context(nc.Block())

        @block.sync
        def _(sp):
            with sp.Fori(0, NT // 2) as m:
                for s in range(2):
                    sp.wait_ge(stored[s], 16 * m)
                    sp.dma_start(total[:, s, :], base_dram[bass.ds(2 * m + s, 1)].rearrange("o p d -> (o p) d")) \
                      .then_inc(base_loaded[s], 16)

        @block.gpsimd
        def _(pool):
            nc.gpsimd.memset(scratch[:], 0.0).then_inc(started, 1)
            pool.wait_ge(started, 1)
            with pool.Fori(0, NT // 2) as m:
                for s in range(2):
                    wait_apart(pool, scratch, 1 + s, gathered[s], 16 * K * m)
                    nc.gpsimd.tensor_copy(slot_now[:, s, :], keep.slots[:, bass.ds((2 * m + s) * K, K)]) \
                        .then_inc(copied[s], 1)
                    pool.wait_ge(added[s], K * m)
                    wait_apart(pool, scratch, 3 + s, copied[s], m + 1)
                    for k in range(K):
                        nc.gpsimd.indirect_dma_start(
                            rows[:, s, k, :], None, y_dram,
                            bass.IndirectOffsetOnAxis(ap=slot_now[:, s, k:k + 1], axis=0)).then_inc(gathered[s], 16)

        @block.vector
        def _(dve):
            with dve.Fori(0, NT // 2) as m:
                for s in range(2):
                    dve.wait_ge(base_loaded[s], 16 * m + 16)
                    dve.wait_ge(gathered[s], 16 * K * m + 16 * K)
                    for k in range(K):
                        w = keep.top_w[:, bass.ds((2 * m + s) * K + k, 1)]
                        nc.vector.scalar_tensor_tensor(out=total[:, s, :], in0=rows[:, s, k, :], scalar=w,
                                                       in1=total[:, s, :], op0=ALU.mult, op1=ALU.add) \
                            .then_inc(added[s], 1)
                        dve.wait_ge(added[s], K * m + k + 1)

        @block.scalar
        def _(act):
            with act.Fori(0, NT // 2) as m:
                for s in range(2):
                    act.wait_ge(added[s], K * m + K)
                    act.dma_start(out[bass.ds(2 * m + s, 1)].rearrange("o p d -> (o p) d"), total[:, s, :]) \
                       .then_inc(stored[s], 16)
            for s in range(2):
                act.wait_ge(stored[s], 16 * (NT // 2))


class Routing:

    def __init__(self, sb):
        self.count = sb("count", [P, E])
        self.rank = sb("rank", [P, NT, E])
        self.hot = sb("hot", [P, NT * K, E], BF16)
        self.top_w = sb("top_w", [P, NT * K])
        self.slots = sb("slots", [P, NT * K], U32)
        self.owner = sb("owner", [P, SLOT_TILES], mybir.dt.int32)


def feed_forward(nc, x2_dram, norm_rows, router_w, shared_w, w1, w2, out, dram):
    h_dram, base_dram, table_dram, y_dram = (
        dram("h", [T, D]), dram("base", [T, D]), dram("table", [SLOTS, 1]), dram("y", [SLOTS, D]))
    with ExitStack() as ctx:
        def sb(name, shape, dt=F32):
            return ctx.enter_context(nc.sbuf_tensor("keep_" + name, shape, dt))

        keep = Routing(sb)
        grouped = lambda a: a.rearrange("(g n) d -> g n d", n=BANK)
        tiled = lambda a: a.rearrange("(n p) d -> n p d", p=P)
        ffn_tokens(nc, keep, grouped(x2_dram), norm_rows, router_w, shared_w, grouped(h_dram), grouped(base_dram))
        dispatch(nc, keep, table_dram)
        experts(nc, keep, table_dram, h_dram, w1, w2, tiled(y_dram))
        combine(nc, keep, y_dram, tiled(base_dram), tiled(out))


def build_program(nc, x, attn_w, w_kv_down, q_norm_rows, k_norm_col, cos, sin, norm_rows, router_w, shared_w,
                  w1, w2, out):
    def dram(name, shape):
        return nc.dram_tensor("scratch_" + name, tuple(shape), F32, kind="Internal").ap()

    w_hi_dram, w_lo_dram = dram("w_hi", [PAIRS, P, WQK + WO]), dram("w_lo", [PAIRS, P, WQK + WO])
    x2_dram = dram("x2", [T, D])
    prepare_weights(nc, attn_w, w_hi_dram, w_lo_dram)
    attention(nc, x, w_kv_down, q_norm_rows, k_norm_col, cos, sin, w_hi_dram, w_lo_dram,
              x2_dram.rearrange("(b s) d -> b s d", b=B))
    feed_forward(nc, x2_dram, norm_rows, router_w, shared_w, w1, w2,
                 out.rearrange("b s d -> (b s) d"), dram)


def kernel(**inputs):
    import concourse.bacc as bacc
    from concourse.bass_utils import run_bass_kernel_spmd

    a = {name.removeprefix("L0_"): np.asarray(value) for name, value in inputs.items()}
    dense = np.ascontiguousarray
    wq = a["attn_wq"].reshape(DC, P, PAIRS, 2 * DK).transpose(2, 1, 0, 3).reshape(PAIRS, P, DC * 2 * DK)
    wk = np.concatenate([a["attn_w_k_rope"].reshape(DL, H, DR), a["attn_w_k_nope"].reshape(DL, H, DK - DR)], 2)
    wk = wk.reshape(DL, PAIRS, 2 * DK).transpose(1, 0, 2)
    wv = a["attn_wv"].reshape(DL, H, DK).transpose(2, 1, 0).reshape(DK, PAIRS, 2 * DL).transpose(1, 0, 2)
    wo = a["attn_wo"].reshape(PAIRS, 2, DK, D).transpose(0, 2, 1, 3).reshape(PAIRS, DK, 2 * D)
    freq = np.float32(1.0 / 10000.0) ** np.linspace(0.0, 1.0, RQ, dtype=np.float32)
    theta = np.arange(S, dtype=np.float32)[:, None] * freq[None, :]
    shared = np.stack([a["ffn_sg"], a["ffn_su"], a["ffn_sd"]])
    arrays = {
        "x": dense(a["attn_x"]),
        "attn_w": dense(np.concatenate([wq, wk, wv, wo], 2)),
        "w_kv_down": dense(a["attn_w_kv_down"].reshape(DC, P, DL).transpose(1, 0, 2)),
        "q_norm_rows": dense(np.broadcast_to(a["attn_q_norm_w"], (P, DK))),
        "k_norm_col": dense(a["attn_k_norm_w"].reshape(DK, 1)),
        "cos": dense(np.cos(theta).reshape(TB, P, RQ).transpose(1, 0, 2)),
        "sin": dense(np.sin(theta).reshape(TB, P, RQ).transpose(1, 0, 2)),
        "norm_rows": dense(np.broadcast_to(a["ffn_norm_w"], (P, D))),
        "router_w": dense(a["ffn_router_w"].T.reshape(DC, P, E).transpose(1, 0, 2)),
        "shared_w": dense(shared.reshape(3, DC, P, SH).transpose(2, 0, 1, 3).reshape(P, 3 * DC * SH)),
        "w1": dense(a["ffn_w1"].reshape(E, DC, P, 2 * I).transpose(0, 2, 1, 3)),
        "w2": dense(a["ffn_w2"].reshape(E, I // P, P, D).transpose(0, 2, 1, 3)),
    }
    nc = bacc.Bacc("TRN2", target_bir_lowering=False, num_devices=1)
    args = {name: nc.dram_tensor("in_" + name, value.shape, mybir.dt.from_np(value.dtype),
                                 kind="ExternalInput").ap() for name, value in arrays.items()}
    out = nc.dram_tensor("out_0", (B, S, D), F32, kind="ExternalOutput").ap()
    build_program(nc, out=out, **args)
    result = run_bass_kernel_spmd(nc, [{"in_" + name: value for name, value in arrays.items()}], core_ids=[0])
    return result.results[0]["out_0"]
```

```python
from contextlib import ExitStack

import concourse.bass as bass
from concourse import mybir
import numpy as np

ALU = mybir.AluOpType
ACT = mybir.ActivationFunctionType
AXIS_X = mybir.AxisListType.X
F32 = mybir.dt.float32
F32R = mybir.dt.float32r
BF16 = mybir.dt.bfloat16
U32 = mybir.dt.uint32

P = 128
B, S, D = 4, 1024, 512
H, DK, DL, DR = 16, 128, 128, 64
T = B * S
E, I, K = 32, 256, 4
SH = 512
BANK = 512
DC = D // P
TB = S // P
NT = T // P
PAIRS = H // 2
GT = BANK // P
RQ = DR // 4
LN_EPS, ATT_EPS, FFN_EPS = 1e-5, 1e-6, 1e-6
MASKED = -1e30
SLOT_TILES = T * K // P + E
SLOTS = SLOT_TILES * P
WQK = DC * 2 * DK + 2 * DK
WV = 2 * DL
WO = 2 * D


def mm3(pe, out, lhs, rhs, start=True, stop=True, signal=None):
    (a, a_rest), (b, b_rest) = lhs, rhs
    pe.matmul(out, a, b, start=start, stop=False)
    pe.matmul(out, a, b_rest, start=False, stop=False)
    last = pe.matmul(out, a_rest, b, start=False, stop=stop)
    if signal is not None:
        last.then_inc(signal, 1)


def wait_apart(eng, scratch, column, sem, value):
    eng.wait_ge(sem, value)
    eng.tensor_tensor(scratch[:, column:column + 1], scratch[:, 0:1], scratch[:, 0:1], ALU.add)


def prepare_weights(nc, attn_w, w_hi_dram, w_lo_dram):
    WIDE = WQK + WV + WO
    with ExitStack() as ctx:
        def sb(name, shape, dt):
            return ctx.enter_context(nc.sbuf_tensor(name, shape, dt))

        def sem(name):
            return ctx.enter_context(nc.semaphore(name))

        raw = sb("pw_raw", [P, 2, WIDE], F32)
        hi = sb("pw_hi", [P, 2, WIDE], F32R)
        lo = sb("pw_lo", [P, 2, WIDE], F32R)
        vo_hi = sb("pw_vo_hi", [P, 2, 2, D], F32R)
        vo_lo = sb("pw_vo_lo", [P, 2, 2, D], F32R)
        vo_ps = ctx.enter_context(nc.psum_tensor("pw_vo_ps", [P, 2, 2, BANK], F32))
        loaded = [sem("pw_loaded0"), sem("pw_loaded1")]
        hi_done, lo_done = sem("pw_hi_done"), sem("pw_lo_done")
        vo_filled, vo_hi_done, vo_lo_done = sem("pw_vo_filled"), sem("pw_vo_hi_done"), sem("pw_vo_lo_done")
        stored = [sem("pw_stored0"), sem("pw_stored1")]
        STORES = 4 * 16

        def wv_of(x, s, h):
            return x[:, s, WQK + h * DL:WQK + (h + 1) * DL]

        def wo_of(x, s, h):
            return x[:, s, WQK + WV + h * D:WQK + WV + (h + 1) * D]

        block = ctx.enter_context(nc.Block())

        @block.sync
        def _(sp):
            with sp.Fori(0, PAIRS // 2) as g:
                for s in range(2):
                    sp.wait_ge(lo_done, 2 * g)
                    sp.dma_start(raw[:, s, :], attn_w[bass.ds(2 * g + s, 1)].rearrange("o p n -> (o p) n")) \
                      .then_inc(loaded[s], 16)

        @block.scalar
        def _(act):
            with act.Fori(0, PAIRS // 2) as g:
                for s in range(2):
                    act.wait_ge(loaded[s], 16 * g + 16)
                    act.wait_ge(stored[s], STORES * g)
                    nc.scalar.activation(hi[:, s, :], raw[:, s, :], ACT.Copy).then_inc(hi_done, 1)
                    act.wait_ge(vo_filled, 2 * g + s + 1)
                    nc.scalar.activation(vo_hi[:, s], vo_ps[:, s], ACT.Copy).then_inc(vo_hi_done, 1)

        @block.vector
        def _(dve):
            with dve.Fori(0, PAIRS // 2) as g:
                for s in range(2):
                    dve.wait_ge(hi_done, 2 * g + s + 1)
                    nc.vector.tensor_tensor(lo[:, s, :], raw[:, s, :], hi[:, s, :], ALU.subtract) \
                      .then_inc(lo_done, 1)
                    dve.wait_ge(vo_hi_done, 2 * g + s + 1)
                    nc.vector.tensor_tensor(vo_lo[:, s], vo_ps[:, s], vo_hi[:, s], ALU.subtract) \
                      .then_inc(vo_lo_done, 1)

        @block.tensor
        def _(pe):
            with pe.Fori(0, PAIRS // 2) as g:
                for s in range(2):
                    pe.wait_ge(lo_done, 2 * g + s + 1)
                    pe.wait_ge(vo_lo_done, 2 * g)
                    for h in range(2):
                        mm3(nc.tensor, vo_ps[:, s, h, :], (wv_of(hi, s, h), wv_of(lo, s, h)),
                            (wo_of(hi, s, h), wo_of(lo, s, h)), signal=vo_filled if h == 1 else None)

        @block.gpsimd
        def _(pool):
            with pool.Fori(0, PAIRS // 2) as g:
                for s in range(2):
                    pool.wait_ge(lo_done, 2 * g + s + 1)
                    for src, dst in ((hi, w_hi_dram), (lo, w_lo_dram)):
                        pool.dma_start(dst[bass.ds(2 * g + s, 1), :, 0:WQK].rearrange("o p n -> (o p) n"),
                                       src[:, s, 0:WQK].bitcast(F32)).then_inc(stored[s], 16)
                    pool.wait_ge(vo_lo_done, 2 * g + s + 1)
                    for src, dst in ((vo_hi, w_hi_dram), (vo_lo, w_lo_dram)):
                        pool.dma_start(dst[bass.ds(2 * g + s, 1), :, WQK:WQK + WO].rearrange("o p n -> (o p) n"),
                                       src[:, s].rearrange("p h n -> p (h n)").bitcast(F32)) \
                            .then_inc(stored[s], 16)
            for s in range(2):
                pool.wait_ge(stored[s], STORES * (PAIRS // 2))


def attention(nc, x, w_kv_down, q_norm_rows, k_norm_col, cos, sin, w_hi_dram, w_lo_dram, x2_dram):
    STEPS = 2 * TB
    GQ = 2
    GROUPS = STEPS // GQ
    LAST_STEP = STEPS + 6
    LAST_HEAD = TB + 2

    def step_of(u):
        group = u // GQ
        return group // 2, group % 2, GQ * (group // 2) + u % GQ

    pv_steps = [GQ * n + GQ + 2 for n in range(GROUPS)]

    SPLIT_LAG = 1

    def out_tiles_at(u):
        n = u - pv_steps[1] - 3
        return [GQ * (n // 4) + n % 4] if 0 <= n and n % 4 < GQ else []

    def chunks(t):
        return [range(a, min(a + GT, t + 1)) for a in range(0, t + 1, GT)]

    AHEAD = 7

    def plan(first_head, with_next):
        steps = [("head", i, 0) for i in range(first_head, TB)]
        for u in range(LAST_STEP + 1):
            if TB + u <= LAST_HEAD:
                steps.append(("head", TB + u, 0))
            steps.append(("softmax", u, 0))
            if with_next and u >= STEPS:
                steps.append(("head", u - STEPS, 1))
        return steps

    ring = [("qk", i) for i in range(TB)]
    turns = {("qkT", i): i for i in range(TB)}
    for u in range(STEPS + 2):
        if u < STEPS:
            ring.append(("scores", u))
        if 2 <= u < STEPS + 2:
            for c in range(len(chunks(step_of(u - 2)[2]))):
                turns["probsT", u - 2, c] = len(turns)
    RING, TURNS = len(ring), len(turns)
    LN_RING, LN_TURNS = 2 + 2, TB
    assert RING % 2 == 0 and TURNS % 2 == 0

    with ExitStack() as ctx:
        def sb(name, shape, dt):
            return ctx.enter_context(nc.sbuf_tensor(name, shape, dt))

        def ps(name, shape):
            return ctx.enter_context(nc.psum_tensor(name, shape, F32))

        def sem(name):
            return ctx.enter_context(nc.semaphore(name))

        ident = sb("at_ident", [P, P], F32)
        ident_b = sb("at_ident_b", [P, P], BF16)
        mask_b = sb("at_mask_b", [P, P], BF16)
        minus_half = sb("at_minus_half", [P, TB], F32)
        scratch = sb("at_scratch", [P, 2], F32)
        ln_eps = sb("at_ln_eps", [P, TB], F32)
        att_eps = sb("at_att_eps", [P, 4], F32)
        cos_t = sb("at_cos", [P, TB, RQ], F32)
        sin_t = sb("at_sin", [P, TB, RQ], F32)
        q_norm = sb("at_q_norm", [P, DK], F32)
        k_norm = sb("at_k_norm", [P, 1], F32)
        k_scale = sb("at_k_scale", [P, 1], F32)
        down_raw = sb("at_down_raw", [P, DC, DL], F32)
        down_hi = sb("at_down_hi", [P, DC, DL], F32R)
        down_lo = sb("at_down_lo", [P, DC, DL], F32R)

        acc = sb("at_acc", [P, TB, D], F32)
        stats = sb("at_stats", [P, TB, 6], F32)
        mean_var = sb("at_mean_var", [P, TB, 2], F32)
        ln_var = sb("at_ln_var", [P, TB], F32)
        ln_rstd = sb("at_ln_rstd", [P, TB], F32)
        xn = sb("at_xn", [P, 2, D], F32)
        xT_hi = sb("at_xT_hi", [P, DC, S], F32R)
        xT_lo = sb("at_xT_lo", [P, DC, S], F32R)
        latT_hi = sb("at_latT_hi", [P, S], F32R)
        latT_lo = sb("at_latT_lo", [P, S], F32R)
        lat_hi = sb("at_lat_hi", [P, TB, DL], F32R)
        lat_lo = sb("at_lat_lo", [P, TB, DL], F32R)

        wqk_hi = sb("at_wqk_hi", [P, WQK], F32R)
        wqk_lo = sb("at_wqk_lo", [P, WQK], F32R)
        wvo_hi = sb("at_wvo_hi", [P, 2, D], F32R)
        wvo_lo = sb("at_wvo_lo", [P, 2, D], F32R)

        squares = sb("at_squares", [P, 4, DK], F32)
        sums = sb("at_sums", [P, TB, 4], F32)
        sums_eps = sb("at_sums_eps", [P, TB, 4], F32)
        rstd = sb("at_rstd", [P, TB, 4], F32)
        qk = sb("at_qk", [P, 4, 4, DK], F32)
        turned = sb("at_turned", [P, 2, 4, 2, RQ], F32)
        qkT_hi = sb("at_qkT_hi", [P, 4, S], F32R)
        qkT_lo = sb("at_qkT_lo", [P, 4, S], F32R)

        row_max = sb("at_row_max", [P, 2], F32)
        shift = sb("at_shift", [P, 2], F32)
        row_sum = sb("at_row_sum", [P, 2], F32)
        row_inv = sb("at_row_inv", [P, 2], F32)
        probs = sb("at_probs", [P, 3, S], F32)
        pT_hi = sb("at_pT_hi", [P, 2, TB, GQ * P], F32R)
        pT_lo = sb("at_pT_lo", [P, 2, TB, GQ * P], F32R)
        oT_hi = sb("at_oT_hi", [P, 4, GQ * P], F32R)
        oT_lo = sb("at_oT_lo", [P, 4, GQ * P], F32R)

        slot = ps("at_slot", [P, 2, 2 * BANK])
        turn = ps("at_turn", [P, 2, 4, P])
        pv = ps("at_pv", [P, GQ * P])
        out_ps = ps("at_out_ps", [P, BANK])

        consts_loaded, consts_made = sem("at_consts_loaded"), sem("at_consts_made")
        down_hi_done, down_lo_done, k_scaled = sem("at_down_hi"), sem("at_down_lo"), sem("at_k_scaled")
        x_loaded, x2_stored = sem("at_x_loaded"), sem("at_x2_stored")
        ln_stats, ln_aggr, ln_var_added, ln_rstd_ready, xn_ready = (
            sem("at_ln_stats"), sem("at_ln_aggr"), sem("at_ln_var_added"), sem("at_ln_rstd"), sem("at_xn_ready"))
        wqk_loaded, wvo_loaded = sem("at_wqk_loaded"), sem("at_wvo_loaded")
        slot_filled = sem("at_slot_filled")
        turn_filled = sem("at_turn_filled")
        out_filled = sem("at_out_filled")
        turn_hi, turn_lo = sem("at_turn_hi"), sem("at_turn_lo")
        lat_hi_done, lat_lo_done, lat_copied = (
            sem("at_lat_hi_done"), sem("at_lat_lo_done"), sem("at_lat_copied"))
        summed, eps_added, rstd_ready = sem("at_summed"), sem("at_eps_added"), sem("at_rstd_ready")
        q_scaled, kr_scaled, rope_parts, rope_done = (
            sem("at_q_scaled"), sem("at_kr_scaled"), sem("at_rope_parts"), sem("at_rope_done"))
        max_ready, shift_ready, exp_done, inv_ready, probs_ready = (
            sem("at_max"), sem("at_shift_ready"), sem("at_exp"), sem("at_inv"), sem("at_probs_ready"))
        pv_filled, oT_hi_done, oT_lo_done = sem("at_pv_filled"), sem("at_oT_hi_done"), sem("at_oT_lo_done")
        out_added = sem("at_out_added")

        def batch_ring(b):
            return b * (LN_RING + PAIRS * RING)

        def round_ring(b, p):
            return batch_ring(b) + LN_RING + p * RING

        def batch_turns(b):
            return b * (LN_TURNS + PAIRS * TURNS)

        def round_turns(b, p):
            return batch_turns(b) + LN_TURNS + p * TURNS

        def rounds(eng, b, step):
            def one_pass(p, first_head, with_next):
                for kind, n, ahead in plan(first_head, with_next):
                    step(kind, n, b * PAIRS + p + ahead, round_ring(b, p + ahead), round_turns(b, p + ahead))

            for i in range(AHEAD):
                step("head", i, b * PAIRS, round_ring(b, 0), round_turns(b, 0))
            with eng.Fori(0, PAIRS - 1) as p:
                one_pass(p, AHEAD, True)
            one_pass(PAIRS - 1, AHEAD, False)

        def use(kind, n):
            return ring.index((kind, n))

        def banks(kind, n):
            at = use(kind, n)
            if at < 2 * TB:
                return slot[:, at // 2 % 2, at % 2 * BANK:(at % 2 + 1) * BANK]
            return slot[:, n % 2, :]

        def wqk(x, c):
            return x[:, c * 2 * DK:(c + 1) * 2 * DK]

        block = ctx.enter_context(nc.Block())

        @block.sync
        def _(sp):
            sp.dma_start(cos_t[:], cos).then_inc(consts_loaded, 16)
            sp.dma_start(sin_t[:], sin).then_inc(consts_loaded, 16)
            sp.dma_start(q_norm[:], q_norm_rows).then_inc(consts_loaded, 16)
            sp.dma_start(k_norm[:], k_norm_col).then_inc(consts_loaded, 16)
            sp.dma_start(down_raw[:], w_kv_down).then_inc(consts_loaded, 16)
            with sp.Fori(0, B) as b:
                sp.wait_ge(x2_stored, 16 * b)
                sp.dma_start(acc[:], x[bass.ds(b, 1)].rearrange("o (t p) d -> p (o t) d", p=P)) \
                  .then_inc(x_loaded, 16)
                with sp.Fori(0, PAIRS) as p:
                    r = b * PAIRS + p
                    sp.wait_ge(kr_scaled, r * TB)
                    for dst, src in ((wqk_hi, w_hi_dram), (wqk_lo, w_lo_dram)):
                        sp.dma_start(dst[:].bitcast(F32), src[bass.ds(p, 1), :, 0:WQK]
                                     .rearrange("o p n -> (o p) n")).then_inc(wqk_loaded, 16)
                    sp.wait_ge(out_added, r * TB)
                    for dst, src in ((wvo_hi, w_hi_dram), (wvo_lo, w_lo_dram)):
                        sp.dma_start(dst[:].rearrange("p h n -> p (h n)").bitcast(F32),
                                     src[bass.ds(p, 1), :, WQK:WQK + WO]
                                     .rearrange("o p n -> (o p) n")).then_inc(wvo_loaded, 16)
                sp.wait_ge(out_added, (b + 1) * (PAIRS * TB))
                sp.dma_start(x2_dram[bass.ds(b, 1)].rearrange("o (t p) d -> p (o t) d", p=P), acc[:]) \
                  .then_inc(x2_stored, 16)
            sp.wait_ge(x2_stored, 16 * B)

        @block.gpsimd
        def _(pool):
            nc.gpsimd.memset(ident[:], 0.0).then_inc(consts_made, 1)
            nc.gpsimd.memset(ident_b[:], 0.0).then_inc(consts_made, 1)
            nc.gpsimd.memset(mask_b[:], 0.0).then_inc(consts_made, 1)
            nc.gpsimd.memset(minus_half[:], -0.5).then_inc(consts_made, 1)
            nc.gpsimd.memset(ln_eps[:], LN_EPS).then_inc(consts_made, 1)
            nc.gpsimd.memset(att_eps[:], ATT_EPS * DK).then_inc(consts_made, 1)
            pool.wait_ge(consts_made, 6)
            for m in (ident, ident_b):
                nc.gpsimd.affine_select(out=m[:], in_=m[:], compare_op=ALU.not_equal, fill=1.0, base=0,
                                        pattern=[[-1, P]], channel_multiplier=1).then_inc(consts_made, 1)
            nc.gpsimd.affine_select(out=mask_b[:], in_=mask_b[:], compare_op=ALU.is_ge, fill=MASKED, base=0,
                                    pattern=[[-1, P]], channel_multiplier=1).then_inc(consts_made, 1)
            pool.wait_ge(consts_loaded, 16 * 5)
            with pool.Fori(0, B) as b:
                pool.wait_ge(ln_aggr, b * TB + TB)
                nc.gpsimd.tensor_tensor(ln_var[:], mean_var[:, :, 1:2].rearrange("p t o -> p (t o)"),
                                        ln_eps[:], ALU.add).then_inc(ln_var_added, 1)
                pool.wait_ge(ln_var_added, b + 1)
                nc.gpsimd.tensor_tensor(ln_rstd[:], ln_var[:], minus_half[:], ALU.pow) \
                  .then_inc(ln_rstd_ready, 1)

                def step(kind, i, r, ring0, turns0):
                    if kind == "head" and i < TB:
                        pool.wait_ge(summed, r * TB + i + 1)
                        nc.gpsimd.tensor_tensor(sums_eps[:, i, :], sums[:, i, :], att_eps[:], ALU.add) \
                            .then_inc(eps_added, 1)
                        if i == 0:
                            pool.wait_ge(exp_done, r * STEPS)
                        pool.wait_ge(eps_added, r * TB + i + 1)
                        nc.gpsimd.tensor_tensor(rstd[:, i, :], sums_eps[:, i, :], minus_half[:, 0:4],
                                                ALU.pow).then_inc(rstd_ready, 1)

                rounds(pool, b, step)

        @block.scalar
        def _(act):
            def high(dst, src, signal, **more):
                nc.scalar.activation(dst, src, ACT.Copy, **more).then_inc(signal, 1)

            act.wait_ge(consts_loaded, 16 * 5)
            high(down_hi[:], down_raw[:], down_hi_done)
            act.wait_ge(k_scaled, 2)
            with act.Fori(0, B) as b:
                for t in range(TB):
                    act.wait_ge(turn_filled, batch_turns(b) + t + 1)
                    high(xT_hi[:, :, t * P:(t + 1) * P], turn[:, t % 2], turn_hi)
                for n in range(2):
                    act.wait_ge(slot_filled, batch_ring(b) + n + 1)
                    high(latT_hi[:, n * BANK:(n + 1) * BANK], slot[:, n, 0:BANK], lat_hi_done)
                for n in range(2):
                    act.wait_ge(slot_filled, batch_ring(b) + 2 + n + 1)
                    high(lat_hi[:, n * GT:(n + 1) * GT, :].rearrange("p t d -> p (t d)"), slot[:, n, 0:BANK],
                         lat_hi_done)

                def step(kind, u, r, ring0, turns0):
                    if kind == "head":
                        if u < TB:
                            act.wait_ge(slot_filled, ring0 + use("qk", u) + 1)
                            if u == 0:
                                act.wait_ge(eps_added, r * TB)
                            act.wait_ge(summed, r * TB + u)
                            for k in range(4):
                                last = nc.scalar.activation(squares[:, k, :],
                                                            banks("qk", u)[:, k * DK:(k + 1) * DK],
                                                            ACT.Square, accum_out=sums[:, u, k:k + 1])
                            last.then_inc(summed, 1)
                        if u >= 3:
                            n = u - 3
                            w = turns["qkT", n]
                            act.wait_ge(turn_filled, turns0 + w + 1)
                            nc.scalar.activation(qkT_hi[:, 0:2, n * P:(n + 1) * P], turn[:, w % 2, 0:2, :],
                                                 ACT.Copy)
                            high(qkT_hi[:, 2:4, n * P:(n + 1) * P], turn[:, w % 2, 2:4, :], turn_hi,
                                 scale=k_scale[:, 0:1])
                        return

                    def exponentials():
                        if u >= STEPS:
                            return
                        _, h, t = step_of(u)
                        width = (t + 1) * P
                        act.wait_ge(shift_ready, r * STEPS + u + 1)
                        if u >= 3:
                            before = turns["probsT", u - 3, len(chunks(step_of(u - 3)[2])) - 1]
                            act.wait_ge(turn_filled, turns0 + before + 1)
                        nc.scalar.activation(probs[:, u % 3, 0:width], banks("scores", u)[:, 0:width],
                                             ACT.Exp, bias=shift[:, u % 2:u % 2 + 1], scale=rstd[:, t, h:h + 1],
                                             accum_out=row_sum[:, u % 2:u % 2 + 1]).then_inc(exp_done, 1)

                    def value_highs():
                        if u - SPLIT_LAG in pv_steps:
                            n = pv_steps.index(u - SPLIT_LAG)
                            act.wait_ge(pv_filled, r * GROUPS + n + 1)
                            high(oT_hi[:, n % 4, :], pv[:], oT_hi_done)

                    def probs_highs():
                        if 2 <= u < STEPS + 2:
                            _, h, t = step_of(u - 2)
                            j = (u - 2) % GQ
                            for c, blocks in enumerate(chunks(t)):
                                w = turns["probsT", u - 2, c]
                                act.wait_ge(turn_filled, turns0 + w + 1)
                                high(pT_hi[:, h, blocks[0]:blocks[-1] + 1, j * P:(j + 1) * P],
                                     turn[:, w % 2, 0:len(blocks), :], turn_hi)

                    probs_highs()
                    exponentials()
                    value_highs()

                rounds(act, b, step)

        @block.vector
        def _(dve):
            def low(dst, src, high, signal):
                nc.vector.tensor_tensor(dst, src, high, ALU.subtract).then_inc(signal, 1)

            dve.wait_ge(consts_loaded, 16 * 5)
            nc.vector.memset(scratch[:], 0.0).then_inc(k_scaled, 1)
            nc.vector.tensor_scalar(k_scale[:], k_norm[:], float(np.sqrt(DK)), None, ALU.mult).then_inc(k_scaled, 1)
            dve.wait_ge(k_scaled, 2)
            for x in (pT_hi, pT_lo):
                nc.vector.tensor_copy(x[:, :, TB - 1, 0:P], scratch[:, 0:1].unsqueeze(1).to_broadcast([P, 2, P]))
            dve.wait_ge(down_hi_done, 1)
            low(down_lo[:], down_raw[:], down_hi[:], down_lo_done)
            with dve.Fori(0, B) as b:
                dve.wait_ge(x_loaded, 16 * b + 16)
                for t in range(TB):
                    nc.vector.bn_stats(stats[:, t, :], acc[:, t, :]).then_inc(ln_stats, 1)
                wait_apart(dve, scratch, 1, ln_stats, b * TB + TB)
                for t in range(TB):
                    nc.vector.bn_aggr(mean_var[:, t, :], stats[:, t, :]).then_inc(ln_aggr, 1)
                dve.wait_ge(ln_rstd_ready, b + 1)
                for t in range(TB + 1):
                    if t < TB:
                        if t >= 2:
                            dve.wait_ge(turn_filled, batch_turns(b) + t - 1)
                        nc.vector.tensor_scalar(xn[:, t % 2, :], acc[:, t, :], mean_var[:, t, 0:1],
                                                ln_rstd[:, t:t + 1], ALU.subtract, ALU.mult).then_inc(xn_ready, 1)
                    if t >= 1:
                        n = t - 1
                        dve.wait_ge(turn_hi, batch_turns(b) + n + 1)
                        low(xT_lo[:, :, n * P:(n + 1) * P], turn[:, n % 2], xT_hi[:, :, n * P:(n + 1) * P], turn_lo)
                for n in range(2):
                    dve.wait_ge(lat_hi_done, b * 4 + n + 1)
                    cols = slice(n * BANK, (n + 1) * BANK)
                    low(latT_lo[:, cols], slot[:, n, 0:BANK], latT_hi[:, cols], lat_lo_done)
                    nc.vector.tensor_copy(xn[:, n, :], slot[:, n, 0:BANK]).then_inc(lat_copied, 1)
                for n in range(2):
                    dve.wait_ge(lat_hi_done, b * 4 + 2 + n + 1)
                    low(lat_lo[:, n * GT:(n + 1) * GT, :].rearrange("p t d -> p (t d)"), slot[:, n, 0:BANK],
                        lat_hi[:, n * GT:(n + 1) * GT, :].rearrange("p t d -> p (t d)"), lat_lo_done)

                def step(kind, u, r, ring0, turns0):
                    if kind == "head":
                        if 1 <= u <= TB:
                            n = u - 1
                            tile = banks("qk", n)[:, 0:4 * DK].rearrange("p (h d) -> p h d", h=4)
                            dve.wait_ge(rstd_ready, r * TB + n + 1)
                            nc.vector.tensor_tensor(qk[:, n % 4, 2:4, :], tile[:, 2:4, :],
                                                    rstd[:, n, 2:4].unsqueeze(2).to_broadcast([P, 2, DK]),
                                                    ALU.mult).then_inc(kr_scaled, 1)
                            both = qk[:, n % 4, :, 0:DR].rearrange("p h (k d) -> p h k d", k=2)[:, :, :, 0:RQ]
                            a, c = both[:, :, 0, :], both[:, :, 1, :]
                            dve.wait_ge(q_scaled, r * TB + n + 1)
                            dve.wait_ge(kr_scaled, r * TB + n + 1)
                            for k, table in enumerate((cos_t, sin_t)):
                                nc.vector.tensor_tensor(
                                    turned[:, k], both,
                                    table[:, n, :].unsqueeze(1).unsqueeze(1).to_broadcast([P, 4, 2, RQ]),
                                    ALU.mult).then_inc(rope_parts, 1)
                            dve.wait_ge(rope_parts, (r * TB + n) * 2 + 2)
                            nc.vector.tensor_tensor(a, turned[:, 0, :, 0, :], turned[:, 1, :, 1, :], ALU.add) \
                                .then_inc(rope_done, 1)
                            nc.vector.tensor_tensor(c, turned[:, 0, :, 1, :], turned[:, 1, :, 0, :],
                                                    ALU.subtract).then_inc(rope_done, 1)
                        if u < TB:
                            tile = banks("qk", u)[:, 0:4 * DK].rearrange("p (h d) -> p h d", h=4)
                            dve.wait_ge(summed, r * TB + u + 1)
                            if u >= 4:
                                dve.wait_ge(turn_filled, turns0 + turns["qkT", u - 4] + 1)
                            nc.vector.tensor_tensor(qk[:, u % 4, 0:2, :], tile[:, 0:2, :],
                                                    q_norm[:].unsqueeze(1).to_broadcast([P, 2, DK]), ALU.mult) \
                                .then_inc(q_scaled, 1)
                        if u >= 3:
                            n = u - 3
                            w = turns["qkT", n]
                            cols = slice(n * P, (n + 1) * P)
                            dve.wait_ge(turn_hi, turns0 + w + 1)
                            nc.vector.tensor_tensor(qkT_lo[:, 0:2, cols], turn[:, w % 2, 0:2, :],
                                                    qkT_hi[:, 0:2, cols], ALU.subtract)
                            nc.vector.scalar_tensor_tensor(out=qkT_lo[:, 2:4, cols], in0=turn[:, w % 2, 2:4, :],
                                                           scalar=k_scale[:, 0:1], in1=qkT_hi[:, 2:4, cols],
                                                           op0=ALU.mult, op1=ALU.subtract).then_inc(turn_lo, 1)
                        return
                    def maxima():
                        if u < STEPS:
                            _, h, t = step_of(u)
                            width = (t + 1) * P
                            one = slice(u % 2, u % 2 + 1)
                            dve.wait_ge(slot_filled, ring0 + use("scores", u) + 1)
                            nc.vector.tensor_reduce(row_max[:, one], banks("scores", u)[:, 0:width],
                                                    AXIS_X, ALU.max).then_inc(max_ready, 1)
                            dve.wait_ge(max_ready, r * STEPS + u + 1)
                            nc.vector.tensor_scalar(shift[:, one], row_max[:, one], rstd[:, t, h:h + 1], -1.0,
                                                    ALU.mult, ALU.mult).then_inc(shift_ready, 1)

                    def normalise():
                        if 1 <= u <= STEPS:
                            n = u - 1
                            width = (step_of(n)[2] + 1) * P
                            one = slice(n % 2, n % 2 + 1)
                            dve.wait_ge(exp_done, r * STEPS + n + 1)
                            nc.vector.reciprocal(row_inv[:, one], row_sum[:, one]).then_inc(inv_ready, 1)
                            dve.wait_ge(inv_ready, r * STEPS + n + 1)
                            nc.vector.tensor_scalar(probs[:, n % 3, 0:width], probs[:, n % 3, 0:width],
                                                    row_inv[:, one], None, ALU.mult).then_inc(probs_ready, 1)

                    def value_lows():
                        if u - SPLIT_LAG in pv_steps:
                            n = pv_steps.index(u - SPLIT_LAG)
                            dve.wait_ge(oT_hi_done, r * GROUPS + n + 1)
                            low(oT_lo[:, n % 4, :], pv[:], oT_hi[:, n % 4, :], oT_lo_done)

                    def probs_lows():
                        if 2 <= u < STEPS + 2:
                            _, h, t = step_of(u - 2)
                            j = (u - 2) % GQ
                            for c, blocks in enumerate(chunks(t)):
                                w = turns["probsT", u - 2, c]
                                there = slice(blocks[0], blocks[-1] + 1)
                                dve.wait_ge(turn_hi, turns0 + w + 1)
                                low(pT_lo[:, h, there, j * P:(j + 1) * P], turn[:, w % 2, 0:len(blocks), :],
                                    pT_hi[:, h, there, j * P:(j + 1) * P], turn_lo)

                    def add_outputs():
                        for t in out_tiles_at(u):
                            dve.wait_ge(out_filled, r * TB + t + 1)
                            nc.vector.tensor_tensor(acc[:, t, :], out_ps[:, 0:D], acc[:, t, :], ALU.add) \
                                .then_inc(out_added, 1)

                    maxima()
                    normalise()
                    probs_lows()
                    add_outputs()
                    value_lows()

                rounds(dve, b, step)

        @block.tensor
        def _(pe):
            pe.wait_ge(consts_made, 9)
            pe.wait_ge(down_lo_done, 1)
            with pe.Fori(0, B) as b:
                for t in range(TB):
                    pe.wait_ge(xn_ready, b * TB + t + 1)
                    if t >= 2:
                        pe.wait_ge(turn_lo, batch_turns(b) + t - 1)
                    for c in range(DC):
                        last = nc.tensor.transpose(turn[:, t % 2, c, :], xn[:, t % 2, c * P:(c + 1) * P], ident[:])
                    last.then_inc(turn_filled, 1)
                pe.wait_ge(turn_lo, batch_turns(b) + TB)
                for n in range(2):
                    cols = slice(n * BANK, (n + 1) * BANK)
                    for c in range(DC):
                        mm3(nc.tensor, slot[:, n, 0:BANK], (down_hi[:, c, :], down_lo[:, c, :]),
                            (xT_hi[:, c, cols], xT_lo[:, c, cols]), start=c == 0, stop=c == DC - 1,
                            signal=slot_filled if c == DC - 1 else None)
                for n in range(2):
                    pe.wait_ge(lat_copied, b * 2 + n + 1)
                    for j in range(GT):
                        last = nc.tensor.transpose(slot[:, n, j * P:(j + 1) * P], xn[:, n, j * P:(j + 1) * P],
                                                   ident[:])
                    last.then_inc(slot_filled, 1)
                pe.wait_ge(lat_lo_done, b * 4 + 4)

                def step(kind, u, r, ring0, turns0):
                    def bank_free(kind, n):
                        at = use(kind, n)
                        if at < 4:
                            pe.wait_ge(exp_done, r * STEPS)
                        elif at < 2 * TB and at - 4 < TB:
                            pe.wait_ge(kr_scaled, r * TB + at - 4 + 1)
                        elif at < 2 * TB:
                            pe.wait_ge(exp_done, r * STEPS + at - 4 - TB + 1)
                        else:
                            pe.wait_ge(exp_done, r * STEPS + n - 2 + 1)

                    def turn_free(w):
                        pe.wait_ge(turn_lo, turns0 + w - 1)

                    def scores(u):
                        _, h, t = step_of(u)
                        if u < TB:
                            pe.wait_ge(turn_lo, turns0 + turns["qkT", max(t, 1)] + 1)
                        elif u == TB:
                            pe.wait_ge(turn_lo, turns0 + turns["qkT", TB - 1] + 1)
                        bank_free("scores", u)
                        into = banks("scores", u)
                        q_cols = slice(t * P, (t + 1) * P)
                        width = (t + 1) * P
                        for a in range(0, width, BANK):
                            z = max(min(a + BANK, width), a + 2 * P)
                            whole = z < width
                            mm3(nc.tensor, into[:, a:z], (qkT_hi[:, h, q_cols], qkT_lo[:, h, q_cols]),
                                (qkT_hi[:, 2 + h, a:z], qkT_lo[:, 2 + h, a:z]), stop=whole)
                        nc.tensor.matmul(into[:, width - P:width], ident_b[:], mask_b[:], start=False,
                                         stop=True).then_inc(slot_filled, 1)

                    if kind == "head":
                        if u == 0:
                            pe.wait_ge(wqk_loaded, 32 * r + 32)
                        if u < TB:
                            bank_free("qk", u)
                            into = banks("qk", u)
                            cols = slice(u * P, (u + 1) * P)
                            for c in range(DC):
                                mm3(nc.tensor, into[:, 0:2 * DK], (xT_hi[:, c, cols], xT_lo[:, c, cols]),
                                    (wqk(wqk_hi, c), wqk(wqk_lo, c)), start=c == 0, stop=c == DC - 1)
                            mm3(nc.tensor, into[:, 2 * DK:4 * DK], (latT_hi[:, cols], latT_lo[:, cols]),
                                (wqk(wqk_hi, DC), wqk(wqk_lo, DC)), signal=slot_filled)
                        if u >= 3:
                            n = u - 3
                            w = turns["qkT", n]
                            pe.wait_ge(rope_done, (r * TB + n) * 2 + 2)
                            turn_free(w)
                            for k in range(4):
                                last = nc.tensor.transpose(turn[:, w % 2, k, :], qk[:, n % 4, k, :], ident[:])
                            last.then_inc(turn_filled, 1)
                        return
                    def score_products():
                        if u == 0:
                            scores(0)
                        if u + 1 < STEPS:
                            scores(u + 1)

                    def outputs():
                        for t in out_tiles_at(u):
                            g, j = t // GQ, t % GQ
                            if j == 0:
                                pe.wait_ge(oT_lo_done, r * GROUPS + 2 * g + 2)
                            if t == 0:
                                pe.wait_ge(wvo_loaded, 32 * r + 32)
                            pe.wait_ge(out_added, r * TB + t)
                            cols = slice(j * P, (j + 1) * P)
                            for h in range(2):
                                mm3(nc.tensor, out_ps[:, 0:D], (oT_hi[:, 2 * (g % 2) + h, cols], oT_lo[:, 2 * (g % 2) + h, cols]),
                                    (wvo_hi[:, h, :], wvo_lo[:, h, :]), start=h == 0, stop=h == 1,
                                    signal=out_filled if h == 1 else None)

                    def value_products():
                        if u in pv_steps:
                            n = pv_steps.index(u)
                            g = n // 2
                            last_turn = turns["probsT", u - 3, len(chunks(step_of(u - 3)[2])) - 1]
                            pe.wait_ge(turn_lo, turns0 + last_turn + 1)
                            pe.wait_ge(oT_lo_done, r * GROUPS + n)
                            for k in range(GQ * g + GQ):
                                a = 0 if k == TB - 1 else max(0, k - GQ * g) * P
                                mm3(nc.tensor, pv[:, a:GQ * P], (lat_hi[:, k, :], lat_lo[:, k, :]),
                                    (pT_hi[:, n % 2, k, a:GQ * P], pT_lo[:, n % 2, k, a:GQ * P]), start=k == 0,
                                    stop=k == GQ * g + GQ - 1,
                                    signal=pv_filled if k == GQ * g + GQ - 1 else None)

                    def turn_probs():
                        if 2 <= u < STEPS + 2:
                            _, _, t = step_of(u - 2)
                            pe.wait_ge(probs_ready, r * STEPS + u - 1)
                            for c, blocks in enumerate(chunks(t)):
                                w = turns["probsT", u - 2, c]
                                turn_free(w)
                                for k in blocks:
                                    last = nc.tensor.transpose(turn[:, w % 2, k - blocks[0], :],
                                                               probs[:, (u - 2) % 3, k * P:(k + 1) * P], ident[:])
                                last.then_inc(turn_filled, 1)

                    turn_probs()
                    outputs()
                    score_products()
                    value_products()

                rounds(pe, b, step)




def ffn_tokens(nc, keep, x2_dram, norm_rows, router_w, shared_w, h_dram, base_dram):
    G = T // BANK
    SF = SH // P
    with ExitStack() as ctx:
        def sb(name, shape, dt=F32):
            return ctx.enter_context(nc.sbuf_tensor("ft_" + name, shape, dt))

        def ps(name, shape):
            return ctx.enter_context(nc.psum_tensor("ft_" + name, shape, F32))

        def sem(name):
            return ctx.enter_context(nc.semaphore("ft_" + name))

        w_raw = sb("w_raw", [P, 3 * DC * SH])
        w_hi = sb("w_hi", [P, 3, DC, SH], F32R)
        w_lo = sb("w_lo", [P, 3, DC, SH], F32R)
        router_raw = sb("router_raw", [P, DC, E])
        router_hi = sb("router_hi", [P, DC, E], F32R)
        router_lo = sb("router_lo", [P, DC, E], F32R)
        norm_raw = sb("norm_raw", [P, D])
        norm = sb("norm", [P, D])
        ident = sb("ident", [P, P])
        before = sb("before", [P, P], BF16)
        ones = sb("ones", [P, P], BF16)
        iota_i = sb("iota_i", [P, E], mybir.dt.int32)
        iota = sb("iota", [P, E])
        minus_half = sb("minus_half", [P, GT])
        ln_eps = sb("ln_eps", [P, GT])
        ffn_eps = sb("ffn_eps", [P, GT])

        scratch = sb("scratch", [P, 5])
        x2 = sb("x2", [P, GT, D])
        stats = sb("stats", [P, GT, 6])
        mean_var = sb("mean_var", [P, GT, 2])
        var = sb("var", [P, GT])
        rstd = sb("rstd", [P, GT])
        h0 = sb("h0", [P, GT, D])
        squares = sb("squares", [P, D])
        sums = sb("sums", [P, GT])
        sums_eps = sb("sums_eps", [P, GT])
        rms = sb("rms", [P, GT])
        h = sb("h", [P, GT, D])
        residual = sb("residual", [P, GT, D])
        base = sb("base", [P, GT, D])
        hT_hi = sb("hT_hi", [P, DC, BANK], F32R)
        hT_lo = sb("hT_lo", [P, DC, BANK], F32R)
        logits = sb("logits", [P, GT, E])
        top = sb("top", [P, GT, 8])
        top_id = sb("top_id", [P, GT, 8], U32)
        top_idf = sb("top_idf", [P, GT, K])
        top_less = sb("top_less", [P, GT, K])
        top_exp = sb("top_exp", [P, GT, K])
        top_sum = sb("top_sum", [P, GT])
        top_inv = sb("top_inv", [P, GT])
        chosen = sb("chosen", [P, GT, E], BF16)
        silu = sb("silu", [P, 2, BANK])
        inner = sb("inner", [P, 2, BANK])
        inner_hi = sb("inner_hi", [P, SF, BANK], F32R)
        inner_lo = sb("inner_lo", [P, SF, BANK], F32R)

        turn = ps("turn", [P, 2, DC, P])
        gate_up = ps("gate_up", [P, 2, 2, BANK])
        small = ps("small", [P, GT, E])
        rank_ps = ps("rank_ps", [P, GT + 1, E])

        loaded, made, w_hi_done, w_lo_done, norm_done = (
            sem("loaded"), sem("made"), sem("w_hi_done"), sem("w_lo_done"), sem("norm_done"))
        x2_loaded, h_stored, base_stored = sem("x2_loaded"), sem("h_stored"), sem("base_stored")
        stats_done, aggr_done, var_done, rstd_done, h0_done = (
            sem("stats_done"), sem("aggr_done"), sem("var_done"), sem("rstd_done"), sem("h0_done"))
        squared, eps_done, rms_done, h_done, residual_done = (
            sem("squared"), sem("eps_done"), sem("rms_done"), sem("h_done"), sem("residual_done"))
        turn_filled, turn_hi, turn_lo = sem("turn_filled"), sem("turn_hi"), sem("turn_lo")
        logits_filled, logits_copied, top_done, id_done = (
            sem("logits_filled"), sem("logits_copied"), sem("top_done"), sem("id_done"))
        less_done, exp_done, sum_done, inv_done, weights_done = (
            sem("less_done"), sem("exp_done"), sem("sum_done"), sem("inv_done"), sem("weights_done"))
        hot_done, chosen_done, rank_filled, rank_done, count_done = (
            sem("hot_done"), sem("chosen_done"), sem("rank_filled"), sem("rank_done"), sem("count_done"))
        gu_filled, silu_done, inner_done, inner_hi_done, inner_lo_done = (
            sem("gu_filled"), sem("silu_done"), sem("inner_done"), sem("inner_hi_done"), sem("inner_lo_done"))
        down_filled, base_done = sem("down_filled"), sem("base_done")

        block = ctx.enter_context(nc.Block())

        @block.sync
        def _(sp):
            sp.dma_start(w_raw[:], shared_w).then_inc(loaded, 16)
            sp.dma_start(router_raw[:], router_w).then_inc(loaded, 16)
            sp.dma_start(norm_raw[:], norm_rows).then_inc(loaded, 16)
            with sp.Fori(0, G) as g:
                sp.wait_ge(residual_done, g)
                sp.dma_start(x2[:], x2_dram[bass.ds(g, 1)].rearrange("o (t p) d -> p (o t) d", p=P)) \
                  .then_inc(x2_loaded, 16)
                sp.wait_ge(h_done, g * GT + GT)
                sp.dma_start(h_dram[bass.ds(g, 1)].rearrange("o (t p) d -> p (o t) d", p=P), h[:]) \
                  .then_inc(h_stored, 16)
                sp.wait_ge(base_done, g * GT + GT)
                sp.dma_start(base_dram[bass.ds(g, 1)].rearrange("o (t p) d -> p (o t) d", p=P), base[:]) \
                  .then_inc(base_stored, 16)
            sp.wait_ge(h_stored, 16 * G)
            sp.wait_ge(base_stored, 16 * G)

        @block.gpsimd
        def _(pool):
            nc.gpsimd.memset(ident[:], 0.0).then_inc(made, 1)
            nc.gpsimd.memset(before[:], 1.0).then_inc(made, 1)
            nc.gpsimd.memset(ones[:], 1.0).then_inc(made, 1)
            nc.gpsimd.memset(minus_half[:], -0.5).then_inc(made, 1)
            nc.gpsimd.memset(ln_eps[:], LN_EPS).then_inc(made, 1)
            nc.gpsimd.memset(ffn_eps[:], FFN_EPS * D).then_inc(made, 1)
            nc.gpsimd.iota(iota_i[:], pattern=[[1, E]], base=0, channel_multiplier=0).then_inc(made, 1)
            pool.wait_ge(made, 7)
            nc.gpsimd.affine_select(out=ident[:], in_=ident[:], compare_op=ALU.not_equal, fill=1.0, base=0,
                                    pattern=[[-1, P]], channel_multiplier=1).then_inc(made, 1)
            nc.gpsimd.affine_select(out=before[:], in_=before[:], compare_op=ALU.is_gt, fill=0.0, base=0,
                                    pattern=[[1, P]], channel_multiplier=-1).then_inc(made, 1)
            nc.gpsimd.tensor_copy(iota[:], iota_i[:]).then_inc(made, 1)
            pool.wait_ge(made, 10)
            with pool.Fori(0, G) as g:
                pool.wait_ge(aggr_done, g * GT + GT)
                nc.gpsimd.tensor_tensor(var[:], mean_var[:, :, 1:2].rearrange("p t o -> p (t o)"), ln_eps[:],
                                        ALU.add).then_inc(var_done, 1)
                pool.wait_ge(var_done, g + 1)
                nc.gpsimd.tensor_tensor(rstd[:], var[:], minus_half[:], ALU.pow).then_inc(rstd_done, 1)
                pool.wait_ge(squared, g * GT + GT)
                nc.gpsimd.tensor_tensor(sums_eps[:], sums[:], ffn_eps[:], ALU.add).then_inc(eps_done, 1)
                pool.wait_ge(eps_done, g + 1)
                nc.gpsimd.tensor_tensor(rms[:], sums_eps[:], minus_half[:], ALU.pow).then_inc(rms_done, 1)
                pool.wait_ge(base_done, g * GT)
                nc.gpsimd.tensor_tensor(residual[:], x2[:], h0[:], ALU.add).then_inc(residual_done, 1)

        @block.scalar
        def _(act):
            act.wait_ge(loaded, 48)
            nc.scalar.activation(w_hi[:].rearrange("p w c n -> p (w c n)"), w_raw[:], ACT.Copy) \
                .then_inc(w_hi_done, 1)
            nc.scalar.activation(router_hi[:], router_raw[:], ACT.Copy).then_inc(w_hi_done, 1)
            with act.Fori(0, G) as g:
                for t in range(GT):
                    act.wait_ge(h0_done, g * GT + t + 1)
                    if t == 0:
                        act.wait_ge(squared, g * GT)
                    else:
                        act.wait_ge(squared, g * GT + t)
                    nc.scalar.activation(squares[:], h0[:, t, :], ACT.Square, accum_out=sums[:, t:t + 1]) \
                        .then_inc(squared, 1)
                for t in range(GT):
                    act.wait_ge(turn_filled, g * GT + t + 1)
                    nc.scalar.activation(hT_hi[:, :, t * P:(t + 1) * P], turn[:, t % 2], ACT.Copy) \
                        .then_inc(turn_hi, 1)
                act.wait_ge(logits_filled, g + 1)
                nc.scalar.activation(logits[:], small[:], ACT.Copy).then_inc(logits_copied, 1)
                act.wait_ge(less_done, g + 1)
                nc.scalar.activation(top_exp[:], top_less[:], ACT.Exp).then_inc(exp_done, 1)
                for f in range(SF):
                    act.wait_ge(gu_filled, g * SF + f + 1)
                    if f >= 2:
                        act.wait_ge(inner_done, g * SF + f - 1)
                    nc.scalar.activation(silu[:, f % 2, :], gate_up[:, f % 2, 0, :], ACT.Silu) \
                        .then_inc(silu_done, 1)
                    act.wait_ge(inner_done, g * SF + f + 1)
                    nc.scalar.activation(inner_hi[:, f, :], inner[:, f % 2, :], ACT.Copy) \
                        .then_inc(inner_hi_done, 1)

        @block.vector
        def _(dve):
            dve.wait_ge(loaded, 48)
            nc.vector.tensor_scalar(norm[:], norm_raw[:], float(np.sqrt(D)), None, ALU.mult).then_inc(norm_done, 1)
            nc.vector.memset(keep.count[:], 0.0).then_inc(count_done, 1)
            nc.vector.memset(scratch[:], 0.0).then_inc(norm_done, 1)
            dve.wait_ge(made, 10)
            dve.wait_ge(w_hi_done, 2)
            nc.vector.tensor_tensor(w_lo[:].rearrange("p w c n -> p (w c n)"), w_raw[:],
                                    w_hi[:].rearrange("p w c n -> p (w c n)"), ALU.subtract) \
                .then_inc(w_lo_done, 1)
            nc.vector.tensor_tensor(router_lo[:], router_raw[:], router_hi[:], ALU.subtract) \
                .then_inc(w_lo_done, 1)
            dve.wait_ge(norm_done, 2)
            with dve.Fori(0, G) as g:
                dve.wait_ge(x2_loaded, 16 * g + 16)
                for t in range(GT):
                    nc.vector.bn_stats(stats[:, t, :], x2[:, t, :]).then_inc(stats_done, 1)
                wait_apart(dve, scratch, 1, stats_done, g * GT + GT)
                for t in range(GT):
                    nc.vector.bn_aggr(mean_var[:, t, :], stats[:, t, :]).then_inc(aggr_done, 1)
                dve.wait_ge(rstd_done, g + 1)
                for t in range(GT):
                    nc.vector.tensor_scalar(h0[:, t, :], x2[:, t, :], mean_var[:, t, 0:1], rstd[:, t:t + 1],
                                            ALU.subtract, ALU.mult).then_inc(h0_done, 1)
                dve.wait_ge(rms_done, g + 1)
                dve.wait_ge(h_stored, 16 * g)
                for t in range(GT):
                    nc.vector.scalar_tensor_tensor(out=h[:, t, :], in0=h0[:, t, :], scalar=rms[:, t:t + 1],
                                                   in1=norm[:], op0=ALU.mult, op1=ALU.mult).then_inc(h_done, 1)
                for t in range(GT):
                    cols = slice(t * P, (t + 1) * P)
                    dve.wait_ge(turn_hi, g * GT + t + 1)
                    nc.vector.tensor_tensor(hT_lo[:, :, cols], turn[:, t % 2], hT_hi[:, :, cols], ALU.subtract) \
                        .then_inc(turn_lo, 1)
                wait_apart(dve, scratch, 2, logits_copied, g + 1)
                for t in range(GT):
                    nc.vector.max(top[:, t, :], logits[:, t, :]).then_inc(top_done, 1)
                wait_apart(dve, scratch, 3, top_done, g * GT + GT)
                for t in range(GT):
                    nc.vector.max_index(top_id[:, t, :], top[:, t, :], logits[:, t, :]).then_inc(id_done, 1)
                nc.vector.tensor_tensor(top_less[:], top[:, :, 0:K], top[:, :, 0:1].to_broadcast([P, GT, K]),
                                        ALU.subtract).then_inc(less_done, 1)
                dve.wait_ge(id_done, g * (GT + 1) + GT)
                nc.vector.tensor_copy(top_idf[:], top_id[:, :, 0:K]).then_inc(id_done, 1)
                dve.wait_ge(id_done, g * (GT + 1) + GT + 1)
                hot = keep.hot[:, bass.ds(g * GT * K, GT * K), :]
                nc.vector.tensor_tensor(hot, iota[:].unsqueeze(1).to_broadcast([P, GT * K, E]),
                                        top_idf[:].rearrange("p t k -> p (t k)").unsqueeze(2)
                                        .to_broadcast([P, GT * K, E]), ALU.is_equal).then_inc(hot_done, 1)
                dve.wait_ge(exp_done, g + 1)
                nc.vector.tensor_reduce(top_sum[:], top_exp[:], AXIS_X, ALU.add).then_inc(sum_done, 1)
                dve.wait_ge(sum_done, g + 1)
                nc.vector.reciprocal(top_inv[:], top_sum[:]).then_inc(inv_done, 1)
                dve.wait_ge(inv_done, g + 1)
                nc.vector.tensor_tensor(keep.top_w[:, bass.ds(g * GT * K, GT * K)].rearrange("p (t k) -> p t k", k=K), top_exp[:],
                                        top_inv[:].unsqueeze(2).to_broadcast([P, GT, K]), ALU.mult) \
                    .then_inc(weights_done, 1)
                wait_apart(dve, scratch, 4, hot_done, g + 1)
                with nc.allow_low_precision("a sum of at most four ones"):
                    nc.vector.tensor_reduce(chosen[:], hot.rearrange("p (t k) e -> p t e k", k=K), AXIS_X,
                                            ALU.add).then_inc(chosen_done, 1)
                dve.wait_ge(rank_filled, g + 1)
                dve.wait_ge(count_done, g + 1)
                nc.vector.tensor_tensor(keep.rank[:, bass.ds(g * GT, GT), :], rank_ps[:, 0:GT, :],
                                        keep.count[:].unsqueeze(1).to_broadcast([P, GT, E]), ALU.add) \
                    .then_inc(rank_done, 1)
                dve.wait_ge(rank_done, g + 1)
                nc.vector.tensor_tensor(keep.count[:], rank_ps[:, GT, :], keep.count[:], ALU.add) \
                    .then_inc(count_done, 1)
                for f in range(SF):
                    dve.wait_ge(silu_done, g * SF + f + 1)
                    if f >= 2:
                        dve.wait_ge(inner_hi_done, g * SF + f - 1)
                        dve.wait_ge(inner_lo_done, g * SF + f - 1)
                    nc.vector.tensor_tensor(inner[:, f % 2, :], gate_up[:, f % 2, 1, :], silu[:, f % 2, :],
                                            ALU.mult).then_inc(inner_done, 1)
                    dve.wait_ge(inner_hi_done, g * SF + f + 1)
                    nc.vector.tensor_tensor(inner_lo[:, f, :], inner[:, f % 2, :], inner_hi[:, f, :],
                                            ALU.subtract).then_inc(inner_lo_done, 1)
                dve.wait_ge(residual_done, g + 1)
                dve.wait_ge(base_stored, 16 * g)
                for t in range(GT):
                    dve.wait_ge(down_filled, g * GT + t + 1)
                    nc.vector.tensor_tensor(base[:, t, :], gate_up[:, t % 2, 0, :], residual[:, t, :], ALU.add) \
                        .then_inc(base_done, 1)

        @block.tensor
        def _(pe):
            pe.wait_ge(made, 10)
            pe.wait_ge(w_lo_done, 2)
            with pe.Fori(0, G) as g:
                for t in range(GT):
                    pe.wait_ge(h_done, g * GT + t + 1)
                    if t < 2:
                        pe.wait_ge(turn_lo, g * GT)
                    else:
                        pe.wait_ge(turn_lo, g * GT + t - 1)
                    for c in range(DC):
                        last = nc.tensor.transpose(turn[:, t % 2, c, :], h[:, t, c * P:(c + 1) * P], ident[:])
                    last.then_inc(turn_filled, 1)
                pe.wait_ge(turn_lo, g * GT + GT)
                pe.wait_ge(logits_copied, g)
                for t in range(GT):
                    cols = slice(t * P, (t + 1) * P)
                    for c in range(DC):
                        mm3(nc.tensor, small[:, t, :], (hT_hi[:, c, cols], hT_lo[:, c, cols]),
                            (router_hi[:, c, :], router_lo[:, c, :]), start=c == 0, stop=c == DC - 1,
                            signal=logits_filled if c == DC - 1 and t == GT - 1 else None)

                def ranks():
                    pe.wait_ge(chosen_done, g + 1)
                    pe.wait_ge(count_done, g + 1)
                    for t in range(GT + 1):
                        for s in range(min(t + 1, GT)):
                            last = nc.tensor.matmul(rank_ps[:, t, :], before[:] if s == t else ones[:],
                                                    chosen[:, s, :], start=s == 0, stop=s == min(t, GT - 1))
                    last.then_inc(rank_filled, 1)

                for f in range(SF):
                    if f < 2:
                        pe.wait_ge(base_done, g * GT)
                    else:
                        pe.wait_ge(inner_done, g * SF + f - 1)
                    for w in range(2):
                        for c in range(DC):
                            cols = slice(f * P, (f + 1) * P)
                            mm3(nc.tensor, gate_up[:, f % 2, w, :], (w_hi[:, w, c, cols], w_lo[:, w, c, cols]),
                                (hT_hi[:, c, :], hT_lo[:, c, :]), start=c == 0, stop=c == DC - 1,
                                signal=gu_filled if c == DC - 1 and w == 1 else None)
                    if f == 1:
                        ranks()
                pe.wait_ge(inner_lo_done, g * SF + SF)
                for t in range(GT):
                    if t >= 2:
                        pe.wait_ge(base_done, g * GT + t - 1)
                    cols = slice(t * P, (t + 1) * P)
                    for f in range(SF):
                        mm3(nc.tensor, gate_up[:, t % 2, 0, :], (inner_hi[:, f, cols], inner_lo[:, f, cols]),
                            (w_hi[:, 2, f, :], w_lo[:, 2, f, :]), start=f == 0, stop=f == SF - 1,
                            signal=down_filled if f == SF - 1 else None)


def dispatch(nc, keep, table_dram):
    with ExitStack() as ctx:
        def sb(name, shape, dt=F32):
            return ctx.enter_context(nc.sbuf_tensor("di_" + name, shape, dt))

        def sem(name):
            return ctx.enter_context(nc.semaphore("di_" + name))

        I32 = mybir.dt.int32
        padded = sb("padded", [P, E], I32)
        tiles_i = sb("tiles_i", [P, E], I32)
        tiles_raw = sb("tiles_raw", [P, E])
        tiles = sb("tiles", [P, E])
        ones = sb("ones", [P, E])
        ends = sb("ends", [P, E])
        starts = sb("starts", [P, E])
        first = sb("first", [P, E])
        place = sb("place", [P, NT, E])
        placed = sb("placed", [P, NT * K, E])
        slot_f = sb("slot_f", [P, NT * K])
        tile_i = sb("tile_i", [P, SLOT_TILES], I32)
        tile_n = sb("tile_n", [P, SLOT_TILES])
        ended = sb("ended", [P, SLOT_TILES, E])
        owner = sb("owner", [P, SLOT_TILES])
        first_tile = sb("first_tile", [P, SLOT_TILES])
        upcoming = sb("upcoming", [P, SLOT_TILES])
        token_i = sb("token_i", [P, NT], I32)
        token = sb("token", [P, NT])
        zeros = sb("zeros", [P, SLOT_TILES])
        scratch = sb("scratch", [P, 5])
        token_now = sb("token_now", [P, 2, 1])
        slot_now = sb("slot_now", [P, 2, K], U32)
        made, step, zeroed, slots_ready = sem("made"), sem("step"), sem("zeroed"), sem("slots_ready")
        copied, scattered = sem("copied"), [sem("scattered0"), sem("scattered1")]
        block = ctx.enter_context(nc.Block())

        @block.sync
        def _(sp):
            sp.wait_ge(made, 4)
            sp.dma_start(table_dram.rearrange("(p n) o -> p (n o)", p=P), zeros[:]).then_inc(zeroed, 16)
            sp.wait_ge(zeroed, 16)

        @block.vector
        def _(dve):
            done = [0]

            def then(ins):
                done[0] += 1
                ins.then_inc(step, 1)
                dve.wait_ge(step, done[0])

            nc.vector.memset(ones[:], 1.0)
            then(nc.vector.tensor_scalar(padded[:], keep.count[:], float(P - 1), None, ALU.add))
            then(nc.vector.tensor_scalar(tiles_i[:], padded[:], P.bit_length() - 1, None,
                                         ALU.logical_shift_right))
            then(nc.vector.tensor_copy(tiles_raw[:], tiles_i[:]))
            then(nc.vector.tensor_scalar(tiles[:], tiles_raw[:], 1.0, None, ALU.max))
            then(nc.vector.tensor_tensor_scan(ends[:], ones[:], tiles[:], 0.0, ALU.mult, ALU.add))
            then(nc.vector.tensor_tensor(starts[:], ends[:], tiles[:], ALU.subtract))
            then(nc.vector.tensor_scalar(first[:], starts[:], float(P), None, ALU.mult))
            then(nc.vector.tensor_tensor(place[:], keep.rank[:], first[:].unsqueeze(1).to_broadcast([P, NT, E]),
                                         ALU.add))
            for k in range(K):
                ins = nc.vector.tensor_tensor(
                    placed[:].rearrange("p (t k) e -> p t k e", k=K)[:, :, k, :],
                    keep.hot[:].rearrange("p (t k) e -> p t k e", k=K)[:, :, k, :], place[:], ALU.mult)
            then(ins)
            then(nc.vector.tensor_reduce(slot_f[:], placed[:], AXIS_X, ALU.add))
            nc.vector.tensor_copy(keep.slots[:], slot_f[:]).then_inc(slots_ready, 1)
            dve.wait_ge(made, 6)
            then(nc.vector.tensor_tensor(ended[:], tile_n[:].unsqueeze(2).to_broadcast([P, SLOT_TILES, E]),
                                         ends[:].unsqueeze(1).to_broadcast([P, SLOT_TILES, E]), ALU.is_ge))
            then(nc.vector.tensor_reduce(owner[:], ended[:], AXIS_X, ALU.add))
            then(nc.vector.tensor_scalar(owner[:], owner[:], float(E - 1), None, ALU.min))
            nc.vector.tensor_copy(keep.owner[:], owner[:])
            then(nc.vector.memset(first_tile[:, 0:1], 1.0))
            then(nc.vector.tensor_tensor(first_tile[:, 1:SLOT_TILES], owner[:, 1:SLOT_TILES],
                                         owner[:, 0:SLOT_TILES - 1], ALU.is_gt))
            then(nc.vector.tensor_scalar(upcoming[:], owner[:], float(E - 1), None, ALU.is_lt))
            then(nc.vector.tensor_tensor(upcoming[:], upcoming[:], first_tile[:], ALU.mult))
            then(nc.vector.scalar_tensor_tensor(out=keep.next_weights[:], in0=owner[:], scalar=1.0,
                                                in1=upcoming[:], op0=ALU.add, op1=ALU.mult))

        @block.gpsimd
        def _(pool):
            nc.gpsimd.iota(tile_i[:], pattern=[[1, SLOT_TILES]], base=0, channel_multiplier=0).then_inc(made, 1)
            nc.gpsimd.iota(token_i[:], pattern=[[P, NT]], base=0, channel_multiplier=1).then_inc(made, 1)
            nc.gpsimd.memset(zeros[:], 0.0).then_inc(made, 1)
            nc.gpsimd.memset(scratch[:], 0.0).then_inc(made, 1)
            pool.wait_ge(made, 4)
            nc.gpsimd.tensor_copy(tile_n[:], tile_i[:]).then_inc(made, 1)
            nc.gpsimd.tensor_copy(token[:], token_i[:]).then_inc(made, 1)
            pool.wait_ge(made, 6)
            pool.wait_ge(slots_ready, 1)
            pool.wait_ge(zeroed, 16)
            with pool.Fori(0, NT // 2) as i:
                for s in range(2):
                    pool.wait_ge(scattered[s], 16 * K * i)
                    nc.gpsimd.tensor_copy(token_now[:, s, :], token[:, bass.ds(2 * i + s, 1)]).then_inc(copied, 1)
                    nc.gpsimd.tensor_copy(slot_now[:, s, :], keep.slots[:, bass.ds((2 * i + s) * K, K)]) \
                        .then_inc(copied, 1)
                    wait_apart(pool, scratch, 1 + s, copied, 4 * i + 2 * s + 2)
                    for k in range(K):
                        nc.gpsimd.indirect_dma_start(
                            table_dram, bass.IndirectOffsetOnAxis(ap=slot_now[:, s, k:k + 1], axis=0),
                            token_now[:, s, :], None).then_inc(scattered[s], 16)
            for s in range(2):
                pool.wait_ge(scattered[s], 16 * K * (NT // 2))


def experts(nc, keep, table_dram, h_dram, w12, y_dram):
    with ExitStack() as ctx:
        def sb(name, shape, dt=F32):
            return ctx.enter_context(nc.sbuf_tensor("ex_" + name, shape, dt))

        def ps(name, shape):
            return ctx.enter_context(nc.psum_tensor("ex_" + name, shape, F32))

        def sem(name):
            return ctx.enter_context(nc.semaphore("ex_" + name))

        def sems(name, n=2):
            return [sem(f"{name}{s}") for s in range(n)]

        FC = I // P
        N = SLOT_TILES
        LEFT = N - P
        W1 = DC * 2 * I
        W12 = W1 + FC * D
        AHEAD = 4
        ident = sb("ident", [P, P])
        table = sb("table", [P, P])
        table_rest = sb("table_rest", [LEFT, P])
        token = sb("token", [P, N], U32)
        scratch = sb("scratch", [P, 1 + 2 * AHEAD])
        token_now = sb("token_now", [P, AHEAD, 1], U32)
        w_raw = sb("w_raw", [P, 2, W12])
        w_hi = sb("w_hi", [P, 2, W12], F32R)
        w_lo = sb("w_lo", [P, 2, W12], F32R)
        rows = sb("rows", [P, AHEAD, D])
        rowsT_hi = sb("rowsT_hi", [P, 2, DC, P], F32R)
        rowsT_lo = sb("rowsT_lo", [P, 2, DC, P], F32R)
        silu = sb("silu", [P, 2, I])
        inner = sb("inner", [P, 2, I])
        innerT_hi = sb("innerT_hi", [P, 2, FC, P], F32R)
        innerT_lo = sb("innerT_lo", [P, 2, FC, P], F32R)
        y = sb("y", [P, 2, D])
        turn = ps("turn", [P, 2, DC, P])
        gate_up = ps("gate_up", [P, 2, 2 * I])
        inner_turn = ps("inner_turn", [P, 2, BANK])
        y_ps = ps("y_ps", [P, 2, D])

        made, table_loaded, table_turned, token_ready = (
            sem("made"), sem("table_loaded"), sem("table_turned"), sem("token_ready"))
        w_loaded, w_hi_done, w_lo_done = sem("w_loaded"), sem("w_hi_done"), sem("w_lo_done")
        copied, gathered, turned = sems("copied", AHEAD), sems("gathered", AHEAD), sems("turned", AHEAD)
        rowsT_hi_done, rowsT_lo_done, gu_filled, silu_done, inner_done = (
            sems("rowsT_hi"), sems("rowsT_lo"), sems("gu_filled"), sems("silu_done"), sems("inner_done"))
        inner_turned, innerT_hi_done, innerT_lo_done, y_filled, y_done, y_stored = (
            sems("inner_turned"), sems("innerT_hi"), sems("innerT_lo"), sems("y_filled"), sems("y_done"),
            sems("y_stored"))
        block = ctx.enter_context(nc.Block())

        def tile_at(i, o):
            return 4 * i + o, o % 2, 2 * i + o // 2, o % AHEAD, i + o // AHEAD

        def steps(eng, step):
            step(*[tile_at(0, 0 + d) if 0 + d >= 0 else None for d in (-2, -1, 0, 1)])
            step(*[tile_at(0, 1 + d) if 1 + d >= 0 else None for d in (-2, -1, 0, 1)])
            with eng.Fori(0, N // 4 - 1) as i:
                for j in range(4):
                    step(*[tile_at(i, 2 + j + d) for d in (-2, -1, 0, 1)])
            for n in range(N - 2, N + 2):
                step(*[tile_at(0, n + d) if n + d < N else None for d in (-2, -1, 0, 1)])

        @block.sync
        def _(sp):
            tiles = table_dram.rearrange("(j s) o -> j (s o)", s=P)
            sp.dma_start(table[:], tiles[0:P, :]).then_inc(table_loaded, 16)
            sp.dma_start(table_rest[:], tiles[P:N, :]).then_inc(table_loaded, 16)
            with sp.Fori(0, E // 2) as g:
                for s in range(2):
                    sp.wait_ge(w_loaded, (2 * g + s) * 16)
                    sp.wait_ge(w_lo_done, 2 * g)
                    sp.dma_start(w_raw[:, s, :], w12[bass.ds(2 * g + s, 1)].rearrange("o p n -> p (o n)")) \
                      .then_inc(w_loaded, 16)

        @block.gpsimd
        def _(pool):
            nc.gpsimd.memset(ident[:], 0.0).then_inc(made, 1)
            nc.gpsimd.memset(scratch[:], 0.0).then_inc(made, 1)
            pool.wait_ge(made, 2)
            nc.gpsimd.affine_select(out=ident[:], in_=ident[:], compare_op=ALU.not_equal, fill=1.0, base=0,
                                    pattern=[[-1, P]], channel_multiplier=1).then_inc(made, 1)
            pool.wait_ge(token_ready, 2)
            with pool.Fori(0, N // AHEAD) as m:
                for q in range(AHEAD):
                    wait_apart(pool, scratch, 1 + q, gathered[q], 16 * m)
                    nc.gpsimd.tensor_copy(token_now[:, q, :], token[:, bass.ds(AHEAD * m + q, 1)]) \
                        .then_inc(copied[q], 1)
                    pool.wait_ge(turned[q], m)
                    wait_apart(pool, scratch, 1 + AHEAD + q, copied[q], m + 1)
                    nc.gpsimd.indirect_dma_start(
                        rows[:, q, :], None, h_dram,
                        bass.IndirectOffsetOnAxis(ap=token_now[:, q, :], axis=0)).then_inc(gathered[q], 16)

        @block.scalar
        def _(act):
            act.wait_ge(w_loaded, 16)
            nc.scalar.activation(w_hi[:, 0, :], w_raw[:, 0, :], ACT.Copy).then_inc(w_hi_done, 1)

            def turned_rows_hi(tile):
                n, s, h, q, m = tile
                act.wait_ge(turned[q], m + 1)
                act.wait_ge(gu_filled[s], h)
                nc.scalar.activation(rowsT_hi[:, s], turn[:, s], ACT.Copy).then_inc(rowsT_hi_done[s], 1)

            def step(stored, finished, now, coming):
                if finished:
                    n, s, h, _, _ = finished
                    act.wait_ge(inner_turned[s], h + 1)
                    act.wait_ge(y_filled[s], h)
                    nc.scalar.activation(innerT_hi[:, s].rearrange("p c n -> p (c n)"), inner_turn[:, s, 0:I],
                                         ACT.Copy).then_inc(innerT_hi_done[s], 1)
                if now:
                    n, s, h, _, _ = now
                    act.wait_ge(gu_filled[s], h + 1)
                    act.wait_ge(inner_done[s], h)
                    nc.scalar.activation(silu[:, s, :], gate_up[:, s, 0:I], ACT.Silu).then_inc(silu_done[s], 1)
                if coming:
                    turned_rows_hi(coming)
                if stored:
                    n, s, h, _, _ = stored
                    act.wait_ge(y_done[s], h + 1)
                    act.dma_start(y_dram[bass.ds(n, 1)].rearrange("o p d -> (o p) d"), y[:, s, :]) \
                       .then_inc(y_stored[s], 16)
                if now:
                    n = now[0]
                    e = act.value_load(keep.next_weights[0:1, bass.ds(n, 1)], min_val=0, max_val=E - 1)
                    with act.If(e > 0):
                        if finished:
                            act.wait_ge(y_filled[finished[1]], finished[2] + 1)
                        act.wait_ge(w_loaded, e * 16 + 16)
                        slot = bass.ds(e % 2, 1)
                        nc.scalar.activation(w_hi[:, slot, :], w_raw[:, slot, :], ACT.Copy).then_inc(w_hi_done, 1)

            turned_rows_hi(tile_at(0, 0))
            steps(act, step)
            for s in range(2):
                act.wait_ge(y_stored[s], 16 * (N // 2))

        @block.vector
        def _(dve):
            dve.wait_ge(w_hi_done, 1)
            nc.vector.tensor_tensor(w_lo[:, 0, :], w_raw[:, 0, :], w_hi[:, 0, :], ALU.subtract) \
                .then_inc(w_lo_done, 1)
            dve.wait_ge(table_turned, 1)
            nc.vector.tensor_copy(token[:, 0:P], turn[:, 0, 0, :]).then_inc(token_ready, 1)
            nc.vector.tensor_copy(token[:, P:N], turn[:, 0, 1, 0:LEFT]).then_inc(token_ready, 1)

            def turned_rows_lo(tile):
                n, s, h, _, _ = tile
                dve.wait_ge(rowsT_hi_done[s], h + 1)
                nc.vector.tensor_tensor(rowsT_lo[:, s], turn[:, s], rowsT_hi[:, s], ALU.subtract) \
                    .then_inc(rowsT_lo_done[s], 1)

            def step(stored, finished, now, coming):
                if finished:
                    n, s, h, _, _ = finished
                    dve.wait_ge(innerT_hi_done[s], h + 1)
                    nc.vector.tensor_tensor(innerT_lo[:, s].rearrange("p c n -> p (c n)"), inner_turn[:, s, 0:I],
                                            innerT_hi[:, s].rearrange("p c n -> p (c n)"), ALU.subtract) \
                        .then_inc(innerT_lo_done[s], 1)
                if now:
                    n, s, h, _, _ = now
                    dve.wait_ge(silu_done[s], h + 1)
                    dve.wait_ge(inner_turned[s], h)
                    nc.vector.tensor_tensor(inner[:, s, :], gate_up[:, s, I:2 * I], silu[:, s, :], ALU.mult) \
                        .then_inc(inner_done[s], 1)
                if coming:
                    turned_rows_lo(coming)
                if finished:
                    n, s, h, _, _ = finished
                    dve.wait_ge(y_filled[s], h + 1)
                    dve.wait_ge(y_stored[s], 16 * h)
                    nc.vector.tensor_copy(y[:, s, :], y_ps[:, s, :]).then_inc(y_done[s], 1)
                if now:
                    n = now[0]
                    e = dve.value_load(keep.next_weights[0:1, bass.ds(n, 1)], min_val=0, max_val=E - 1)
                    with dve.If(e > 0):
                        dve.wait_ge(w_hi_done, e + 1)
                        slot = bass.ds(e % 2, 1)
                        nc.vector.tensor_tensor(w_lo[:, slot, :], w_raw[:, slot, :], w_hi[:, slot, :],
                                                ALU.subtract).then_inc(w_lo_done, 1)

            turned_rows_lo(tile_at(0, 0))
            steps(dve, step)

        @block.tensor
        def _(pe):
            pe.wait_ge(made, 3)
            pe.wait_ge(table_loaded, 32)
            nc.tensor.transpose(turn[:, 0, 0, :], table[:], ident[:])
            nc.tensor.transpose(turn[:, 0, 1, 0:LEFT], table_rest[:], ident[0:LEFT, 0:LEFT]) \
                .then_inc(table_turned, 1)
            pe.wait_ge(token_ready, 2)

            def turn_rows(tile):
                n, s, h, q, m = tile
                pe.wait_ge(gathered[q], 16 * m + 16)
                pe.wait_ge(rowsT_lo_done[s], h)
                for c in range(DC):
                    last = nc.tensor.transpose(turn[:, s, c, :], rows[:, q, c * P:(c + 1) * P], ident[:])
                last.then_inc(turned[q], 1)

            def weights(x, slot, column):
                return x[:, slot, column:column + BANK].rearrange("p o n -> p (o n)")

            def step(stored, finished, now, coming):
                if finished:
                    n, s, h, _, _ = finished
                    pe.wait_ge(inner_done[s], h + 1)
                    pe.wait_ge(innerT_lo_done[s], h)
                    for c in range(FC):
                        last = nc.tensor.transpose(inner_turn[:, s, c * P:(c + 1) * P],
                                                   inner[:, s, c * P:(c + 1) * P], ident[:])
                    last.then_inc(inner_turned[s], 1)
                if now:
                    n, s, h, _, _ = now
                    e = pe.value_load(keep.owner[0:1, bass.ds(n, 1)], min_val=0, max_val=E - 1)
                    pe.wait_ge(rowsT_lo_done[s], h + 1)
                    pe.wait_ge(inner_done[s], h)
                    pe.wait_ge(w_lo_done, e + 1)
                    slot = bass.ds(pe.snap(e % 2), 1)
                    for c in range(DC):
                        mm3(nc.tensor, gate_up[:, s, :], (rowsT_hi[:, s, c, :], rowsT_lo[:, s, c, :]),
                            (weights(w_hi, slot, c * BANK), weights(w_lo, slot, c * BANK)),
                            start=c == 0, stop=c == DC - 1, signal=gu_filled[s] if c == DC - 1 else None)
                if coming:
                    turn_rows(coming)
                if finished:
                    n, s, h, _, _ = finished
                    e = pe.value_load(keep.owner[0:1, bass.ds(n, 1)], min_val=0, max_val=E - 1)
                    slot = bass.ds(pe.snap(e % 2), 1)
                    pe.wait_ge(innerT_lo_done[s], h + 1)
                    pe.wait_ge(y_done[s], h)
                    for c in range(FC):
                        mm3(nc.tensor, y_ps[:, s, :], (innerT_hi[:, s, c, :], innerT_lo[:, s, c, :]),
                            (weights(w_hi, slot, W1 + c * BANK), weights(w_lo, slot, W1 + c * BANK)),
                            start=c == 0, stop=c == FC - 1, signal=y_filled[s] if c == FC - 1 else None)

            turn_rows(tile_at(0, 0))
            steps(pe, step)


def combine(nc, keep, y_dram, base_dram, out):
    with ExitStack() as ctx:
        def sb(name, shape, dt=F32):
            return ctx.enter_context(nc.sbuf_tensor("co_" + name, shape, dt))

        def sems(name):
            return [ctx.enter_context(nc.semaphore(f"co_{name}{s}")) for s in range(2)]

        started = ctx.enter_context(nc.semaphore("co_started"))
        scratch = sb("scratch", [P, 5])
        slot_now = sb("slot_now", [P, 2, K], U32)
        rows = sb("rows", [P, 2, K, D])
        total = sb("total", [P, 2, D])
        base_loaded, copied, gathered, added, stored = (
            sems("base_loaded"), sems("copied"), sems("gathered"), sems("added"), sems("stored"))
        block = ctx.enter_context(nc.Block())

        @block.sync
        def _(sp):
            with sp.Fori(0, NT // 2) as m:
                for s in range(2):
                    sp.wait_ge(stored[s], 16 * m)
                    sp.dma_start(total[:, s, :], base_dram[bass.ds(2 * m + s, 1)].rearrange("o p d -> (o p) d")) \
                      .then_inc(base_loaded[s], 16)

        @block.gpsimd
        def _(pool):
            nc.gpsimd.memset(scratch[:], 0.0).then_inc(started, 1)
            pool.wait_ge(started, 1)
            with pool.Fori(0, NT // 2) as m:
                for s in range(2):
                    wait_apart(pool, scratch, 1 + s, gathered[s], 16 * K * m)
                    nc.gpsimd.tensor_copy(slot_now[:, s, :], keep.slots[:, bass.ds((2 * m + s) * K, K)]) \
                        .then_inc(copied[s], 1)
                    pool.wait_ge(added[s], K * m)
                    wait_apart(pool, scratch, 3 + s, copied[s], m + 1)
                    for k in range(K):
                        nc.gpsimd.indirect_dma_start(
                            rows[:, s, k, :], None, y_dram,
                            bass.IndirectOffsetOnAxis(ap=slot_now[:, s, k:k + 1], axis=0)).then_inc(gathered[s], 16)

        @block.vector
        def _(dve):
            with dve.Fori(0, NT // 2) as m:
                for s in range(2):
                    dve.wait_ge(base_loaded[s], 16 * m + 16)
                    dve.wait_ge(gathered[s], 16 * K * m + 16 * K)
                    for k in range(K):
                        w = keep.top_w[:, bass.ds((2 * m + s) * K + k, 1)]
                        nc.vector.scalar_tensor_tensor(out=total[:, s, :], in0=rows[:, s, k, :], scalar=w,
                                                       in1=total[:, s, :], op0=ALU.mult, op1=ALU.add) \
                            .then_inc(added[s], 1)
                        dve.wait_ge(added[s], K * m + k + 1)

        @block.scalar
        def _(act):
            with act.Fori(0, NT // 2) as m:
                for s in range(2):
                    act.wait_ge(added[s], K * m + K)
                    act.dma_start(out[bass.ds(2 * m + s, 1)].rearrange("o p d -> (o p) d"), total[:, s, :]) \
                       .then_inc(stored[s], 16)
            for s in range(2):
                act.wait_ge(stored[s], 16 * (NT // 2))


class Routing:

    def __init__(self, sb):
        self.count = sb("count", [P, E])
        self.rank = sb("rank", [P, NT, E])
        self.hot = sb("hot", [P, NT * K, E], BF16)
        self.top_w = sb("top_w", [P, NT * K])
        self.slots = sb("slots", [P, NT * K], U32)
        self.owner = sb("owner", [P, SLOT_TILES], mybir.dt.int32)
        self.next_weights = sb("next_weights", [P, SLOT_TILES], mybir.dt.int32)


def feed_forward(nc, x2_dram, norm_rows, router_w, shared_w, w12, out, dram):
    h_dram, base_dram, table_dram, y_dram = (
        dram("h", [T, D]), dram("base", [T, D]), dram("table", [SLOTS, 1]), dram("y", [SLOTS, D]))
    with ExitStack() as ctx:
        def sb(name, shape, dt=F32):
            return ctx.enter_context(nc.sbuf_tensor("keep_" + name, shape, dt))

        keep = Routing(sb)
        grouped = lambda a: a.rearrange("(g n) d -> g n d", n=BANK)
        tiled = lambda a: a.rearrange("(n p) d -> n p d", p=P)
        ffn_tokens(nc, keep, grouped(x2_dram), norm_rows, router_w, shared_w, grouped(h_dram), grouped(base_dram))
        dispatch(nc, keep, table_dram)
        experts(nc, keep, table_dram, h_dram, w12, tiled(y_dram))
        combine(nc, keep, y_dram, tiled(base_dram), tiled(out))


def build_program(nc, x, attn_w, w_kv_down, q_norm_rows, k_norm_col, cos, sin, norm_rows, router_w, shared_w,
                  w12, out):
    def dram(name, shape):
        return nc.dram_tensor("scratch_" + name, tuple(shape), F32, kind="Internal").ap()

    w_hi_dram, w_lo_dram = dram("w_hi", [PAIRS, P, WQK + WO]), dram("w_lo", [PAIRS, P, WQK + WO])
    x2_dram = dram("x2", [T, D])
    prepare_weights(nc, attn_w, w_hi_dram, w_lo_dram)
    attention(nc, x, w_kv_down, q_norm_rows, k_norm_col, cos, sin, w_hi_dram, w_lo_dram,
              x2_dram.rearrange("(b s) d -> b s d", b=B))
    feed_forward(nc, x2_dram, norm_rows, router_w, shared_w, w12,
                 out.rearrange("b s d -> (b s) d"), dram)


def kernel(**inputs):
    import concourse.bacc as bacc
    from concourse.bass_utils import run_bass_kernel_spmd

    a = {name.removeprefix("L0_"): np.asarray(value) for name, value in inputs.items()}
    dense = np.ascontiguousarray
    wq = a["attn_wq"].reshape(DC, P, PAIRS, 2 * DK).transpose(2, 1, 0, 3).reshape(PAIRS, P, DC * 2 * DK)
    wk = np.concatenate([a["attn_w_k_rope"].reshape(DL, H, DR), a["attn_w_k_nope"].reshape(DL, H, DK - DR)], 2)
    wk = wk.reshape(DL, PAIRS, 2 * DK).transpose(1, 0, 2)
    wv = a["attn_wv"].reshape(DL, H, DK).transpose(2, 1, 0).reshape(DK, PAIRS, 2 * DL).transpose(1, 0, 2)
    wo = a["attn_wo"].reshape(PAIRS, 2, DK, D).transpose(0, 2, 1, 3).reshape(PAIRS, DK, 2 * D)
    freq = np.float32(1.0 / 10000.0) ** np.linspace(0.0, 1.0, RQ, dtype=np.float32)
    theta = np.arange(S, dtype=np.float32)[:, None] * freq[None, :]
    shared = np.stack([a["ffn_sg"], a["ffn_su"], a["ffn_sd"]])
    w1 = a["ffn_w1"].reshape(E, DC, P, 2 * I).transpose(0, 2, 1, 3).reshape(E, P, DC * 2 * I)
    w2 = a["ffn_w2"].reshape(E, I // P, P, D).transpose(0, 2, 1, 3).reshape(E, P, I // P * D)
    arrays = {
        "x": dense(a["attn_x"]),
        "attn_w": dense(np.concatenate([wq, wk, wv, wo], 2)),
        "w_kv_down": dense(a["attn_w_kv_down"].reshape(DC, P, DL).transpose(1, 0, 2)),
        "q_norm_rows": dense(np.broadcast_to(a["attn_q_norm_w"], (P, DK))),
        "k_norm_col": dense(a["attn_k_norm_w"].reshape(DK, 1)),
        "cos": dense(np.cos(theta).reshape(TB, P, RQ).transpose(1, 0, 2)),
        "sin": dense(np.sin(theta).reshape(TB, P, RQ).transpose(1, 0, 2)),
        "norm_rows": dense(np.broadcast_to(a["ffn_norm_w"], (P, D))),
        "router_w": dense(a["ffn_router_w"].T.reshape(DC, P, E).transpose(1, 0, 2)),
        "shared_w": dense(shared.reshape(3, DC, P, SH).transpose(2, 0, 1, 3).reshape(P, 3 * DC * SH)),
        "w12": dense(np.concatenate([w1, w2], 2)),
    }
    nc = bacc.Bacc("TRN2", target_bir_lowering=False, num_devices=1)
    args = {name: nc.dram_tensor("in_" + name, value.shape, mybir.dt.from_np(value.dtype),
                                 kind="ExternalInput").ap() for name, value in arrays.items()}
    out = nc.dram_tensor("out_0", (B, S, D), F32, kind="ExternalOutput").ap()
    build_program(nc, out=out, **args)
    result = run_bass_kernel_spmd(nc, [{"in_" + name: value for name, value in arrays.items()}], core_ids=[0])
    return result.results[0]["out_0"]
```

```python
from contextlib import ExitStack

import concourse.bass as bass
from concourse import mybir
import numpy as np

ALU = mybir.AluOpType
ACT = mybir.ActivationFunctionType
AXIS_X = mybir.AxisListType.X
F32 = mybir.dt.float32
F32R = mybir.dt.float32r
BF16 = mybir.dt.bfloat16
U32 = mybir.dt.uint32

P = 128
B, S, D = 4, 1024, 512
H, DK, DL, DR = 16, 128, 128, 64
T = B * S
E, I, K = 32, 256, 4
SH = 512
BANK = 512
DC = D // P
TB = S // P
NT = T // P
PAIRS = H // 2
GT = BANK // P
RQ = DR // 4
LN_EPS, ATT_EPS, FFN_EPS = 1e-5, 1e-6, 1e-6
MASKED = -1e30
SLOT_TILES = T * K // P + E
SLOTS = SLOT_TILES * P
WQK = DC * 2 * DK + 2 * DK
WV = 2 * DL
WO = 2 * D


def mm3(pe, out, lhs, rhs, start=True, stop=True, signal=None):
    (a, a_rest), (b, b_rest) = lhs, rhs
    pe.matmul(out, a, b, start=start, stop=False)
    pe.matmul(out, a, b_rest, start=False, stop=False)
    last = pe.matmul(out, a_rest, b, start=False, stop=stop)
    if signal is not None:
        last.then_inc(signal, 1)


def wait_apart(eng, scratch, column, sem, value):
    eng.wait_ge(sem, value)
    eng.tensor_tensor(scratch[:, column:column + 1], scratch[:, 0:1], scratch[:, 0:1], ALU.add)


def prepare_weights(nc, attn_w, w_hi_dram, w_lo_dram):
    WIDE = WQK + WV + WO
    with ExitStack() as ctx:
        def sb(name, shape, dt):
            return ctx.enter_context(nc.sbuf_tensor(name, shape, dt))

        def sem(name):
            return ctx.enter_context(nc.semaphore(name))

        raw = sb("pw_raw", [P, 2, WIDE], F32)
        hi = sb("pw_hi", [P, 2, WIDE], F32R)
        lo = sb("pw_lo", [P, 2, WIDE], F32R)
        vo_hi = sb("pw_vo_hi", [P, 2, 2, D], F32R)
        vo_lo = sb("pw_vo_lo", [P, 2, 2, D], F32R)
        vo_ps = ctx.enter_context(nc.psum_tensor("pw_vo_ps", [P, 2, 2, BANK], F32))
        loaded = [sem("pw_loaded0"), sem("pw_loaded1")]
        hi_done, lo_done = sem("pw_hi_done"), [sem("pw_lo_done0"), sem("pw_lo_done1")]
        vo_filled, vo_hi_done, vo_lo_done = sem("pw_vo_filled"), sem("pw_vo_hi_done"), sem("pw_vo_lo_done")
        stored = [sem("pw_stored0"), sem("pw_stored1")]
        STORES = 4 * 16

        def wv_of(x, s, h):
            return x[:, s, WQK + h * DL:WQK + (h + 1) * DL]

        def wo_of(x, s, h):
            return x[:, s, WQK + WV + h * D:WQK + WV + (h + 1) * D]

        block = ctx.enter_context(nc.Block())

        @block.sync
        def _(sp):
            with sp.Fori(0, PAIRS // 2) as g:
                for s in range(2):
                    sp.wait_ge(lo_done[s], g)
                    sp.dma_start(raw[:, s, :], attn_w[bass.ds(2 * g + s, 1)].rearrange("o p n -> (o p) n")) \
                      .then_inc(loaded[s], 16)

        @block.scalar
        def _(act):
            with act.Fori(0, PAIRS // 2) as g:
                for s in range(2):
                    act.wait_ge(loaded[s], 16 * g + 16)
                    act.wait_ge(stored[s], STORES * g)
                    nc.scalar.activation(hi[:, s, :], raw[:, s, :], ACT.Copy).then_inc(hi_done, 1)
                    act.wait_ge(vo_filled, 2 * g + s + 1)
                    nc.scalar.activation(vo_hi[:, s], vo_ps[:, s], ACT.Copy).then_inc(vo_hi_done, 1)

        @block.vector
        def _(dve):
            with dve.Fori(0, PAIRS // 2) as g:
                for s in range(2):
                    dve.wait_ge(hi_done, 2 * g + s + 1)
                    nc.vector.tensor_tensor(lo[:, s, :], raw[:, s, :], hi[:, s, :], ALU.subtract) \
                      .then_inc(lo_done[s], 1)
                    dve.wait_ge(vo_hi_done, 2 * g + s + 1)
                    nc.vector.tensor_tensor(vo_lo[:, s], vo_ps[:, s], vo_hi[:, s], ALU.subtract) \
                      .then_inc(vo_lo_done, 1)

        @block.tensor
        def _(pe):
            with pe.Fori(0, PAIRS // 2) as g:
                for s in range(2):
                    pe.wait_ge(lo_done[s], g + 1)
                    pe.wait_ge(vo_lo_done, 2 * g)
                    for h in range(2):
                        mm3(nc.tensor, vo_ps[:, s, h, :], (wv_of(hi, s, h), wv_of(lo, s, h)),
                            (wo_of(hi, s, h), wo_of(lo, s, h)), signal=vo_filled if h == 1 else None)

        @block.gpsimd
        def _(pool):
            with pool.Fori(0, PAIRS // 2) as g:
                for s in range(2):
                    pool.wait_ge(lo_done[s], g + 1)
                    for src, dst in ((hi, w_hi_dram), (lo, w_lo_dram)):
                        pool.dma_start(dst[bass.ds(2 * g + s, 1), :, 0:WQK].rearrange("o p n -> (o p) n"),
                                       src[:, s, 0:WQK].bitcast(F32)).then_inc(stored[s], 16)
                    pool.wait_ge(vo_lo_done, 2 * g + s + 1)
                    for src, dst in ((vo_hi, w_hi_dram), (vo_lo, w_lo_dram)):
                        pool.dma_start(dst[bass.ds(2 * g + s, 1), :, WQK:WQK + WO].rearrange("o p n -> (o p) n"),
                                       src[:, s].rearrange("p h n -> p (h n)").bitcast(F32)) \
                            .then_inc(stored[s], 16)
            for s in range(2):
                pool.wait_ge(stored[s], STORES * (PAIRS // 2))


def attention(nc, x, w_kv_down, q_norm_rows, k_norm_col, cos, sin, w_hi_dram, w_lo_dram, x2_dram):
    STEPS = 2 * TB
    GQ = 2
    GROUPS = STEPS // GQ
    LAST_STEP = STEPS + 6
    LAST_HEAD = TB + 2

    def step_of(u):
        group = u // GQ
        return group // 2, group % 2, GQ * (group // 2) + u % GQ

    pv_steps = [GQ * n + GQ + 2 for n in range(GROUPS)]

    SPLIT_LAG = 1

    def out_tiles_at(u):
        n = u - pv_steps[1] - 3
        return [GQ * (n // 4) + n % 4] if 0 <= n and n % 4 < GQ else []

    def chunks(t):
        return [range(a, min(a + GT, t + 1)) for a in range(0, t + 1, GT)]

    AHEAD = 7

    def plan(first_head, with_next):
        steps = [("head", i, 0) for i in range(first_head, TB)]
        for u in range(LAST_STEP + 1):
            if TB + u <= LAST_HEAD:
                steps.append(("head", TB + u, 0))
            if with_next and u >= STEPS:
                steps.append(("head", u - STEPS, 1))
            steps.append(("softmax", u, 0))
        return steps

    ring = [("qk", i) for i in range(TB)]
    turns = {("qkT", i): i for i in range(TB)}
    for u in range(STEPS + 2):
        if u < STEPS:
            ring.append(("scores", u))
        if 2 <= u < STEPS + 2:
            for c in range(len(chunks(step_of(u - 2)[2]))):
                turns["probsT", u - 2, c] = len(turns)
    RING, TURNS = len(ring), len(turns)
    LN_RING, LN_TURNS = 2 + 2, TB
    assert RING % 2 == 0 and TURNS % 2 == 0

    with ExitStack() as ctx:
        def sb(name, shape, dt):
            return ctx.enter_context(nc.sbuf_tensor(name, shape, dt))

        def ps(name, shape):
            return ctx.enter_context(nc.psum_tensor(name, shape, F32))

        def sem(name):
            return ctx.enter_context(nc.semaphore(name))

        ident = sb("at_ident", [P, P], F32)
        ident_b = sb("at_ident_b", [P, P], BF16)
        mask_b = sb("at_mask_b", [P, P], BF16)
        minus_half = sb("at_minus_half", [P, TB], F32)
        scratch = sb("at_scratch", [P, 2], F32)
        ln_eps = sb("at_ln_eps", [P, TB], F32)
        att_eps = sb("at_att_eps", [P, 4], F32)
        cos_t = sb("at_cos", [P, TB, RQ], F32)
        sin_t = sb("at_sin", [P, TB, RQ], F32)
        q_norm = sb("at_q_norm", [P, DK], F32)
        k_norm = sb("at_k_norm", [P, 1], F32)
        k_scale = sb("at_k_scale", [P, 1], F32)
        down_raw = sb("at_down_raw", [P, DC, DL], F32)
        down_hi = sb("at_down_hi", [P, DC, DL], F32R)
        down_lo = sb("at_down_lo", [P, DC, DL], F32R)

        x_in = sb("at_x_in", [P, TB, D], F32)
        acc = sb("at_acc", [P, TB, D], F32)
        stats = sb("at_stats", [P, TB, 6], F32)
        mean_var = sb("at_mean_var", [P, TB, 2], F32)
        ln_var = sb("at_ln_var", [P, TB], F32)
        ln_rstd = sb("at_ln_rstd", [P, TB], F32)
        xn = sb("at_xn", [P, 2, D], F32)
        xT_hi = sb("at_xT_hi", [P, DC, S], F32R)
        xT_lo = sb("at_xT_lo", [P, DC, S], F32R)
        latT_hi = sb("at_latT_hi", [P, S], F32R)
        latT_lo = sb("at_latT_lo", [P, S], F32R)
        lat_hi = sb("at_lat_hi", [P, TB, DL], F32R)
        lat_lo = sb("at_lat_lo", [P, TB, DL], F32R)

        wqk_hi = sb("at_wqk_hi", [P, WQK], F32R)
        wqk_lo = sb("at_wqk_lo", [P, WQK], F32R)
        wvo_hi = sb("at_wvo_hi", [P, 2, D], F32R)
        wvo_lo = sb("at_wvo_lo", [P, 2, D], F32R)

        squares = sb("at_squares", [P, 4, DK], F32)
        sums = sb("at_sums", [P, TB, 4], F32)
        sums_eps = sb("at_sums_eps", [P, TB, 4], F32)
        rstd = sb("at_rstd", [P, TB, 4], F32)
        qk = sb("at_qk", [P, 4, 4, DK], F32)
        turned = sb("at_turned", [P, 2, 4, 2, RQ], F32)
        qkT_hi = sb("at_qkT_hi", [P, 4, S], F32R)
        qkT_lo = sb("at_qkT_lo", [P, 4, S], F32R)

        row_max = sb("at_row_max", [P, 2], F32)
        shift = sb("at_shift", [P, 2], F32)
        row_sum = sb("at_row_sum", [P, 2], F32)
        row_inv = sb("at_row_inv", [P, 2], F32)
        probs = sb("at_probs", [P, 3, S], F32)
        pT_hi = sb("at_pT_hi", [P, 2, TB, GQ * P], F32R)
        pT_lo = sb("at_pT_lo", [P, 2, TB, GQ * P], F32R)
        oT_hi = sb("at_oT_hi", [P, 4, GQ * P], F32R)
        oT_lo = sb("at_oT_lo", [P, 4, GQ * P], F32R)

        slot = ps("at_slot", [P, 2, 2 * BANK])
        turn = ps("at_turn", [P, 2, 4, P])
        pv = ps("at_pv", [P, GQ * P])
        out_ps = ps("at_out_ps", [P, BANK])

        consts_loaded, consts_made = sem("at_consts_loaded"), sem("at_consts_made")
        down_hi_done, down_lo_done, k_scaled = sem("at_down_hi"), sem("at_down_lo"), sem("at_k_scaled")
        x_loaded, x_copied, x2_stored = sem("at_x_loaded"), sem("at_x_copied"), sem("at_x2_stored")
        ln_stats, ln_aggr, ln_var_added, ln_rstd_ready, xn_ready = (
            sem("at_ln_stats"), sem("at_ln_aggr"), sem("at_ln_var_added"), sem("at_ln_rstd"), sem("at_xn_ready"))
        wqk_loaded, wvo_loaded = sem("at_wqk_loaded"), sem("at_wvo_loaded")
        slot_filled = sem("at_slot_filled")
        turn_filled = sem("at_turn_filled")
        out_filled = sem("at_out_filled")
        turn_hi, turn_lo = sem("at_turn_hi"), sem("at_turn_lo")
        lat_hi_done, lat_lo_done, lat_copied = (
            sem("at_lat_hi_done"), sem("at_lat_lo_done"), sem("at_lat_copied"))
        summed, eps_added, rstd_ready = sem("at_summed"), sem("at_eps_added"), sem("at_rstd_ready")
        q_scaled, kr_scaled, rope_parts, rope_done = (
            sem("at_q_scaled"), sem("at_kr_scaled"), sem("at_rope_parts"), sem("at_rope_done"))
        max_ready, shift_ready, exp_done, inv_ready, probs_ready = (
            sem("at_max"), sem("at_shift_ready"), sem("at_exp"), sem("at_inv"), sem("at_probs_ready"))
        pv_filled, oT_hi_done, oT_lo_done = sem("at_pv_filled"), sem("at_oT_hi_done"), sem("at_oT_lo_done")
        out_added = sem("at_out_added")

        def batch_ring(b):
            return b * (LN_RING + PAIRS * RING)

        def round_ring(b, p):
            return batch_ring(b) + LN_RING + p * RING

        def batch_turns(b):
            return b * (LN_TURNS + PAIRS * TURNS)

        def round_turns(b, p):
            return batch_turns(b) + LN_TURNS + p * TURNS

        def rounds(eng, b, step):
            def one_pass(p, first_head, with_next):
                for kind, n, ahead in plan(first_head, with_next):
                    step(kind, n, b * PAIRS + p + ahead, round_ring(b, p + ahead), round_turns(b, p + ahead))

            for i in range(AHEAD):
                step("head", i, b * PAIRS, round_ring(b, 0), round_turns(b, 0))
            with eng.Fori(0, PAIRS - 1) as p:
                one_pass(p, AHEAD, True)
            one_pass(PAIRS - 1, AHEAD, False)

        def use(kind, n):
            return ring.index((kind, n))

        def banks(kind, n):
            at = use(kind, n)
            if at < 2 * TB:
                return slot[:, at // 2 % 2, at % 2 * BANK:(at % 2 + 1) * BANK]
            return slot[:, n % 2, :]

        def wqk(x, c):
            return x[:, c * 2 * DK:(c + 1) * 2 * DK]

        block = ctx.enter_context(nc.Block())

        @block.sync
        def _(sp):
            sp.dma_start(cos_t[:], cos).then_inc(consts_loaded, 16)
            sp.dma_start(sin_t[:], sin).then_inc(consts_loaded, 16)
            sp.dma_start(q_norm[:], q_norm_rows).then_inc(consts_loaded, 16)
            sp.dma_start(k_norm[:], k_norm_col).then_inc(consts_loaded, 16)
            sp.dma_start(down_raw[:], w_kv_down).then_inc(consts_loaded, 16)
            def load_x(b):
                x_rows = x[bass.ds(b, 1)].rearrange("o (t p) d -> p (o t) d", p=P)
                sp.wait_ge(x_copied, b)
                sp.dma_start(x_in[:], x_rows) \
                  .then_inc(x_loaded, 16)

            def batch(b, with_next):
                with sp.Fori(0, PAIRS) as p:
                    r = b * PAIRS + p
                    sp.wait_ge(kr_scaled, r * TB)
                    for dst, src in ((wqk_hi, w_hi_dram), (wqk_lo, w_lo_dram)):
                        sp.dma_start(dst[:].bitcast(F32), src[bass.ds(p, 1), :, 0:WQK]
                                     .rearrange("o p n -> (o p) n")).then_inc(wqk_loaded, 16)
                    sp.wait_ge(out_added, r * TB)
                    for dst, src in ((wvo_hi, w_hi_dram), (wvo_lo, w_lo_dram)):
                        sp.dma_start(dst[:].rearrange("p h n -> p (h n)").bitcast(F32),
                                     src[bass.ds(p, 1), :, WQK:WQK + WO]
                                     .rearrange("o p n -> (o p) n")).then_inc(wvo_loaded, 16)
                if with_next:
                    load_x(sp.snap(b + 1))
                sp.wait_ge(out_added, (b + 1) * (PAIRS * TB))
                sp.dma_start(x2_dram[bass.ds(b, 1)].rearrange("o (t p) d -> p (o t) d", p=P), acc[:]) \
                  .then_inc(x2_stored, 16)

            load_x(0)
            if B > 1:
                with sp.Fori(0, B - 1) as b:
                    batch(b, True)
            batch(B - 1, False)
            sp.wait_ge(x2_stored, 16 * B)

        @block.gpsimd
        def _(pool):
            nc.gpsimd.memset(ident[:], 0.0).then_inc(consts_made, 1)
            nc.gpsimd.memset(ident_b[:], 0.0).then_inc(consts_made, 1)
            nc.gpsimd.memset(mask_b[:], 0.0).then_inc(consts_made, 1)
            nc.gpsimd.memset(minus_half[:], -0.5).then_inc(consts_made, 1)
            nc.gpsimd.memset(ln_eps[:], LN_EPS).then_inc(consts_made, 1)
            nc.gpsimd.memset(att_eps[:], ATT_EPS * DK).then_inc(consts_made, 1)
            pool.wait_ge(consts_made, 6)
            for m in (ident, ident_b):
                nc.gpsimd.affine_select(out=m[:], in_=m[:], compare_op=ALU.not_equal, fill=1.0, base=0,
                                        pattern=[[-1, P]], channel_multiplier=1).then_inc(consts_made, 1)
            nc.gpsimd.affine_select(out=mask_b[:], in_=mask_b[:], compare_op=ALU.is_ge, fill=MASKED, base=0,
                                    pattern=[[-1, P]], channel_multiplier=1).then_inc(consts_made, 1)
            pool.wait_ge(consts_loaded, 16 * 5)
            with pool.Fori(0, B) as b:
                pool.wait_ge(ln_aggr, b * TB + TB)
                nc.gpsimd.tensor_tensor(ln_var[:], mean_var[:, :, 1:2].rearrange("p t o -> p (t o)"),
                                        ln_eps[:], ALU.add).then_inc(ln_var_added, 1)
                pool.wait_ge(ln_var_added, b + 1)
                nc.gpsimd.tensor_tensor(ln_rstd[:], ln_var[:], minus_half[:], ALU.pow) \
                  .then_inc(ln_rstd_ready, 1)

                def step(kind, i, r, ring0, turns0):
                    if kind == "head" and i < TB:
                        pool.wait_ge(summed, r * TB + i + 1)
                        nc.gpsimd.tensor_tensor(sums_eps[:, i, :], sums[:, i, :], att_eps[:], ALU.add) \
                            .then_inc(eps_added, 1)
                        if i == 0:
                            pool.wait_ge(exp_done, r * STEPS)
                        pool.wait_ge(eps_added, r * TB + i + 1)
                        nc.gpsimd.tensor_tensor(rstd[:, i, :], sums_eps[:, i, :], minus_half[:, 0:4],
                                                ALU.pow).then_inc(rstd_ready, 1)

                rounds(pool, b, step)

        @block.scalar
        def _(act):
            def high(dst, src, signal, **more):
                nc.scalar.activation(dst, src, ACT.Copy, **more).then_inc(signal, 1)

            act.wait_ge(consts_loaded, 16 * 5)
            high(down_hi[:], down_raw[:], down_hi_done)
            act.wait_ge(k_scaled, 2)
            with act.Fori(0, B) as b:
                for t in range(TB):
                    act.wait_ge(turn_filled, batch_turns(b) + t + 1)
                    high(xT_hi[:, :, t * P:(t + 1) * P], turn[:, t % 2], turn_hi)
                for n in range(2):
                    act.wait_ge(slot_filled, batch_ring(b) + n + 1)
                    high(latT_hi[:, n * BANK:(n + 1) * BANK], slot[:, n, 0:BANK], lat_hi_done)
                for n in range(2):
                    act.wait_ge(slot_filled, batch_ring(b) + 2 + n + 1)
                    high(lat_hi[:, n * GT:(n + 1) * GT, :].rearrange("p t d -> p (t d)"), slot[:, n, 0:BANK],
                         lat_hi_done)
                act.wait_ge(x_loaded, 16 * b + 16)
                act.wait_ge(x2_stored, 16 * b)
                nc.scalar.activation(acc[:], x_in[:], ACT.Copy).then_inc(x_copied, 1)


                def step(kind, u, r, ring0, turns0):
                    if kind == "head":
                        if u < TB:
                            act.wait_ge(slot_filled, ring0 + use("qk", u) + 1)
                            if u == 0:
                                act.wait_ge(eps_added, r * TB)
                            act.wait_ge(summed, r * TB + u)
                            for k in range(4):
                                last = nc.scalar.activation(squares[:, k, :],
                                                            banks("qk", u)[:, k * DK:(k + 1) * DK],
                                                            ACT.Square, accum_out=sums[:, u, k:k + 1])
                            last.then_inc(summed, 1)
                        if u >= 3:
                            n = u - 3
                            w = turns["qkT", n]
                            act.wait_ge(turn_filled, turns0 + w + 1)
                            nc.scalar.activation(qkT_hi[:, 0:2, n * P:(n + 1) * P], turn[:, w % 2, 0:2, :],
                                                 ACT.Copy)
                            high(qkT_hi[:, 2:4, n * P:(n + 1) * P], turn[:, w % 2, 2:4, :], turn_hi,
                                 scale=k_scale[:, 0:1])
                        return

                    def exponentials():
                        if u >= STEPS:
                            return
                        _, h, t = step_of(u)
                        width = (t + 1) * P
                        act.wait_ge(shift_ready, r * STEPS + u + 1)
                        if u >= 3:
                            before = turns["probsT", u - 3, len(chunks(step_of(u - 3)[2])) - 1]
                            act.wait_ge(turn_filled, turns0 + before + 1)
                        nc.scalar.activation(probs[:, u % 3, 0:width], banks("scores", u)[:, 0:width],
                                             ACT.Exp, bias=shift[:, u % 2:u % 2 + 1], scale=rstd[:, t, h:h + 1],
                                             accum_out=row_sum[:, u % 2:u % 2 + 1]).then_inc(exp_done, 1)

                    def value_highs():
                        if u - SPLIT_LAG in pv_steps:
                            n = pv_steps.index(u - SPLIT_LAG)
                            act.wait_ge(pv_filled, r * GROUPS + n + 1)
                            high(oT_hi[:, n % 4, :], pv[:], oT_hi_done)

                    def probs_highs():
                        if 2 <= u < STEPS + 2:
                            _, h, t = step_of(u - 2)
                            j = (u - 2) % GQ
                            for c, blocks in enumerate(chunks(t)):
                                w = turns["probsT", u - 2, c]
                                act.wait_ge(turn_filled, turns0 + w + 1)
                                high(pT_hi[:, h, blocks[0]:blocks[-1] + 1, j * P:(j + 1) * P],
                                     turn[:, w % 2, 0:len(blocks), :], turn_hi)

                    probs_highs()
                    exponentials()
                    value_highs()

                rounds(act, b, step)

        @block.vector
        def _(dve):
            def low(dst, src, high, signal):
                nc.vector.tensor_tensor(dst, src, high, ALU.subtract).then_inc(signal, 1)

            dve.wait_ge(consts_loaded, 16 * 5)
            nc.vector.memset(scratch[:], 0.0).then_inc(k_scaled, 1)
            nc.vector.tensor_scalar(k_scale[:], k_norm[:], float(np.sqrt(DK)), None, ALU.mult).then_inc(k_scaled, 1)
            dve.wait_ge(k_scaled, 2)
            dve.wait_ge(down_hi_done, 1)
            low(down_lo[:], down_raw[:], down_hi[:], down_lo_done)
            with dve.Fori(0, B) as b:
                dve.wait_ge(x_loaded, 16 * b + 16)
                for t in range(TB):
                    nc.vector.bn_stats(stats[:, t, :], x_in[:, t, :]).then_inc(ln_stats, 1)
                wait_apart(dve, scratch, 1, ln_stats, b * TB + TB)
                for t in range(TB):
                    nc.vector.bn_aggr(mean_var[:, t, :], stats[:, t, :]).then_inc(ln_aggr, 1)
                dve.wait_ge(ln_rstd_ready, b + 1)
                for t in range(TB + 1):
                    if t < TB:
                        if t >= 2:
                            dve.wait_ge(turn_filled, batch_turns(b) + t - 1)
                        nc.vector.tensor_scalar(xn[:, t % 2, :], x_in[:, t, :], mean_var[:, t, 0:1],
                                                ln_rstd[:, t:t + 1], ALU.subtract, ALU.mult).then_inc(xn_ready, 1)
                    if t >= 1:
                        n = t - 1
                        dve.wait_ge(turn_hi, batch_turns(b) + n + 1)
                        low(xT_lo[:, :, n * P:(n + 1) * P], turn[:, n % 2], xT_hi[:, :, n * P:(n + 1) * P], turn_lo)
                for n in range(2):
                    dve.wait_ge(lat_hi_done, b * 4 + n + 1)
                    cols = slice(n * BANK, (n + 1) * BANK)
                    low(latT_lo[:, cols], slot[:, n, 0:BANK], latT_hi[:, cols], lat_lo_done)
                    nc.vector.tensor_copy(xn[:, n, :], slot[:, n, 0:BANK]).then_inc(lat_copied, 1)
                for n in range(2):
                    dve.wait_ge(lat_hi_done, b * 4 + 2 + n + 1)
                    low(lat_lo[:, n * GT:(n + 1) * GT, :].rearrange("p t d -> p (t d)"), slot[:, n, 0:BANK],
                        lat_hi[:, n * GT:(n + 1) * GT, :].rearrange("p t d -> p (t d)"), lat_lo_done)
                dve.wait_ge(x_copied, b + 1)


                def step(kind, u, r, ring0, turns0):
                    if kind == "head":
                        if 1 <= u <= TB:
                            n = u - 1
                            tile = banks("qk", n)[:, 0:4 * DK].rearrange("p (h d) -> p h d", h=4)
                            dve.wait_ge(rstd_ready, r * TB + n + 1)
                            nc.vector.tensor_tensor(qk[:, n % 4, 2:4, :], tile[:, 2:4, :],
                                                    rstd[:, n, 2:4].unsqueeze(2).to_broadcast([P, 2, DK]),
                                                    ALU.mult).then_inc(kr_scaled, 1)
                            both = qk[:, n % 4, :, 0:DR].rearrange("p h (k d) -> p h k d", k=2)[:, :, :, 0:RQ]
                            a, c = both[:, :, 0, :], both[:, :, 1, :]
                            dve.wait_ge(q_scaled, r * TB + n + 1)
                            dve.wait_ge(kr_scaled, r * TB + n + 1)
                            for k, table in enumerate((cos_t, sin_t)):
                                nc.vector.tensor_tensor(
                                    turned[:, k], both,
                                    table[:, n, :].unsqueeze(1).unsqueeze(1).to_broadcast([P, 4, 2, RQ]),
                                    ALU.mult).then_inc(rope_parts, 1)
                            dve.wait_ge(rope_parts, (r * TB + n) * 2 + 2)
                            nc.vector.tensor_tensor(a, turned[:, 0, :, 0, :], turned[:, 1, :, 1, :], ALU.add) \
                                .then_inc(rope_done, 1)
                            nc.vector.tensor_tensor(c, turned[:, 0, :, 1, :], turned[:, 1, :, 0, :],
                                                    ALU.subtract).then_inc(rope_done, 1)
                        if u < TB:
                            tile = banks("qk", u)[:, 0:4 * DK].rearrange("p (h d) -> p h d", h=4)
                            dve.wait_ge(summed, r * TB + u + 1)
                            if u >= 4:
                                dve.wait_ge(turn_filled, turns0 + turns["qkT", u - 4] + 1)
                            nc.vector.tensor_tensor(qk[:, u % 4, 0:2, :], tile[:, 0:2, :],
                                                    q_norm[:].unsqueeze(1).to_broadcast([P, 2, DK]), ALU.mult) \
                                .then_inc(q_scaled, 1)
                        if u >= 3:
                            n = u - 3
                            w = turns["qkT", n]
                            cols = slice(n * P, (n + 1) * P)
                            dve.wait_ge(turn_hi, turns0 + w + 1)
                            nc.vector.tensor_tensor(qkT_lo[:, 0:2, cols], turn[:, w % 2, 0:2, :],
                                                    qkT_hi[:, 0:2, cols], ALU.subtract)
                            nc.vector.scalar_tensor_tensor(out=qkT_lo[:, 2:4, cols], in0=turn[:, w % 2, 2:4, :],
                                                           scalar=k_scale[:, 0:1], in1=qkT_hi[:, 2:4, cols],
                                                           op0=ALU.mult, op1=ALU.subtract).then_inc(turn_lo, 1)
                        return
                    def maxima():
                        if u < STEPS:
                            _, h, t = step_of(u)
                            width = (t + 1) * P
                            one = slice(u % 2, u % 2 + 1)
                            dve.wait_ge(slot_filled, ring0 + use("scores", u) + 1)
                            nc.vector.tensor_reduce(row_max[:, one], banks("scores", u)[:, 0:width],
                                                    AXIS_X, ALU.max).then_inc(max_ready, 1)
                            dve.wait_ge(max_ready, r * STEPS + u + 1)
                            nc.vector.tensor_scalar(shift[:, one], row_max[:, one], rstd[:, t, h:h + 1], -1.0,
                                                    ALU.mult, ALU.mult).then_inc(shift_ready, 1)

                    def normalise():
                        if 1 <= u <= STEPS:
                            n = u - 1
                            width = (step_of(n)[2] + 1) * P
                            one = slice(n % 2, n % 2 + 1)
                            dve.wait_ge(exp_done, r * STEPS + n + 1)
                            nc.vector.reciprocal(row_inv[:, one], row_sum[:, one]).then_inc(inv_ready, 1)
                            dve.wait_ge(inv_ready, r * STEPS + n + 1)
                            nc.vector.tensor_scalar(probs[:, n % 3, 0:width], probs[:, n % 3, 0:width],
                                                    row_inv[:, one], None, ALU.mult).then_inc(probs_ready, 1)

                    def value_lows():
                        if u - SPLIT_LAG in pv_steps:
                            n = pv_steps.index(u - SPLIT_LAG)
                            dve.wait_ge(oT_hi_done, r * GROUPS + n + 1)
                            low(oT_lo[:, n % 4, :], pv[:], oT_hi[:, n % 4, :], oT_lo_done)

                    def probs_lows():
                        if 2 <= u < STEPS + 2:
                            _, h, t = step_of(u - 2)
                            j = (u - 2) % GQ
                            for c, blocks in enumerate(chunks(t)):
                                w = turns["probsT", u - 2, c]
                                there = slice(blocks[0], blocks[-1] + 1)
                                dve.wait_ge(turn_hi, turns0 + w + 1)
                                low(pT_lo[:, h, there, j * P:(j + 1) * P], turn[:, w % 2, 0:len(blocks), :],
                                    pT_hi[:, h, there, j * P:(j + 1) * P], turn_lo)

                    def add_outputs():
                        for t in out_tiles_at(u):
                            dve.wait_ge(out_filled, r * TB + t + 1)
                            nc.vector.tensor_tensor(acc[:, t, :], out_ps[:, 0:D], acc[:, t, :], ALU.add) \
                                .then_inc(out_added, 1)

                    maxima()
                    normalise()
                    probs_lows()
                    add_outputs()
                    value_lows()

                rounds(dve, b, step)

        @block.tensor
        def _(pe):
            pe.wait_ge(consts_made, 9)
            pe.wait_ge(down_lo_done, 1)
            with pe.Fori(0, B) as b:
                for t in range(TB):
                    pe.wait_ge(xn_ready, b * TB + t + 1)
                    if t >= 2:
                        pe.wait_ge(turn_lo, batch_turns(b) + t - 1)
                    for c in range(DC):
                        last = nc.tensor.transpose(turn[:, t % 2, c, :], xn[:, t % 2, c * P:(c + 1) * P], ident[:])
                    last.then_inc(turn_filled, 1)
                pe.wait_ge(turn_lo, batch_turns(b) + TB)
                for n in range(2):
                    cols = slice(n * BANK, (n + 1) * BANK)
                    for c in range(DC):
                        mm3(nc.tensor, slot[:, n, 0:BANK], (down_hi[:, c, :], down_lo[:, c, :]),
                            (xT_hi[:, c, cols], xT_lo[:, c, cols]), start=c == 0, stop=c == DC - 1,
                            signal=slot_filled if c == DC - 1 else None)
                for n in range(2):
                    pe.wait_ge(lat_copied, b * 2 + n + 1)
                    for j in range(GT):
                        last = nc.tensor.transpose(slot[:, n, j * P:(j + 1) * P], xn[:, n, j * P:(j + 1) * P],
                                                   ident[:])
                    last.then_inc(slot_filled, 1)
                pe.wait_ge(lat_lo_done, b * 4 + 4)

                def step(kind, u, r, ring0, turns0):
                    def bank_free(kind, n):
                        at = use(kind, n)
                        if at < 4:
                            pe.wait_ge(exp_done, r * STEPS)
                        elif at < 2 * TB and at - 4 < TB:
                            pe.wait_ge(kr_scaled, r * TB + at - 4 + 1)
                        elif at < 2 * TB:
                            pe.wait_ge(exp_done, r * STEPS + at - 4 - TB + 1)
                        else:
                            pe.wait_ge(exp_done, r * STEPS + n - 2 + 1)

                    def turn_free(w):
                        pe.wait_ge(turn_lo, turns0 + w - 1)

                    def scores(u):
                        _, h, t = step_of(u)
                        if u < TB:
                            pe.wait_ge(turn_lo, turns0 + turns["qkT", max(t, 1)] + 1)
                        elif u == TB:
                            pe.wait_ge(turn_lo, turns0 + turns["qkT", TB - 1] + 1)
                        bank_free("scores", u)
                        into = banks("scores", u)
                        q_cols = slice(t * P, (t + 1) * P)
                        width = (t + 1) * P
                        for a in range(0, width, BANK):
                            z = min(a + BANK, width)
                            whole = z < width
                            mm3(nc.tensor, into[:, a:z], (qkT_hi[:, h, q_cols], qkT_lo[:, h, q_cols]),
                                (qkT_hi[:, 2 + h, a:z], qkT_lo[:, 2 + h, a:z]), stop=whole)
                        nc.tensor.matmul(into[:, width - P:width], ident_b[:], mask_b[:], start=False,
                                         stop=True).then_inc(slot_filled, 1)

                    if kind == "head":
                        if u == 0:
                            pe.wait_ge(wqk_loaded, 32 * r + 32)
                        if u < TB:
                            bank_free("qk", u)
                            into = banks("qk", u)
                            cols = slice(u * P, (u + 1) * P)
                            for c in range(DC):
                                mm3(nc.tensor, into[:, 0:2 * DK], (xT_hi[:, c, cols], xT_lo[:, c, cols]),
                                    (wqk(wqk_hi, c), wqk(wqk_lo, c)), start=c == 0, stop=c == DC - 1)
                            mm3(nc.tensor, into[:, 2 * DK:4 * DK], (latT_hi[:, cols], latT_lo[:, cols]),
                                (wqk(wqk_hi, DC), wqk(wqk_lo, DC)), signal=slot_filled)
                        if u >= 3:
                            n = u - 3
                            w = turns["qkT", n]
                            pe.wait_ge(rope_done, (r * TB + n) * 2 + 2)
                            turn_free(w)
                            for k in range(4):
                                last = nc.tensor.transpose(turn[:, w % 2, k, :], qk[:, n % 4, k, :], ident[:])
                            last.then_inc(turn_filled, 1)
                        return
                    def score_products():
                        if u == 0:
                            scores(0)
                        if u + 1 < STEPS:
                            scores(u + 1)

                    def outputs():
                        for t in out_tiles_at(u):
                            g, j = t // GQ, t % GQ
                            if j == 0:
                                pe.wait_ge(oT_lo_done, r * GROUPS + 2 * g + 2)
                            if t == 0:
                                pe.wait_ge(wvo_loaded, 32 * r + 32)
                            pe.wait_ge(out_added, r * TB + t)
                            cols = slice(j * P, (j + 1) * P)
                            for h in range(2):
                                o = 2 * (g % 2) + h
                                mm3(nc.tensor, out_ps[:, 0:D], (oT_hi[:, o, cols], oT_lo[:, o, cols]),
                                    (wvo_hi[:, h, :], wvo_lo[:, h, :]), start=h == 0, stop=h == 1,
                                    signal=out_filled if h == 1 else None)

                    def value_products():
                        if u in pv_steps:
                            n = pv_steps.index(u)
                            g = n // 2
                            last_turn = turns["probsT", u - 3, len(chunks(step_of(u - 3)[2])) - 1]
                            pe.wait_ge(turn_lo, turns0 + last_turn + 1)
                            pe.wait_ge(oT_lo_done, r * GROUPS + n)
                            for k in range(GQ * g + GQ):
                                a = max(0, k - GQ * g) * P
                                mm3(nc.tensor, pv[:, a:GQ * P], (lat_hi[:, k, :], lat_lo[:, k, :]),
                                    (pT_hi[:, n % 2, k, a:GQ * P], pT_lo[:, n % 2, k, a:GQ * P]), start=k == 0,
                                    stop=k == GQ * g + GQ - 1,
                                    signal=pv_filled if k == GQ * g + GQ - 1 else None)

                    def turn_probs():
                        if 2 <= u < STEPS + 2:
                            _, _, t = step_of(u - 2)
                            pe.wait_ge(probs_ready, r * STEPS + u - 1)
                            for c, blocks in enumerate(chunks(t)):
                                w = turns["probsT", u - 2, c]
                                turn_free(w)
                                for k in blocks:
                                    last = nc.tensor.transpose(turn[:, w % 2, k - blocks[0], :],
                                                               probs[:, (u - 2) % 3, k * P:(k + 1) * P], ident[:])
                                last.then_inc(turn_filled, 1)

                    turn_probs()
                    outputs()
                    score_products()
                    value_products()

                rounds(pe, b, step)




def ffn_tokens(nc, keep, x2_dram, norm_rows, router_w, shared_w, h_dram, base_dram, table_dram):
    G = T // BANK
    SF = SH // P
    TURN_LAG = 2
    with ExitStack() as ctx:
        def sb(name, shape, dt=F32):
            return ctx.enter_context(nc.sbuf_tensor("ft_" + name, shape, dt))

        def ps(name, shape):
            return ctx.enter_context(nc.psum_tensor("ft_" + name, shape, F32))

        def sem(name):
            return ctx.enter_context(nc.semaphore("ft_" + name))

        w_raw = sb("w_raw", [P, 3 * DC * SH])
        w_hi = sb("w_hi", [P, 3, DC, SH], F32R)
        w_lo = sb("w_lo", [P, 3, DC, SH], F32R)
        router_raw = sb("router_raw", [P, DC, P])
        router_hi = sb("router_hi", [P, DC, P], F32R)
        router_lo = sb("router_lo", [P, DC, P], F32R)
        norm_raw = sb("norm_raw", [P, D])
        norm = sb("norm", [P, D])
        ident = sb("ident", [P, P])
        before = sb("before", [P, P], BF16)
        ones = sb("ones", [P, P], BF16)
        iota_i = sb("iota_i", [P, E], mybir.dt.int32)
        iota = sb("iota", [P, E])
        minus_half = sb("minus_half", [P, GT])
        ln_eps = sb("ln_eps", [P, GT])
        ffn_eps = sb("ffn_eps", [P, GT])

        scratch = sb("scratch", [P, 10])
        x2 = sb("x2", [P, GT, D])
        stats = sb("stats", [P, GT, 6])
        mean_var = sb("mean_var", [P, GT, 2])
        var = sb("var", [P, GT])
        rstd = sb("rstd", [P, GT])
        h0 = sb("h0", [P, GT, D])
        squares = sb("squares", [P, D])
        sums = sb("sums", [P, GT])
        sums_eps = sb("sums_eps", [P, GT])
        rms = sb("rms", [P, GT])
        h = sb("h", [P, GT, D])
        residual = sb("residual", [P, GT, D])
        base = sb("base", [P, GT, D])
        hT_hi = sb("hT_hi", [P, DC, BANK], F32R)
        hT_lo = sb("hT_lo", [P, DC, BANK], F32R)
        logitsT = sb("logitsT", [P, BANK])
        logits = sb("logits", [P, GT, E])
        top = sb("top", [P, GT, 8])
        top_id = sb("top_id", [P, GT, 8], U32)
        top_idf = sb("top_idf", [P, GT, K])
        top_less = sb("top_less", [P, GT, K])
        top_exp = sb("top_exp", [P, GT, K])
        top_sum = sb("top_sum", [P, GT])
        top_inv = sb("top_inv", [P, GT])
        chosen = sb("chosen", [P, GT, E], BF16)
        expert_start = sb("expert_start", [P, E])
        entry = sb("entry", [P, GT, E])
        entry_hot = sb("entry_hot", [P, GT * K, E])
        entry_f = sb("entry_f", [P, GT * K])
        entry_u = sb("entry_u", [P, GT * K], U32)
        token_i = sb("token_i", [P, NT], mybir.dt.int32)
        token = sb("token", [P, NT])
        token_now = sb("token_now", [P, GT])
        zeros = sb("zeros", [P, E * T // P])
        pool_scratch = sb("pool_scratch", [P, 5])
        silu = sb("silu", [P, 2, BANK])
        inner = sb("inner", [P, 2, BANK])
        inner_hi = sb("inner_hi", [P, SF, BANK], F32R)
        inner_lo = sb("inner_lo", [P, SF, BANK], F32R)

        turn = ps("turn", [P, 2, DC, P])
        gate_up = ps("gate_up", [P, 2, 2, BANK])
        small = ps("small", [P, GT, P])
        rank_ps = ps("rank_ps", [P, GT + 1, E])

        loaded, made, w_hi_done, w_lo_done, norm_done = (
            sem("loaded"), sem("made"), sem("w_hi_done"), sem("w_lo_done"), sem("norm_done"))
        x2_loaded, h_stored, base_stored = sem("x2_loaded"), sem("h_stored"), sem("base_stored")
        stats_done, aggr_done, var_done, rstd_done, h0_done = (
            sem("stats_done"), sem("aggr_done"), sem("var_done"), sem("rstd_done"), sem("h0_done"))
        squared, eps_done, rms_done, h_done, residual_done = (
            sem("squared"), sem("eps_done"), sem("rms_done"), sem("h_done"), sem("residual_done"))
        turn_filled, turn_hi, turn_lo = sem("turn_filled"), sem("turn_hi"), sem("turn_lo")
        router_zeroed = sem("router_zeroed")
        zeros_made, table_zeroed, entry_step, token_copied, scattered = (
            sem("zeros_made"), sem("table_zeroed"), sem("entry_step"), sem("token_copied"), sem("scattered"))
        logitsT_filled, logitsT_copied = sem("logitsT_filled"), sem("logitsT_copied")
        logits_filled, logits_copied, top_done, id_done = (
            sem("logits_filled"), sem("logits_copied"), sem("top_done"), sem("id_done"))
        less_done, exp_done, sum_done, inv_done, weights_done = (
            sem("less_done"), sem("exp_done"), sem("sum_done"), sem("inv_done"), sem("weights_done"))
        hot_done, chosen_done, rank_filled, rank_done, count_done = (
            sem("hot_done"), sem("chosen_done"), sem("rank_filled"), sem("rank_done"), sem("count_done"))
        gu_filled, silu_done, inner_done, inner_hi_done, inner_lo_done = (
            sem("gu_filled"), sem("silu_done"), sem("inner_done"), sem("inner_hi_done"), sem("inner_lo_done"))
        down_filled, base_done = sem("down_filled"), sem("base_done")

        block = ctx.enter_context(nc.Block())

        @block.sync
        def _(sp):
            sp.dma_start(w_raw[:], shared_w).then_inc(loaded, 16)
            sp.wait_ge(router_zeroed, 1)
            sp.dma_start(router_raw[:, :, 0:E], router_w).then_inc(loaded, 16)
            sp.dma_start(norm_raw[:], norm_rows).then_inc(loaded, 16)
            def load_and_store_h(g):
                sp.wait_ge(residual_done, g * GT)
                sp.dma_start(x2[:], x2_dram[bass.ds(g, 1)].rearrange("o (t p) d -> p (o t) d", p=P)) \
                  .then_inc(x2_loaded, 16)
                sp.wait_ge(h_done, g * GT + GT)
                sp.dma_start(h_dram[bass.ds(g, 1)].rearrange("o (t p) d -> p (o t) d", p=P), h[:]) \
                  .then_inc(h_stored, 16)

            def store_base(g):
                sp.wait_ge(base_done, g * GT + GT)
                sp.dma_start(base_dram[bass.ds(g, 1)].rearrange("o (t p) d -> p (o t) d", p=P), base[:]) \
                  .then_inc(base_stored, 16)

            sp.wait_ge(zeros_made, 4)
            sp.dma_start(table_dram.rearrange("(p n) o -> p (n o)", p=P), zeros[:]).then_inc(table_zeroed, 16)
            load_and_store_h(0)
            with sp.Fori(0, G - 1) as g:
                load_and_store_h(g + 1)
                store_base(g)
            store_base(G - 1)
            sp.wait_ge(h_stored, 16 * G)
            sp.wait_ge(base_stored, 16 * G)

        @block.gpsimd
        def _(pool):
            nc.gpsimd.memset(router_raw[:], 0.0).then_inc(router_zeroed, 1)
            nc.gpsimd.memset(ident[:], 0.0).then_inc(made, 1)
            nc.gpsimd.memset(before[:], 1.0).then_inc(made, 1)
            nc.gpsimd.memset(ones[:], 1.0).then_inc(made, 1)
            nc.gpsimd.memset(minus_half[:], -0.5).then_inc(made, 1)
            nc.gpsimd.memset(ln_eps[:], LN_EPS).then_inc(made, 1)
            nc.gpsimd.memset(ffn_eps[:], FFN_EPS * D).then_inc(made, 1)
            nc.gpsimd.iota(iota_i[:], pattern=[[1, E]], base=0, channel_multiplier=0).then_inc(made, 1)
            pool.wait_ge(made, 7)
            nc.gpsimd.affine_select(out=ident[:], in_=ident[:], compare_op=ALU.not_equal, fill=1.0, base=0,
                                    pattern=[[-1, P]], channel_multiplier=1).then_inc(made, 1)
            nc.gpsimd.affine_select(out=before[:], in_=before[:], compare_op=ALU.is_gt, fill=0.0, base=0,
                                    pattern=[[1, P]], channel_multiplier=-1).then_inc(made, 1)
            nc.gpsimd.tensor_copy(iota[:], iota_i[:]).then_inc(made, 1)
            pool.wait_ge(made, 10)
            nc.gpsimd.memset(zeros[:], 0.0).then_inc(zeros_made, 1)
            nc.gpsimd.memset(pool_scratch[:], 0.0).then_inc(zeros_made, 1)
            nc.gpsimd.iota(token_i[:], pattern=[[P, NT]], base=0, channel_multiplier=1).then_inc(zeros_made, 1)
            pool.wait_ge(zeros_made, 3)
            nc.gpsimd.tensor_copy(token[:], token_i[:]).then_inc(zeros_made, 1)
            pool.wait_ge(zeros_made, 4)

            def norms(g):
                pool.wait_ge(aggr_done, g * GT + GT)
                nc.gpsimd.tensor_tensor(var[:], mean_var[:, :, 1:2].rearrange("p t o -> p (t o)"), ln_eps[:],
                                        ALU.add).then_inc(var_done, 1)
                pool.wait_ge(var_done, g + 1)
                nc.gpsimd.tensor_tensor(rstd[:], var[:], minus_half[:], ALU.pow).then_inc(rstd_done, 1)
                pool.wait_ge(squared, g * GT + GT)
                nc.gpsimd.tensor_tensor(sums_eps[:], sums[:], ffn_eps[:], ALU.add).then_inc(eps_done, 1)
                pool.wait_ge(eps_done, g + 1)
                nc.gpsimd.tensor_tensor(rms[:], sums_eps[:], minus_half[:], ALU.pow).then_inc(rms_done, 1)

            def scatter(g, column):
                pool.wait_ge(scattered, 16 * GT * K * g)
                nc.gpsimd.tensor_copy(token_now[:], token[:, bass.ds(g * GT, GT)]).then_inc(token_copied, 1)
                wait_apart(pool, pool_scratch, column, token_copied, g + 1)
                wait_apart(pool, pool_scratch, column + 1, entry_step, 4 * g + 4)
                for t in range(GT):
                    for k in range(K):
                        nc.gpsimd.indirect_dma_start(
                            table_dram, bass.IndirectOffsetOnAxis(ap=entry_u[:, t * K + k:t * K + k + 1], axis=0),
                            token_now[:, t:t + 1], None).then_inc(scattered, 16)

            pool.wait_ge(table_zeroed, 16)
            norms(0)
            with pool.Fori(0, G - 1) as g:
                norms(g + 1)
                scatter(g, 1)
            scatter(G - 1, 3)
            pool.wait_ge(scattered, 16 * GT * K * G)

        @block.scalar
        def _(act):
            act.wait_ge(loaded, 48)
            nc.scalar.activation(w_hi[:].rearrange("p w c n -> p (w c n)"), w_raw[:], ACT.Copy) \
                .then_inc(w_hi_done, 1)
            nc.scalar.activation(router_hi[:], router_raw[:], ACT.Copy).then_inc(w_hi_done, 1)

            def square_sums(g):
                for t in range(GT):
                    act.wait_ge(h0_done, g * GT + t + 1)
                    act.wait_ge(squared, g * GT + t)
                    nc.scalar.activation(squares[:], h0[:, t, :], ACT.Square, accum_out=sums[:, t:t + 1]) \
                        .then_inc(squared, 1)

            def turned_highs(g):
                for t in range(GT):
                    act.wait_ge(turn_filled, g * GT + t + 1)
                    nc.scalar.activation(hT_hi[:, :, t * P:(t + 1) * P], turn[:, t % 2], ACT.Copy) \
                        .then_inc(turn_hi, 1)
                act.wait_ge(logitsT_filled, g + 1)
                nc.scalar.activation(logitsT[:], turn[:, 0].rearrange("p c n -> p (c n)"), ACT.Copy) \
                    .then_inc(logitsT_copied, 1)

            def shared(g, f):
                act.wait_ge(gu_filled, g * SF + f + 1)
                if f >= 2:
                    act.wait_ge(inner_done, g * SF + f - 1)
                nc.scalar.activation(silu[:, f % 2, :], gate_up[:, f % 2, 0, :], ACT.Silu).then_inc(silu_done, 1)
                act.wait_ge(inner_done, g * SF + f + 1)
                nc.scalar.activation(inner_hi[:, f, :], inner[:, f % 2, :], ACT.Copy).then_inc(inner_hi_done, 1)

            def group(g, with_next):
                shared(g, 0)
                act.wait_ge(logits_filled, g + 1)
                nc.scalar.activation(logits[:], small[:, :, 0:E], ACT.Copy).then_inc(logits_copied, 1)
                shared(g, 1)
                act.wait_ge(less_done, g + 1)
                nc.scalar.activation(top_exp[:], top_less[:], ACT.Exp).then_inc(exp_done, 1)
                shared(g, 2)
                if with_next:
                    square_sums(g + 1)
                shared(g, 3)
                if with_next:
                    turned_highs(g + 1)

            square_sums(0)
            turned_highs(0)
            with act.Fori(0, G - 1) as g:
                group(g, True)
            group(G - 1, False)

        @block.vector
        def _(dve):
            dve.wait_ge(loaded, 48)
            nc.vector.tensor_scalar(norm[:], norm_raw[:], float(np.sqrt(D)), None, ALU.mult).then_inc(norm_done, 1)
            nc.vector.memset(keep.count[:], 0.0).then_inc(count_done, 1)
            nc.vector.memset(scratch[:], 0.0).then_inc(norm_done, 1)
            dve.wait_ge(made, 10)
            nc.vector.tensor_scalar(expert_start[:], iota[:], float(T), None, ALU.mult).then_inc(norm_done, 1)
            dve.wait_ge(w_hi_done, 2)
            nc.vector.tensor_tensor(w_lo[:].rearrange("p w c n -> p (w c n)"), w_raw[:],
                                    w_hi[:].rearrange("p w c n -> p (w c n)"), ALU.subtract) \
                .then_inc(w_lo_done, 1)
            nc.vector.tensor_tensor(router_lo[:], router_raw[:], router_hi[:], ALU.subtract) \
                .then_inc(w_lo_done, 1)
            dve.wait_ge(norm_done, 3)

            def token_stats(g, column):
                dve.wait_ge(x2_loaded, 16 * g + 16)
                for t in range(GT):
                    nc.vector.bn_stats(stats[:, t, :], x2[:, t, :]).then_inc(stats_done, 1)
                wait_apart(dve, scratch, column, stats_done, g * GT + GT)
                for t in range(GT):
                    nc.vector.bn_aggr(mean_var[:, t, :], stats[:, t, :]).then_inc(aggr_done, 1)

            def layernorm(g):
                dve.wait_ge(rstd_done, g + 1)
                for t in range(GT):
                    nc.vector.tensor_scalar(h0[:, t, :], x2[:, t, :], mean_var[:, t, 0:1], rstd[:, t:t + 1],
                                            ALU.subtract, ALU.mult).then_inc(h0_done, 1)

            def rmsnorm(g):
                dve.wait_ge(rms_done, g + 1)
                dve.wait_ge(h_stored, 16 * g)
                for t in range(GT):
                    nc.vector.scalar_tensor_tensor(out=h[:, t, :], in0=h0[:, t, :], scalar=rms[:, t:t + 1],
                                                   in1=norm[:], op0=ALU.mult, op1=ALU.mult).then_inc(h_done, 1)

            def residuals(g, t):
                nc.vector.tensor_tensor(residual[:, t, :], x2[:, t, :], h0[:, t, :], ALU.add) \
                    .then_inc(residual_done, 1)

            def turned_low(g, t):
                cols = slice(t * P, (t + 1) * P)
                dve.wait_ge(turn_hi, g * GT + t + 1)
                nc.vector.tensor_tensor(hT_lo[:, :, cols], turn[:, t % 2], hT_hi[:, :, cols], ALU.subtract) \
                    .then_inc(turn_lo, 1)

            def shared(g, f):
                dve.wait_ge(silu_done, g * SF + f + 1)
                if f >= 2:
                    dve.wait_ge(inner_hi_done, g * SF + f - 1)
                    dve.wait_ge(inner_lo_done, g * SF + f - 1)
                nc.vector.tensor_tensor(inner[:, f % 2, :], gate_up[:, f % 2, 1, :], silu[:, f % 2, :],
                                        ALU.mult).then_inc(inner_done, 1)
                dve.wait_ge(inner_hi_done, g * SF + f + 1)
                nc.vector.tensor_tensor(inner_lo[:, f, :], inner[:, f % 2, :], inner_hi[:, f, :],
                                        ALU.subtract).then_inc(inner_lo_done, 1)

            def group(g, column, with_next):
                shared(g, 0)
                wait_apart(dve, scratch, column, logits_copied, g + 1)
                for t in range(GT):
                    nc.vector.max(top[:, t, :], logits[:, t, :]).then_inc(top_done, 1)
                wait_apart(dve, scratch, column + 1, top_done, g * GT + GT)
                for t in range(GT):
                    nc.vector.max_index(top_id[:, t, :], top[:, t, :], logits[:, t, :]).then_inc(id_done, 1)
                nc.vector.tensor_tensor(top_less[:], top[:, :, 0:K], top[:, :, 0:1].to_broadcast([P, GT, K]),
                                        ALU.subtract).then_inc(less_done, 1)
                if with_next:
                    token_stats(g + 1, column + 2)
                shared(g, 1)
                dve.wait_ge(id_done, g * (GT + 1) + GT)
                nc.vector.tensor_copy(top_idf[:], top_id[:, :, 0:K]).then_inc(id_done, 1)
                dve.wait_ge(id_done, g * (GT + 1) + GT + 1)
                hot = keep.hot[:, bass.ds(g * GT * K, GT * K), :]
                nc.vector.tensor_tensor(hot, iota[:].unsqueeze(1).to_broadcast([P, GT * K, E]),
                                        top_idf[:].rearrange("p t k -> p (t k)").unsqueeze(2)
                                        .to_broadcast([P, GT * K, E]), ALU.is_equal).then_inc(hot_done, 1)
                dve.wait_ge(exp_done, g + 1)
                nc.vector.tensor_reduce(top_sum[:], top_exp[:], AXIS_X, ALU.add).then_inc(sum_done, 1)
                dve.wait_ge(sum_done, g + 1)
                nc.vector.reciprocal(top_inv[:], top_sum[:]).then_inc(inv_done, 1)
                dve.wait_ge(inv_done, g + 1)
                top_w = keep.top_w[:, bass.ds(g * GT * K, GT * K)].rearrange("p (t k) -> p t k", k=K)
                nc.vector.tensor_tensor(top_w, top_exp[:], top_inv[:].unsqueeze(2).to_broadcast([P, GT, K]),
                                        ALU.mult).then_inc(weights_done, 1)
                wait_apart(dve, scratch, column + 3, hot_done, g + 1)
                with nc.allow_low_precision("a sum of at most four ones"):
                    nc.vector.tensor_reduce(chosen[:], hot.rearrange("p (t k) e -> p t e k", k=K), AXIS_X,
                                            ALU.add).then_inc(chosen_done, 1)
                if with_next:
                    layernorm(g + 1)
                shared(g, 2)
                dve.wait_ge(rank_filled, g + 1)
                dve.wait_ge(count_done, g + 1)
                nc.vector.tensor_tensor(keep.rank[:, bass.ds(g * GT, GT), :], rank_ps[:, 0:GT, :],
                                        keep.count[:].unsqueeze(1).to_broadcast([P, GT, E]), ALU.add) \
                    .then_inc(rank_done, 1)
                dve.wait_ge(rank_done, g + 1)
                nc.vector.tensor_tensor(keep.count[:], rank_ps[:, GT, :], keep.count[:], ALU.add) \
                    .then_inc(count_done, 1)
                nc.vector.tensor_tensor(entry[:], keep.rank[:, bass.ds(g * GT, GT), :],
                                        expert_start[:].unsqueeze(1).to_broadcast([P, GT, E]), ALU.add) \
                    .then_inc(entry_step, 1)
                dve.wait_ge(entry_step, 4 * g + 1)
                nc.vector.tensor_tensor(entry_hot[:].rearrange("p (t k) e -> p t k e", k=K),
                                        hot.rearrange("p (t k) e -> p t k e", k=K),
                                        entry[:].unsqueeze(2).to_broadcast([P, GT, K, E]), ALU.mult) \
                    .then_inc(entry_step, 1)
                dve.wait_ge(entry_step, 4 * g + 2)
                nc.vector.tensor_reduce(entry_f[:], entry_hot[:], AXIS_X, ALU.add).then_inc(entry_step, 1)
                dve.wait_ge(entry_step, 4 * g + 3)
                dve.wait_ge(scattered, 16 * GT * K * g)
                nc.vector.tensor_copy(entry_u[:], entry_f[:]).then_inc(entry_step, 1)
                shared(g, 3)
                if with_next:
                    rmsnorm(g + 1)
                dve.wait_ge(residual_done, g * GT + GT)
                dve.wait_ge(base_stored, 16 * g)
                for t in range(GT + TURN_LAG):
                    if t < GT:
                        dve.wait_ge(down_filled, g * GT + t + 1)
                        nc.vector.tensor_tensor(base[:, t, :], gate_up[:, t % 2, 0, :], residual[:, t, :],
                                                ALU.add).then_inc(base_done, 1)
                    if t >= TURN_LAG and with_next:
                        turned_low(g + 1, t - TURN_LAG)
                    if t < GT and with_next:
                        dve.wait_ge(base_done, g * GT + t + 1)
                        residuals(g + 1, t)

            token_stats(0, 1)
            layernorm(0)
            rmsnorm(0)
            for t in range(GT):
                residuals(0, t)
                turned_low(0, t)
            with dve.Fori(0, G - 1) as g:
                group(g, 2, True)
            group(G - 1, 6, False)

        @block.tensor
        def _(pe):
            pe.wait_ge(made, 10)
            pe.wait_ge(w_lo_done, 2)

            def turn_h(g, t):
                pe.wait_ge(h_done, g * GT + t + 1)
                pe.wait_ge(turn_lo, g * GT + max(t - 1, 0))
                for c in range(DC):
                    last = nc.tensor.transpose(turn[:, t % 2, c, :], h[:, t, c * P:(c + 1) * P], ident[:])
                last.then_inc(turn_filled, 1)

            def router(g):
                pe.wait_ge(turn_lo, g * GT + GT)
                for c in range(DC):
                    mm3(nc.tensor, turn[:, 0].rearrange("p c n -> p (c n)"),
                        (router_hi[:, c, :], router_lo[:, c, :]), (hT_hi[:, c, :], hT_lo[:, c, :]),
                        start=c == 0, stop=c == DC - 1, signal=logitsT_filled if c == DC - 1 else None)

            def turn_logits(g):
                pe.wait_ge(logitsT_copied, g + 1)
                pe.wait_ge(logits_copied, g)
                for t in range(GT):
                    last = nc.tensor.transpose(small[:, t, :], logitsT[:, t * P:(t + 1) * P], ident[:])
                last.then_inc(logits_filled, 1)

            def ranks(g):
                pe.wait_ge(chosen_done, g + 1)
                pe.wait_ge(count_done, g + 1)
                for t in range(GT + 1):
                    for s in range(min(t + 1, GT)):
                        last = nc.tensor.matmul(rank_ps[:, t, :], before[:] if s == t else ones[:],
                                                chosen[:, s, :], start=s == 0, stop=s == min(t, GT - 1))
                last.then_inc(rank_filled, 1)

            def down(g, t):
                if t >= 2:
                    pe.wait_ge(base_done, g * GT + t - 1)
                cols = slice(t * P, (t + 1) * P)
                for f in range(SF):
                    if t == 0 and f in (0, SF - 1):
                        pe.wait_ge(inner_lo_done, g * SF + (SF - 1 if f == 0 else SF))
                    mm3(nc.tensor, gate_up[:, t % 2, 0, :], (inner_hi[:, f, cols], inner_lo[:, f, cols]),
                        (w_hi[:, 2, f, :], w_lo[:, 2, f, :]), start=f == 0, stop=f == SF - 1,
                        signal=down_filled if f == SF - 1 else None)

            def group(g, with_next):
                for f in range(SF):
                    if f < 2:
                        pe.wait_ge(base_done, g * GT)
                    else:
                        pe.wait_ge(inner_done, g * SF + f - 1)
                    for w in range(2):
                        for c in range(DC):
                            cols = slice(f * P, (f + 1) * P)
                            mm3(nc.tensor, gate_up[:, f % 2, w, :], (w_hi[:, w, c, cols], w_lo[:, w, c, cols]),
                                (hT_hi[:, c, :], hT_lo[:, c, :]), start=c == 0, stop=c == DC - 1,
                                signal=gu_filled if c == DC - 1 and w == 1 else None)
                    if f == 0:
                        turn_logits(g)
                    if f == SF - 2:
                        ranks(g)
                for t in range(GT + TURN_LAG):
                    if t < GT:
                        down(g, t)
                    if t >= TURN_LAG and with_next:
                        turn_h(g + 1, t - TURN_LAG)
                if with_next:
                    router(g + 1)

            for t in range(GT):
                turn_h(0, t)
            router(0)
            with pe.Fori(0, G - 1) as g:
                group(g, True)
            group(G - 1, False)


def dispatch(nc, keep):
    with ExitStack() as ctx:
        def sb(name, shape, dt=F32):
            return ctx.enter_context(nc.sbuf_tensor("di_" + name, shape, dt))

        def sem(name):
            return ctx.enter_context(nc.semaphore("di_" + name))

        I32 = mybir.dt.int32
        padded = sb("padded", [P, E], I32)
        tiles_i = sb("tiles_i", [P, E], I32)
        tiles_raw = sb("tiles_raw", [P, E])
        tiles = sb("tiles", [P, E])
        ones = sb("ones", [P, E])
        ends = sb("ends", [P, E])
        starts = sb("starts", [P, E])
        first = sb("first", [P, E])
        place = sb("place", [P, NT, E])
        placed = sb("placed", [P, NT * K, E])
        slot_f = sb("slot_f", [P, NT * K])
        tile_i = sb("tile_i", [P, SLOT_TILES], I32)
        tile_n = sb("tile_n", [P, SLOT_TILES])
        ended = sb("ended", [P, SLOT_TILES, E])
        owner = sb("owner", [P, SLOT_TILES])
        first_tile = sb("first_tile", [P, SLOT_TILES])
        upcoming = sb("upcoming", [P, SLOT_TILES])
        part_tile_i = sb("part_tile_i", [P, 2], I32)
        part_tile = sb("part_tile", [P, 2])
        part_ended = sb("part_ended", [P, 2, E])
        part_ends = sb("part_ends", [P, 2, E])
        part_owner = sb("part_owner", [P, 2])
        part_start = sb("part_start", [P, 2])
        part_row = sb("part_row", [P, 2])
        made, step = sem("made"), sem("step")
        block = ctx.enter_context(nc.Block())

        @block.vector
        def _(dve):
            done = [0]

            def then(ins):
                done[0] += 1
                ins.then_inc(step, 1)
                dve.wait_ge(step, done[0])

            nc.vector.memset(ones[:], 1.0)
            then(nc.vector.tensor_scalar(padded[:], keep.count[:], float(P - 1), None, ALU.add))
            then(nc.vector.tensor_scalar(tiles_i[:], padded[:], P.bit_length() - 1, None,
                                         ALU.logical_shift_right))
            then(nc.vector.tensor_copy(tiles_raw[:], tiles_i[:]))
            then(nc.vector.tensor_scalar(tiles[:], tiles_raw[:], 1.0, None, ALU.max))
            then(nc.vector.tensor_tensor_scan(ends[:], ones[:], tiles[:], 0.0, ALU.mult, ALU.add))
            then(nc.vector.tensor_tensor(starts[:], ends[:], tiles[:], ALU.subtract))
            then(nc.vector.tensor_scalar(first[:], starts[:], float(P), None, ALU.mult))
            then(nc.vector.tensor_tensor(place[:], keep.rank[:], first[:].unsqueeze(1).to_broadcast([P, NT, E]),
                                         ALU.add))
            for k in range(K):
                ins = nc.vector.tensor_tensor(
                    placed[:].rearrange("p (t k) e -> p t k e", k=K)[:, :, k, :],
                    keep.hot[:].rearrange("p (t k) e -> p t k e", k=K)[:, :, k, :], place[:], ALU.mult)
            then(ins)
            then(nc.vector.tensor_reduce(slot_f[:], placed[:], AXIS_X, ALU.add))
            nc.vector.tensor_copy(keep.slots[:], slot_f[:])
            dve.wait_ge(made, 4)
            then(nc.vector.tensor_tensor(ended[:], tile_n[:].unsqueeze(2).to_broadcast([P, SLOT_TILES, E]),
                                         ends[:].unsqueeze(1).to_broadcast([P, SLOT_TILES, E]), ALU.is_ge))
            then(nc.vector.tensor_reduce(owner[:], ended[:], AXIS_X, ALU.add))
            then(nc.vector.tensor_scalar(owner[:], owner[:], float(E - 1), None, ALU.min))
            nc.vector.tensor_copy(keep.owner[:], owner[:])
            then(nc.vector.tensor_tensor(part_ended[:], part_tile[:].unsqueeze(2).to_broadcast([P, 2, E]),
                                         ends[:].unsqueeze(1).to_broadcast([P, 2, E]), ALU.is_ge))
            then(nc.vector.tensor_reduce(part_owner[:], part_ended[:], AXIS_X, ALU.add))
            then(nc.vector.tensor_scalar(part_owner[:], part_owner[:], float(E - 1), None, ALU.min))
            then(nc.vector.tensor_tensor(part_ends[:], part_ended[:],
                                         ends[:].unsqueeze(1).to_broadcast([P, 2, E]), ALU.mult))
            then(nc.vector.tensor_reduce(part_start[:], part_ends[:], AXIS_X, ALU.max))
            then(nc.vector.scalar_tensor_tensor(out=part_row[:], in0=part_owner[:], scalar=float(T // P),
                                                in1=part_tile[:], op0=ALU.mult, op1=ALU.add))
            then(nc.vector.tensor_tensor(part_row[:], part_row[:], part_start[:], ALU.subtract))
            then(nc.vector.tensor_scalar(part_row[:], part_row[:], float(E * T // P - 1), None, ALU.min))
            nc.vector.tensor_copy(keep.table_rows[:], part_row[:])
            then(nc.vector.memset(first_tile[:, 0:1], 1.0))
            then(nc.vector.tensor_tensor(first_tile[:, 1:SLOT_TILES], owner[:, 1:SLOT_TILES],
                                         owner[:, 0:SLOT_TILES - 1], ALU.is_gt))
            then(nc.vector.tensor_scalar(upcoming[:], owner[:], float(E - 1), None, ALU.is_lt))
            then(nc.vector.tensor_tensor(upcoming[:], upcoming[:], first_tile[:], ALU.mult))
            then(nc.vector.scalar_tensor_tensor(out=keep.next_weights[:], in0=owner[:], scalar=1.0,
                                                in1=upcoming[:], op0=ALU.add, op1=ALU.mult))

        @block.gpsimd
        def _(pool):
            nc.gpsimd.iota(tile_i[:], pattern=[[1, SLOT_TILES]], base=0, channel_multiplier=0).then_inc(made, 1)
            nc.gpsimd.iota(part_tile_i[:], pattern=[[P, 2]], base=0, channel_multiplier=1).then_inc(made, 1)
            pool.wait_ge(made, 2)
            nc.gpsimd.tensor_copy(tile_n[:], tile_i[:]).then_inc(made, 1)
            nc.gpsimd.tensor_copy(part_tile[:], part_tile_i[:]).then_inc(made, 1)


def experts(nc, keep, table_dram, h_dram, w12, y_dram):
    with ExitStack() as ctx:
        def sb(name, shape, dt=F32):
            return ctx.enter_context(nc.sbuf_tensor("ex_" + name, shape, dt))

        def ps(name, shape):
            return ctx.enter_context(nc.psum_tensor("ex_" + name, shape, F32))

        def sem(name):
            return ctx.enter_context(nc.semaphore("ex_" + name))

        def sems(name, n=2):
            return [sem(f"{name}{s}") for s in range(n)]

        FC = I // P
        N = SLOT_TILES
        LEFT = N - P
        W1 = DC * 2 * I
        W12 = W1 + FC * D
        AHEAD = 4
        ident = sb("ident", [P, P])
        table = sb("table", [P, P])
        table_rest = sb("table_rest", [P, P])
        token = sb("token", [P, N], U32)
        scratch = sb("scratch", [P, 1 + 4 * AHEAD])
        token_now = sb("token_now", [P, AHEAD, 1], U32)
        w_raw = sb("w_raw", [P, 2, W12])
        w_hi = sb("w_hi", [P, 2, W12], F32R)
        w_lo = sb("w_lo", [P, 2, W12], F32R)
        rows = sb("rows", [P, AHEAD, D])
        rowsT_hi = sb("rowsT_hi", [P, 2, DC, P], F32R)
        rowsT_lo = sb("rowsT_lo", [P, 2, DC, P], F32R)
        silu = sb("silu", [P, 2, I])
        inner = sb("inner", [P, 2, I])
        innerT_hi = sb("innerT_hi", [P, 2, FC, P], F32R)
        innerT_lo = sb("innerT_lo", [P, 2, FC, P], F32R)
        y = sb("y", [P, 2, D])
        turn = ps("turn", [P, 2, DC, P])
        gate_up = ps("gate_up", [P, 2, 2 * I])
        inner_turn = ps("inner_turn", [P, 2, BANK])
        y_ps = ps("y_ps", [P, 2, D])

        made, table_loaded, table_turned, token_ready = (
            sem("made"), sem("table_loaded"), sem("table_turned"), sem("token_ready"))
        w_loaded, w_hi_done, w_lo_done = sem("w_loaded"), sem("w_hi_done"), sem("w_lo_done")
        copied, gathered, turned = sems("copied", AHEAD), sems("gathered", AHEAD), sems("turned", AHEAD)
        rowsT_hi_done, rowsT_lo_done, gu_filled, silu_done, inner_done = (
            sems("rowsT_hi"), sems("rowsT_lo"), sems("gu_filled"), sems("silu_done"), sems("inner_done"))
        inner_turned, innerT_hi_done, innerT_lo_done, y_filled, y_done, y_stored = (
            sems("inner_turned"), sems("innerT_hi"), sems("innerT_lo"), sems("y_filled"), sems("y_done"),
            sems("y_stored"))
        block = ctx.enter_context(nc.Block())

        def tile_at(i, o):
            return 4 * i + o, o % 2, 2 * i + o // 2, o % AHEAD, i + o // AHEAD

        def steps(eng, step):
            step(*[tile_at(0, 0 + d) if 0 + d >= 0 else None for d in (-2, -1, 0, 1)])
            step(*[tile_at(0, 1 + d) if 1 + d >= 0 else None for d in (-2, -1, 0, 1)])
            with eng.Fori(0, N // 4 - 1) as i:
                for j in range(4):
                    step(*[tile_at(i, 2 + j + d) for d in (-2, -1, 0, 1)])
            for n in range(N - 2, N + 2):
                step(*[tile_at(0, n + d) if n + d < N else None for d in (-2, -1, 0, 1)])

        @block.sync
        def _(sp):
            with sp.Fori(0, E // 2) as g:
                for s in range(2):
                    sp.wait_ge(w_loaded, (2 * g + s) * 16)
                    sp.wait_ge(w_lo_done, 2 * g)
                    sp.dma_start(w_raw[:, s, :], w12[bass.ds(2 * g + s, 1)].rearrange("o p n -> p (o n)")) \
                      .then_inc(w_loaded, 16)

        @block.gpsimd
        def _(pool):
            nc.gpsimd.memset(ident[:], 0.0).then_inc(made, 1)
            nc.gpsimd.memset(scratch[:], 0.0).then_inc(made, 1)
            pool.wait_ge(made, 2)
            nc.gpsimd.affine_select(out=ident[:], in_=ident[:], compare_op=ALU.not_equal, fill=1.0, base=0,
                                    pattern=[[-1, P]], channel_multiplier=1).then_inc(made, 1)
            for c, dst in enumerate((table, table_rest)):
                nc.gpsimd.indirect_dma_start(
                    dst[:], None, table_dram.rearrange("(j s) o -> j (s o)", s=P),
                    bass.IndirectOffsetOnAxis(ap=keep.table_rows[:, c:c + 1], axis=0)).then_inc(table_loaded, 16)
            pool.wait_ge(token_ready, 2)

            def gather(m, q, column):
                wait_apart(pool, scratch, column, gathered[q], 16 * m)
                nc.gpsimd.tensor_copy(token_now[:, q, :], token[:, bass.ds(AHEAD * m + q, 1)]) \
                    .then_inc(copied[q], 1)
                pool.wait_ge(turned[q], m)
                wait_apart(pool, scratch, column + AHEAD, copied[q], m + 1)
                nc.gpsimd.indirect_dma_start(
                    rows[:, q, :], None, h_dram,
                    bass.IndirectOffsetOnAxis(ap=token_now[:, q, :], axis=0)).then_inc(gathered[q], 16)

            def rest_of_weights(n):
                e = pool.value_load(keep.next_weights[0:1, bass.ds(n, 1)], min_val=0, max_val=E - 1)
                with pool.If(e > 0):
                    pool.wait_ge(w_hi_done, e + 1)
                    slot = bass.ds(e % 2, 1)
                    nc.gpsimd.tensor_tensor(w_lo[:, slot, :], w_raw[:, slot, :], w_hi[:, slot, :],
                                            ALU.subtract).then_inc(w_lo_done, 1)

            LAG = AHEAD - 1
            for q in range(AHEAD):
                gather(0, q, 1 + q)
            rest_of_weights(0)
            with pool.Fori(1, N // AHEAD) as m:
                for q in range(AHEAD):
                    gather(m, q, 1 + 2 * AHEAD + q)
                    rest_of_weights(AHEAD * m + q - LAG)
            for n in range(N - LAG, N):
                rest_of_weights(n)

        @block.scalar
        def _(act):
            act.wait_ge(w_loaded, 16)
            nc.scalar.activation(w_hi[:, 0, :], w_raw[:, 0, :], ACT.Copy).then_inc(w_hi_done, 1)

            def turned_rows_hi(tile):
                n, s, h, q, m = tile
                act.wait_ge(turned[q], m + 1)
                act.wait_ge(gu_filled[s], h)
                nc.scalar.activation(rowsT_hi[:, s], turn[:, s], ACT.Copy).then_inc(rowsT_hi_done[s], 1)

            def step(stored, finished, now, coming):
                if finished:
                    n, s, h, _, _ = finished
                    act.wait_ge(inner_turned[s], h + 1)
                    act.wait_ge(y_filled[s], h)
                    nc.scalar.activation(innerT_hi[:, s].rearrange("p c n -> p (c n)"), inner_turn[:, s, 0:I],
                                         ACT.Copy).then_inc(innerT_hi_done[s], 1)
                if now:
                    n, s, h, _, _ = now
                    act.wait_ge(gu_filled[s], h + 1)
                    act.wait_ge(inner_done[s], h)
                    nc.scalar.activation(silu[:, s, :], gate_up[:, s, 0:I], ACT.Silu).then_inc(silu_done[s], 1)
                if coming:
                    turned_rows_hi(coming)
                if stored:
                    n, s, h, _, _ = stored
                    act.wait_ge(y_done[s], h + 1)
                    act.dma_start(y_dram[bass.ds(n, 1)].rearrange("o p d -> (o p) d"), y[:, s, :]) \
                       .then_inc(y_stored[s], 16)
                if now:
                    n = now[0]
                    e = act.value_load(keep.next_weights[0:1, bass.ds(n, 1)], min_val=0, max_val=E - 1)
                    with act.If(e > 0):
                        if finished:
                            act.wait_ge(y_filled[finished[1]], finished[2] + 1)
                        act.wait_ge(w_loaded, e * 16 + 16)
                        slot = bass.ds(e % 2, 1)
                        nc.scalar.activation(w_hi[:, slot, :], w_raw[:, slot, :], ACT.Copy).then_inc(w_hi_done, 1)

            turned_rows_hi(tile_at(0, 0))
            steps(act, step)
            for s in range(2):
                act.wait_ge(y_stored[s], 16 * (N // 2))

        @block.vector
        def _(dve):
            dve.wait_ge(w_hi_done, 1)
            nc.vector.tensor_tensor(w_lo[:, 0, :], w_raw[:, 0, :], w_hi[:, 0, :], ALU.subtract) \
                .then_inc(w_lo_done, 1)
            dve.wait_ge(table_turned, 1)
            nc.vector.tensor_copy(token[:, 0:P], turn[:, 0, 0, :]).then_inc(token_ready, 1)
            nc.vector.tensor_copy(token[:, P:N], turn[:, 0, 1, 0:LEFT]).then_inc(token_ready, 1)

            def turned_rows_lo(tile):
                n, s, h, _, _ = tile
                dve.wait_ge(rowsT_hi_done[s], h + 1)
                nc.vector.tensor_tensor(rowsT_lo[:, s], turn[:, s], rowsT_hi[:, s], ALU.subtract) \
                    .then_inc(rowsT_lo_done[s], 1)

            def step(stored, finished, now, coming):
                if finished:
                    n, s, h, _, _ = finished
                    dve.wait_ge(innerT_hi_done[s], h + 1)
                    nc.vector.tensor_tensor(innerT_lo[:, s].rearrange("p c n -> p (c n)"), inner_turn[:, s, 0:I],
                                            innerT_hi[:, s].rearrange("p c n -> p (c n)"), ALU.subtract) \
                        .then_inc(innerT_lo_done[s], 1)
                if now:
                    n, s, h, _, _ = now
                    dve.wait_ge(silu_done[s], h + 1)
                    dve.wait_ge(inner_turned[s], h)
                    nc.vector.tensor_tensor(inner[:, s, :], gate_up[:, s, I:2 * I], silu[:, s, :], ALU.mult) \
                        .then_inc(inner_done[s], 1)
                if coming:
                    turned_rows_lo(coming)
                if finished:
                    n, s, h, _, _ = finished
                    dve.wait_ge(y_filled[s], h + 1)
                    dve.wait_ge(y_stored[s], 16 * h)
                    nc.vector.tensor_copy(y[:, s, :], y_ps[:, s, :]).then_inc(y_done[s], 1)

            turned_rows_lo(tile_at(0, 0))
            steps(dve, step)

        @block.tensor
        def _(pe):
            pe.wait_ge(made, 3)
            pe.wait_ge(table_loaded, 32)
            nc.tensor.transpose(turn[:, 0, 0, :], table[:], ident[:])
            nc.tensor.transpose(turn[:, 0, 1, 0:LEFT], table_rest[0:LEFT], ident[0:LEFT, 0:LEFT]) \
                .then_inc(table_turned, 1)
            pe.wait_ge(token_ready, 2)

            def turn_rows(tile):
                n, s, h, q, m = tile
                pe.wait_ge(gathered[q], 16 * m + 16)
                pe.wait_ge(rowsT_lo_done[s], h)
                for c in range(DC):
                    last = nc.tensor.transpose(turn[:, s, c, :], rows[:, q, c * P:(c + 1) * P], ident[:])
                last.then_inc(turned[q], 1)

            def weights(x, slot, column):
                return x[:, slot, column:column + BANK].rearrange("p o n -> p (o n)")

            def step(stored, finished, now, coming):
                if finished:
                    n, s, h, _, _ = finished
                    pe.wait_ge(inner_done[s], h + 1)
                    pe.wait_ge(innerT_lo_done[s], h)
                    for c in range(FC):
                        last = nc.tensor.transpose(inner_turn[:, s, c * P:(c + 1) * P],
                                                   inner[:, s, c * P:(c + 1) * P], ident[:])
                    last.then_inc(inner_turned[s], 1)
                if now:
                    n, s, h, _, _ = now
                    e = pe.value_load(keep.owner[0:1, bass.ds(n, 1)], min_val=0, max_val=E - 1)
                    pe.wait_ge(rowsT_lo_done[s], h + 1)
                    pe.wait_ge(inner_done[s], h)
                    pe.wait_ge(w_lo_done, e + 1)
                    slot = bass.ds(pe.snap(e % 2), 1)
                    for c in range(DC):
                        mm3(nc.tensor, gate_up[:, s, :], (rowsT_hi[:, s, c, :], rowsT_lo[:, s, c, :]),
                            (weights(w_hi, slot, c * BANK), weights(w_lo, slot, c * BANK)),
                            start=c == 0, stop=c == DC - 1, signal=gu_filled[s] if c == DC - 1 else None)
                if coming:
                    turn_rows(coming)
                if finished:
                    n, s, h, _, _ = finished
                    e = pe.value_load(keep.owner[0:1, bass.ds(n, 1)], min_val=0, max_val=E - 1)
                    slot = bass.ds(pe.snap(e % 2), 1)
                    pe.wait_ge(innerT_lo_done[s], h + 1)
                    pe.wait_ge(y_done[s], h)
                    for c in range(FC):
                        mm3(nc.tensor, y_ps[:, s, :], (innerT_hi[:, s, c, :], innerT_lo[:, s, c, :]),
                            (weights(w_hi, slot, W1 + c * BANK), weights(w_lo, slot, W1 + c * BANK)),
                            start=c == 0, stop=c == FC - 1, signal=y_filled[s] if c == FC - 1 else None)

            turn_rows(tile_at(0, 0))
            steps(pe, step)


def combine(nc, keep, y_dram, base_dram, out):
    with ExitStack() as ctx:
        def sb(name, shape, dt=F32):
            return ctx.enter_context(nc.sbuf_tensor("co_" + name, shape, dt))

        def sems(name):
            return [ctx.enter_context(nc.semaphore(f"co_{name}{s}")) for s in range(2)]

        started = ctx.enter_context(nc.semaphore("co_started"))
        scratch = sb("scratch", [P, 5])
        slot_now = sb("slot_now", [P, 2, K], U32)
        rows = sb("rows", [P, 2, K, D])
        total = sb("total", [P, 2, D])
        base_loaded, copied, gathered, added, stored = (
            sems("base_loaded"), sems("copied"), sems("gathered"), sems("added"), sems("stored"))
        block = ctx.enter_context(nc.Block())

        @block.sync
        def _(sp):
            with sp.Fori(0, NT // 2) as m:
                for s in range(2):
                    sp.wait_ge(stored[s], 16 * m)
                    sp.dma_start(total[:, s, :], base_dram[bass.ds(2 * m + s, 1)].rearrange("o p d -> (o p) d")) \
                      .then_inc(base_loaded[s], 16)

        @block.gpsimd
        def _(pool):
            nc.gpsimd.memset(scratch[:], 0.0).then_inc(started, 1)
            pool.wait_ge(started, 1)
            with pool.Fori(0, NT // 2) as m:
                for s in range(2):
                    wait_apart(pool, scratch, 1 + s, gathered[s], 16 * K * m)
                    nc.gpsimd.tensor_copy(slot_now[:, s, :], keep.slots[:, bass.ds((2 * m + s) * K, K)]) \
                        .then_inc(copied[s], 1)
                    pool.wait_ge(added[s], K * m)
                    wait_apart(pool, scratch, 3 + s, copied[s], m + 1)
                    for k in range(K):
                        nc.gpsimd.indirect_dma_start(
                            rows[:, s, k, :], None, y_dram,
                            bass.IndirectOffsetOnAxis(ap=slot_now[:, s, k:k + 1], axis=0)).then_inc(gathered[s], 16)

        @block.vector
        def _(dve):
            with dve.Fori(0, NT // 2) as m:
                for s in range(2):
                    dve.wait_ge(base_loaded[s], 16 * m + 16)
                    dve.wait_ge(gathered[s], 16 * K * m + 16 * K)
                    for k in range(K):
                        w = keep.top_w[:, bass.ds((2 * m + s) * K + k, 1)]
                        nc.vector.scalar_tensor_tensor(out=total[:, s, :], in0=rows[:, s, k, :], scalar=w,
                                                       in1=total[:, s, :], op0=ALU.mult, op1=ALU.add) \
                            .then_inc(added[s], 1)
                        dve.wait_ge(added[s], K * m + k + 1)

        @block.scalar
        def _(act):
            with act.Fori(0, NT // 2) as m:
                for s in range(2):
                    act.wait_ge(added[s], K * m + K)
                    act.dma_start(out[bass.ds(2 * m + s, 1)].rearrange("o p d -> (o p) d"), total[:, s, :]) \
                       .then_inc(stored[s], 16)
            for s in range(2):
                act.wait_ge(stored[s], 16 * (NT // 2))


class Routing:

    def __init__(self, sb):
        self.count = sb("count", [P, E])
        self.rank = sb("rank", [P, NT, E])
        self.hot = sb("hot", [P, NT * K, E], BF16)
        self.top_w = sb("top_w", [P, NT * K])
        self.slots = sb("slots", [P, NT * K], U32)
        self.owner = sb("owner", [P, SLOT_TILES], mybir.dt.int32)
        self.table_rows = sb("table_rows", [P, 2], U32)
        self.next_weights = sb("next_weights", [P, SLOT_TILES], mybir.dt.int32)


def feed_forward(nc, x2_dram, norm_rows, router_w, shared_w, w12, out, dram):
    h_dram, base_dram, table_dram, y_dram = (
        dram("h", [T, D]), dram("base", [T, D]), dram("table", [E * T, 1]), dram("y", [SLOTS, D]))
    with ExitStack() as ctx:
        def sb(name, shape, dt=F32):
            return ctx.enter_context(nc.sbuf_tensor("keep_" + name, shape, dt))

        keep = Routing(sb)
        grouped = lambda a: a.rearrange("(g n) d -> g n d", n=BANK)
        tiled = lambda a: a.rearrange("(n p) d -> n p d", p=P)
        ffn_tokens(nc, keep, grouped(x2_dram), norm_rows, router_w, shared_w, grouped(h_dram), grouped(base_dram),
                   table_dram)
        dispatch(nc, keep)
        experts(nc, keep, table_dram, h_dram, w12, tiled(y_dram))
        combine(nc, keep, y_dram, tiled(base_dram), tiled(out))


def build_program(nc, x, attn_w, w_kv_down, q_norm_rows, k_norm_col, cos, sin, norm_rows, router_w, shared_w,
                  w12, out):
    def dram(name, shape):
        return nc.dram_tensor("scratch_" + name, tuple(shape), F32, kind="Internal").ap()

    w_hi_dram, w_lo_dram = dram("w_hi", [PAIRS, P, WQK + WO]), dram("w_lo", [PAIRS, P, WQK + WO])
    x2_dram = dram("x2", [T, D])
    prepare_weights(nc, attn_w, w_hi_dram, w_lo_dram)
    attention(nc, x, w_kv_down, q_norm_rows, k_norm_col, cos, sin, w_hi_dram, w_lo_dram,
              x2_dram.rearrange("(b s) d -> b s d", b=B))
    feed_forward(nc, x2_dram, norm_rows, router_w, shared_w, w12,
                 out.rearrange("b s d -> (b s) d"), dram)


def kernel(**inputs):
    import concourse.bacc as bacc
    from concourse.bass_utils import run_bass_kernel_spmd

    a = {name.removeprefix("L0_"): np.asarray(value) for name, value in inputs.items()}
    dense = np.ascontiguousarray
    wq = a["attn_wq"].reshape(DC, P, PAIRS, 2 * DK).transpose(2, 1, 0, 3).reshape(PAIRS, P, DC * 2 * DK)
    wk = np.concatenate([a["attn_w_k_rope"].reshape(DL, H, DR), a["attn_w_k_nope"].reshape(DL, H, DK - DR)], 2)
    wk = wk.reshape(DL, PAIRS, 2 * DK).transpose(1, 0, 2)
    wv = a["attn_wv"].reshape(DL, H, DK).transpose(2, 1, 0).reshape(DK, PAIRS, 2 * DL).transpose(1, 0, 2)
    wo = a["attn_wo"].reshape(PAIRS, 2, DK, D).transpose(0, 2, 1, 3).reshape(PAIRS, DK, 2 * D)
    freq = np.float32(1.0 / 10000.0) ** np.linspace(0.0, 1.0, RQ, dtype=np.float32)
    theta = np.arange(S, dtype=np.float32)[:, None] * freq[None, :]
    shared = np.stack([a["ffn_sg"], a["ffn_su"], a["ffn_sd"]])
    w1 = a["ffn_w1"].reshape(E, DC, P, 2 * I).transpose(0, 2, 1, 3).reshape(E, P, DC * 2 * I)
    w2 = a["ffn_w2"].reshape(E, I // P, P, D).transpose(0, 2, 1, 3).reshape(E, P, I // P * D)
    arrays = {
        "x": dense(a["attn_x"]),
        "attn_w": dense(np.concatenate([wq, wk, wv, wo], 2)),
        "w_kv_down": dense(a["attn_w_kv_down"].reshape(DC, P, DL).transpose(1, 0, 2)),
        "q_norm_rows": dense(np.broadcast_to(a["attn_q_norm_w"], (P, DK))),
        "k_norm_col": dense(a["attn_k_norm_w"].reshape(DK, 1)),
        "cos": dense(np.cos(theta).reshape(TB, P, RQ).transpose(1, 0, 2)),
        "sin": dense(np.sin(theta).reshape(TB, P, RQ).transpose(1, 0, 2)),
        "norm_rows": dense(np.broadcast_to(a["ffn_norm_w"], (P, D))),
        "router_w": dense(a["ffn_router_w"].T.reshape(DC, P, E).transpose(1, 0, 2)),
        "shared_w": dense(shared.reshape(3, DC, P, SH).transpose(2, 0, 1, 3).reshape(P, 3 * DC * SH)),
        "w12": dense(np.concatenate([w1, w2], 2)),
    }
    nc = bacc.Bacc("TRN2", target_bir_lowering=False, num_devices=1)
    args = {name: nc.dram_tensor("in_" + name, value.shape, mybir.dt.from_np(value.dtype),
                                 kind="ExternalInput").ap() for name, value in arrays.items()}
    out = nc.dram_tensor("out_0", (B, S, D), F32, kind="ExternalOutput").ap()
    build_program(nc, out=out, **args)
    result = run_bass_kernel_spmd(nc, [{"in_" + name: value for name, value in arrays.items()}], core_ids=[0])
    return result.results[0]["out_0"]
```
